# Optimizing a Trainium2 kernel written in Bass

```python
import numpy as np
import jax
import jax.numpy as jnp

def _softmax(x, axis=-1):
    return jax.nn.softmax(x, axis=axis)

def _gelu(x):
    return jax.nn.gelu(x, approximate=True)

def _silu(x):
    return jax.nn.silu(x)

def _sigmoid(x):
    return jax.nn.sigmoid(x)

def _layernorm(x, axis=-1, eps=1e-05):
    m = jnp.mean(x, axis=axis, keepdims=True)
    v = jnp.var(x, axis=axis, keepdims=True)
    return (x - m) / jnp.sqrt(v + eps)

def _scatter_add(tgt, idx, src, axis=0):
    return tgt.at[idx].add(src)

def _segment_sum(src, seg, n):
    return jax.ops.segment_sum(src, seg, n)
kernel_name = 'mk_sandwich_d1_jaxref_r4_043234'

def setup_inputs(seed: int=0):
    np.random.seed(seed)
    _w = jnp.asarray

    def _L0_attn_setup():
        import jax, jax.numpy as jnp
        import numpy as np
        D_MODEL = 256
        N_HEADS = 32
        HEAD_DIM = D_MODEL // N_HEADS
        EPS = 1e-05
        key = jax.random.key(seed)
        ks = jax.random.split(key, 6)
        B, S = (2, 512)
        scale = 1.0 / np.sqrt(D_MODEL)
        return {'x': jax.random.normal(ks[0], (B, S, D_MODEL), dtype=jnp.float32), 'Wqkv_w': jax.random.normal(ks[1], (3 * D_MODEL, D_MODEL), dtype=jnp.float32) * scale, 'Wqkv_b': jax.random.normal(ks[2], (3 * D_MODEL,), dtype=jnp.float32) * 0.01, 'gn_w': jnp.ones((D_MODEL,), dtype=jnp.float32), 'gn_b': jnp.zeros((D_MODEL,), dtype=jnp.float32), 'out_w': jax.random.normal(ks[3], (D_MODEL, D_MODEL), dtype=jnp.float32) * scale, 'out_b': jax.random.normal(ks[4], (D_MODEL,), dtype=jnp.float32) * 0.01}
    _L0_attn_in = _L0_attn_setup()

    def _L0_ffn_setup():
        import jax, jax.numpy as jnp
        import numpy as np
        TOP_K = 2

        def _ffn(x, gw, uw, dw):
            return jax.nn.silu(x @ gw.T) * (x @ uw.T) @ dw.T
        key = jax.random.key(seed)
        ks = jax.random.split(key, 8)
        w = lambda k, shape: jax.random.normal(k, shape, jnp.float32) * 0.02
        return dict(x=jax.random.normal(ks[0], (4, 512, 256), jnp.float32), gate_w=w(ks[1], (8, 256)), expert_gate=w(ks[2], (8, 704, 256)), expert_up=w(ks[3], (8, 704, 256)), expert_down=w(ks[4], (8, 256, 704)), shared_gate=w(ks[5], (704, 256)), shared_up=w(ks[6], (704, 256)), shared_down=w(ks[7], (256, 704)))
    _L0_ffn_in = _L0_ffn_setup()
    _d = {'L0_attn_x': _L0_attn_in['x'], 'L0_attn_Wqkv_w': _L0_attn_in['Wqkv_w'], 'L0_attn_Wqkv_b': _L0_attn_in['Wqkv_b'], 'L0_attn_gn_w': _L0_attn_in['gn_w'], 'L0_attn_gn_b': _L0_attn_in['gn_b'], 'L0_attn_out_w': _L0_attn_in['out_w'], 'L0_attn_out_b': _L0_attn_in['out_b'], 'L0_ffn_gate_w': _L0_ffn_in['gate_w'], 'L0_ffn_expert_gate': _L0_ffn_in['expert_gate'], 'L0_ffn_expert_up': _L0_ffn_in['expert_up'], 'L0_ffn_expert_down': _L0_ffn_in['expert_down'], 'L0_ffn_shared_gate': _L0_ffn_in['shared_gate'], 'L0_ffn_shared_up': _L0_ffn_in['shared_up'], 'L0_ffn_shared_down': _L0_ffn_in['shared_down']}
    _x0 = _d['L0_attn_x']
    _d['L0_attn_x'] = jax.random.normal(jax.random.fold_in(jax.random.key(seed), 1), (8, 512, 256), dtype=_x0.dtype)
    del _x0
    return _d

def reference(L0_attn_x, L0_attn_Wqkv_w, L0_attn_Wqkv_b, L0_attn_gn_w, L0_attn_gn_b, L0_attn_out_w, L0_attn_out_b, L0_ffn_gate_w, L0_ffn_expert_gate, L0_ffn_expert_up, L0_ffn_expert_down, L0_ffn_shared_gate, L0_ffn_shared_up, L0_ffn_shared_down):

    def _L0_attn_ref(x, Wqkv_w, Wqkv_b, gn_w, gn_b, out_w, out_b):
        import jax, jax.numpy as jnp
        import numpy as np
        D_MODEL = 256
        N_HEADS = 32
        HEAD_DIM = D_MODEL // N_HEADS
        EPS = 1e-05
        B, S, Dm = x.shape
        H, Dh = (N_HEADS, HEAD_DIM)
        qkv = x @ Wqkv_w.T + Wqkv_b
        qkv = qkv.reshape(B, S, 3, H, Dh)
        q, k, v = (qkv[:, :, 0], qkv[:, :, 1], qkv[:, :, 2])
        a = jnp.einsum('bthd,bshd->bhts', q, k)
        ctx = jnp.einsum('bhts,bshd->bthd', a, v)
        g = ctx.transpose(0, 2, 3, 1)
        mean = g.mean(axis=(2, 3), keepdims=True)
        var = ((g - mean) ** 2).mean(axis=(2, 3), keepdims=True)
        gh = (g - mean) * jax.lax.rsqrt(var + EPS)
        gh = gh * gn_w.reshape(H, Dh, 1) + gn_b.reshape(H, Dh, 1)
        ctx = gh.transpose(0, 3, 1, 2).reshape(B, S, Dm)
        return ctx @ out_w.T + out_b

    def _L0_ffn_ref(x, gate_w, expert_gate, expert_up, expert_down, shared_gate, shared_up, shared_down):
        import jax, jax.numpy as jnp
        import numpy as np
        TOP_K = 2

        def _ffn(x, gw, uw, dw):
            return jax.nn.silu(x @ gw.T) * (x @ uw.T) @ dw.T
        B, S, H = x.shape
        xf = x.reshape(-1, H)
        T = xf.shape[0]
        E = expert_gate.shape[0]
        shared = _ffn(xf, shared_gate, shared_up, shared_down)
        logits = xf @ gate_w.T
        probs = jax.nn.softmax(logits, axis=-1)
        topw, topi = jax.lax.top_k(probs, TOP_K)
        topw = topw / (topw.sum(-1, keepdims=True) + 1e-20)
        comb = jnp.zeros((T, E), xf.dtype).at[jnp.arange(T)[:, None], topi].add(topw)

        def body(acc, ws):
            gw, uw, dw, wcol = ws
            return (acc + _ffn(xf, gw, uw, dw) * wcol[:, None], None)
        routed, _ = jax.lax.scan(body, jnp.zeros_like(xf), (expert_gate, expert_up, expert_down, comb.T))
        return (shared + routed).reshape(B, S, H)
    x = L0_attn_x
    x = x + _layernorm(_L0_attn_ref(_layernorm(x, axis=-1), L0_attn_Wqkv_w, L0_attn_Wqkv_b, L0_attn_gn_w, L0_attn_gn_b, L0_attn_out_w, L0_attn_out_b), axis=-1)
    x = x + _layernorm(_L0_ffn_ref(_layernorm(x, axis=-1), L0_ffn_gate_w, L0_ffn_expert_gate, L0_ffn_expert_up, L0_ffn_expert_down, L0_ffn_shared_gate, L0_ffn_shared_up, L0_ffn_shared_down), axis=-1)
    return x

_drawn_inputs = setup_inputs


def setup_inputs(seed=0):
    import zlib

    import numpy as np

    out = dict(_drawn_inputs(seed))
    spreads = {'L0_attn_gn_w': (1.0, 0.2), 'L0_attn_gn_b': (0.0, 0.1)}
    factors = {}
    for name, (base, spread) in spreads.items():
        noise = np.random.default_rng([zlib.crc32(name.encode()), seed]).standard_normal(out[name].shape)
        drawn = base * np.exp(spread * noise) if base else spread * noise
        out[name] = jnp.asarray(drawn.astype(out[name].dtype))
    for name, factor in factors.items():
        out[name] = (out[name] * factor).astype(out[name].dtype)
    return out
```

```python
from contextlib import ExitStack

import concourse.bass as bass
from concourse import mybir

F32 = mybir.dt.float32
F16 = mybir.dt.float16
I32 = mybir.dt.int32
ALU = mybir.AluOpType
ACT = mybir.ActivationFunctionType
AX = mybir.AxisListType

P = 128
B, S, D = 8, 512, 256
HD = 8
TOK = B * S
NT = S // P
KD = D // P
E = 8
F = 704
FC = 6
GU = 2 * F
GJ = GU // P
TW = 256
TT = TW // P
NTILE = 2 * TOK // TW + E - 1
NCOL = NTILE * TT
NTB = TOK // P
EPS = 1e-5
X_SCALE = 2.0 ** 11
SLOT_GU = 2 * KD * GU
SLOT_DN = FC * 2 * D
NSLOT = E + 1
USES = 18

ORDER = [("load",), ("ln1",), ("G", 0), ("G", 1), ("G", 2), ("D", 0), ("turn1",), ("G", 3), ("D", 1), ("q",), ("kv",),
         ("G", 4), ("D", 2), ("state",), ("prep_scale",), ("G", 5), ("D", 3), ("ctx",), ("G", 6), ("D", 4), ("group_mean",),
         ("G", 7), ("D", 5), ("group_var",), ("prep", 0), ("G", 8), ("D", 6), ("prep", 1), ("ctx_norm",), ("out",), ("prep", 2), ("G", 9), ("D", 7),
         ("prep", 3), ("lno",), ("prep", 4), ("prep", 5), ("prep", 6),
         ("G", 10), ("D", 8), ("prep", 7), ("prep", 8), ("G", 11), ("D", 9), ("D", 10), ("D", 11), ("turn2",), ("logits",)]
TAIL = [("load",), ("G", 0), ("route_probs",), ("G", 1), ("route_top1",), ("G", 2), ("D", 0), ("route_top2",), ("G", 3), ("D", 1), ("prep_scale",),
        ("route_slots",), ("G", 4), ("D", 2), ("prep", 0), ("G", 5), ("D", 3), ("prep", 1), ("route_positions",), ("G", 6), ("D", 4), ("prep", 2),
        ("route_invert",), ("prep", 3), ("G", 7), ("D", 5), ("prep", 4), ("G", 8), ("D", 6),
        ("prep", 5), ("G", 9), ("D", 7), ("prep", 6), ("prep", 7), ("G", 10), ("D", 8), ("prep", 8), ("G", 11), ("D", 9), ("D", 10), ("D", 11)]


def build(nc, x_in, Wqkv, bqkv, gn_w, gn_b, Wout, bout, gate_w, eg, eu, ed, sg, su, sd, out):
    xf = x_in.rearrange("b s d -> (b s) d")
    of = out.rearrange("b s d -> (b s) d")
    with ExitStack() as ctx:
        def sb(name, cols, dt=F32, parts=P):
            return ctx.enter_context(nc.sbuf_tensor(name, [parts, cols], dt))

        def sem(name):
            return ctx.enter_context(nc.semaphore(name))

        xn2_d = nc.dram_tensor("xn2_d", (TOK, D), F32, kind="Internal").ap()
        x2_d = nc.dram_tensor("x2_d", (TOK, D), F32, kind="Internal").ap()
        sh_d = nc.dram_tensor("sh_d", (TOK, D), F32, kind="Internal").ap()
        y_d = nc.dram_tensor("y_d", (NTILE * TW, D), F32, kind="Internal").ap()

        wgu = sb("wgu", NSLOT * SLOT_GU, F16)
        wdn = sb("wdn", NSLOT * SLOT_DN, F16)
        att = sb("att", 5120)
        xres = att[:, 0:1024].rearrange("p (t d) -> p t d", t=NT)
        xn = att[:, 1024:2048].rearrange("p (t d) -> p t d", t=NT)
        kv = att[:, 1024:3072].rearrange("p (t c) -> p t c", t=NT)
        orow = att[:, 2048:3072].rearrange("p (t d) -> p t d", t=NT)
        xT = att[:, 3072:4096].rearrange("p (k s) -> p k s", k=KD)
        qT = att[:, 4096:5120].rearrange("p (k s) -> p k s", k=KD)
        xhl = sb("xhl", 2 * KD * S, F16)
        xhl_v = xhl[:, :].rearrange("p (h k s) -> p h k s", h=2, k=KD)
        attw = sb("attw", 2816)
        wqkvT = attw[:, 0:1536].rearrange("p (k c) -> p k c", k=KD)
        woT = attw[:, 1536:2048].rearrange("p (k c) -> p k c", k=KD)
        kvb = attw[:, 2048:2560]
        outb = attw[:, 2560:2816]
        silu = sb("silu", 2 * TW)
        hf = sb("hf", 2 * TW)
        hT = sb("hT", FC * 2 * TW, F16)
        ysb = sb("ysb", TT * D)
        ident = sb("ident", P)
        mask = sb("mask", P)
        upper = sb("upper", P)
        ones = sb("ones", P)
        iota = sb("iota", P)
        iota_i = silu[:, 0:P].bitcast(I32)
        rev = sb("rev", E)
        state = sb("state", KD * P)
        logits = sb("logits", NTB * E)
        gateT = sb("gateT", KD * E)
        sc = sb("sc", NSLOT * 4)
        colv = sb("colv", 8)
        st6 = sb("st6", NT * 6)
        mv = sb("mv", NT * 2)
        ve = sb("ve", NT)
        rstd = sb("rstd", NT)
        nmr = sb("nmr", NT)
        mhalf = sb("mhalf", NT)
        gst = sb("gst", 16)
        mx = sb("mx", 2)
        mxa = sb("mxa", 2)
        pw = sb("pw", 8)
        small = sb("small", 224)
        tokf = sb("tokf", NTB)
        posi = sb("posi", 2 * NTB, I32)
        wts = sb("wts", 2 * NTB)
        lohi_i = sb("lohi_i", 2 * NTB, I32)
        idx = sb("idx", NCOL, I32)
        idxc = sb("idxc", 4, I32)
        eid = sb("eid", NTILE, I32)

        stg_gu = wgu[:, E * SLOT_GU:].bitcast(F32).rearrange("p (j d) -> p j d", j=GJ)
        stg_dn = wdn[:, E * SLOT_DN:].bitcast(F32).rearrange("p (t f) -> p t f", t=KD)
        last_gu = att[:, 0:2816].rearrange("p (j d) -> p j d", j=GJ)
        last_dn = att[:, 2816:4352].rearrange("p (t f) -> p t f", t=KD)

        def rt(n):
            return attw[:, 256 * n:256 * n + 256]
        r_p, r_t, r_o1, r_o2, r_m, r_c, r_s, r_x = (rt(n) for n in range(8))
        oh_lo = attw[:, 2048:2304].rearrange("p (r c) -> p r c", r=2)
        oh_hi = attw[:, 2304:2464].rearrange("p (r c) -> p r c", r=2)
        posf, lof, hif = (attw[:, 2464 + 2 * NTB * n:2464 + 2 * NTB * (n + 1)] for n in range(3))
        xg = attw[:, 0:1024].rearrange("p (r t d) -> p r t d", r=2, t=TT)
        xt16 = att[:, 0:1024].bitcast(F16).rearrange("p (r h k s) -> p r h k s", r=2, h=2, k=KD)
        cmb = att[:, 1024:5120].rearrange("p (r a t d) -> p r a t d", r=2, a=4, t=2)

        ps = [ctx.enter_context(nc.psum_tensor(f"ps{i}", [P, 512], F32)) for i in range(8)]
        gu_ps, y_ps, att_ps, prep_ps = ps[0:2], ps[2:4], ps[4:6], ps[6:8]

        const_made = sem("const_made")
        wait_passed = sem("wait_passed")
        setup_loaded = sem("setup_loaded")
        wqkv_staged = sem("wqkv_staged")
        setup_turned = sem("setup_turned")
        setup_copied = sem("setup_copied")
        x_loaded = sem("x_loaded")
        stage_loaded = sem("stage_loaded")
        x2_made = sem("x2_made")
        xn2_made = sem("xn2_made")
        x2_stored = sem("x2_stored")
        xn2_stored = sem("xn2_stored")
        xn_made = sem("xn_made")
        ve_made = sem("ve_made")
        rstd_made = sem("rstd_made")
        att_done = sem("att_done")
        link_v = sem("link_v")
        link_p = sem("link_p")
        xTa_made = sem("xTa_made")
        xTb_made = sem("xTb_made")
        gmean_made = sem("gmean_made")
        gvar_made = sem("gvar_made")
        o_made = sem("o_made")
        q_made = sem("q_made")
        kv_made = sem("kv_made")
        state_made = sem("state_made")
        ctx_made = sem("ctx_made")
        gstat_made = sem("gstat_made")
        ctxn_made = sem("ctxn_made")
        nmr_made = sem("nmr_made")
        o_scaled = sem("o_scaled")
        xhl_made = sem("xhl_made")
        hi_x_made = sem("hi_x_made")
        logits_made = sem("logits_made")
        max_made = sem("max_made")
        maxall_made = sem("maxall_made")
        scale_made = sem("scale_made")
        prep_turned = sem("prep_turned")
        prep_hi = sem("prep_hi")
        prep_lo = sem("prep_lo")
        gu_done = sem("gu_done")
        silu_made = sem("silu_made")
        h_made = sem("h_made")
        hi_made = sem("hi_made")
        lo_made = sem("lo_made")
        dn_done = sem("dn_done")
        y_made = sem("y_made")
        y_stored = sem("y_stored")
        rt_link = sem("rt_link")
        diff_made = sem("diff_made")
        exp_made = sem("exp_made")
        m_made = sem("m_made")
        counted = sem("counted")
        eid_made = sem("eid_made")
        onehot_made = sem("onehot_made")
        onehot_used = sem("onehot_used")
        inverted = sem("inverted")
        idx_made = sem("idx_made")
        idxc_made = sem("idxc_made")
        xg_loaded = [sem("xg_loaded0"), sem("xg_loaded1")]
        xg_turned = sem("xg_turned")
        xt_hi = sem("xt_hi")
        xt_lo = sem("xt_lo")
        gath = [sem("gath0"), sem("gath1")]
        cmb_loaded = [sem("cmb_loaded0"), sem("cmb_loaded1")]
        cmb_link = sem("cmb_link")
        cmb_ve = sem("cmb_ve")
        cmb_sd = sem("cmb_sd")
        cmb_nmr = sem("cmb_nmr")
        cmb_norm = sem("cmb_norm")
        out_made = sem("out_made")
        out_stored = [sem("out_stored0"), sem("out_stored1")]

        def wait(eng, s, value):
            if not (isinstance(value, int) and value <= 0):
                eng.wait_ge(s, value)

        def slot_gu(slot, h, k, j, n=1):
            return wgu[:, bass.ds(slot * SLOT_GU + ((h * KD + k) * GJ + j) * P, n * P)]

        def slot_dn(slot, c, h):
            return wdn[:, bass.ds(slot * SLOT_DN + (c * 2 + h) * D, D)]

        def scale_of(slot, n, lo=0, hi=P):
            return sc[lo:hi, bass.ds(slot * 4 + n, 1)]

        TURN1, QU, KVU, STATE, CTX, GMEAN, GVAR, OUT, TURN2, LOGIT = 0, 2, 4, 8, 9, 11, 12, 13, 15, 17

        def passed(eng):
            eng.sem_inc(wait_passed, 1)

        READ = ([(xTa_made, 2, 1), (xTb_made, 2, 1)] + [(q_made, KD, m + 1) for m in range(KD)] + [(kv_made, NT, t + 1) for t in range(NT)]
                + [(state_made, 1, 1)] + [(ctx_made, KD, m + 1) for m in range(KD)] + [(gmean_made, 1, 1), (gvar_made, 1, 1)]
                + [(o_made, 2, h + 1) for h in range(2)] + [(xTa_made, 2, 2), (xTb_made, 2, 2)] + [(logits_made, 1, 1)])
        assert len(READ) == USES

        def att_bank(n):
            return att_ps[n % 2]

        def bank_ready(pe, b, n):
            s, per, count = READ[n - 2]
            wait(pe, s, (b * per + count) if n >= 2 else (b * per + count - per))

        def xg_ps(r):
            return ps[6 + r][:, :].rearrange("p (k s) -> p k s", k=KD)

        def use_done(eng, b, n):
            eng.wait_ge(att_done, b * USES + n + 1)

        GROUPS = [("gu", k, j, min(4, GJ - j)) for k in range(KD) for j in (0, 4, 8)] + [("dn", 0, c, 2) for c in (0, 2, 4)]
        NG = len(GROUPS)

        block = ctx.enter_context(nc.Block())

        @block.sync
        def _(sp):
            sp.dma_start(att[:, 0:1536].rearrange("p (j d) -> p j d", j=6), Wqkv.rearrange("(j p) d -> p j d", p=P)).then_inc(wqkv_staged, 16)
            sp.dma_start(att[:, 1536:2048].rearrange("p (j d) -> p j d", j=2), Wout.rearrange("(j p) d -> p j d", p=P)).then_inc(wqkv_staged, 16)
            sp.dma_start(att[0:E, 2048:2304], gate_w).then_inc(wqkv_staged, 16)
            sp.dma_start(att[0:2, 2304:2432], bqkv[0:D].rearrange("(k p) -> k p", p=P)).then_inc(wqkv_staged, 16)
            sp.dma_start(att[0:2, 2432:2560], gn_w.rearrange("(k p) -> k p", p=P)).then_inc(wqkv_staged, 16)
            sp.dma_start(att[0:2, 2560:2688], gn_b.rearrange("(k p) -> k p", p=P)).then_inc(wqkv_staged, 16)
            sp.dma_start(kvb, bqkv[D:3 * D].rearrange("(o n) -> o n", o=1).to_broadcast([P, 2 * D])).then_inc(setup_loaded, 16)
            sp.dma_start(outb, bout.rearrange("(o n) -> o n", o=1).to_broadcast([P, D])).then_inc(setup_loaded, 16)

            def load_stage(g_src, u_src, d_src, gu, dn):
                n5 = 5 * P
                sp.dma_start(gu[:, 0:5, :], g_src[0:n5].rearrange("(j p) d -> p j d", p=P)).then_inc(stage_loaded, 16)
                sp.dma_start(gu[:, 5:10, :], u_src[0:n5].rearrange("(j p) d -> p j d", p=P)).then_inc(stage_loaded, 16)
                sp.dma_start(gu[0:64, 10, :], g_src[n5:F]).then_inc(stage_loaded, 16)
                sp.dma_start(gu[64:P, 10, :], u_src[n5:F]).then_inc(stage_loaded, 16)
                sp.dma_start(dn[:, :, 0:F], d_src.rearrange("(t p) f -> p t f", p=P)).then_inc(stage_loaded, 16)
                sp.dma_start(dn[:, :, F:F + 64], d_src[:, n5:F].rearrange("(t p) f -> p t f", p=P)).then_inc(stage_loaded, 16)

            def load_expert(e, gu, dn):
                load_stage(eg[bass.ds(e, 1)].rearrange("e f d -> (e f) d"), eu[bass.ds(e, 1)].rearrange("e f d -> (e f) d"),
                           ed[bass.ds(e, 1)].rearrange("e d f -> (e d) f"), gu, dn)

            def batch(b):
                if isinstance(b, int):
                    sp.wait_ge(setup_turned, 8)
                else:
                    sp.wait_ge(x2_stored, b * 16)
                    sp.wait_ge(xn2_made, b)
                sp.dma_start(xres, xf[bass.ds(b * S, S), :].rearrange("(t p) d -> p t d", p=P)).then_inc(x_loaded, 16)
                if isinstance(b, int):
                    load_stage(sg, su, sd, stg_gu, stg_dn)
                else:
                    sp.wait_ge(prep_turned, b * NG)
                    load_expert(b - 1, stg_gu, stg_dn)
                if not isinstance(b, int):
                    for u in range(2):
                        store_shared(2 * b - 2 + u)
                sp.wait_ge(x2_made, b + 1)
                sp.dma_start(x2_d[bass.ds(b * S, S), :].rearrange("(t p) d -> p t d", p=P), xres).then_inc(x2_stored, 16)
                sp.wait_ge(xn2_made, b + 1)
                sp.dma_start(xn2_d[bass.ds(b * S, S), :].rearrange("(t p) d -> p t d", p=P), xn).then_inc(xn2_stored, 16)

            def store_shared(t):
                sp.wait_ge(y_made, (t + 2) * TT)
                sp.dma_start(sh_d[bass.ds(t * TW, TW), :].rearrange("(t p) d -> p t d", p=P),
                             ysb[:, :].rearrange("p (t d) -> p t d", t=TT)).then_inc(y_stored, 16)

            batch(0)
            with sp.Fori(1, B) as b:
                batch(b)
            sp.wait_ge(x2_stored, B * 16)
            sp.wait_ge(xn2_stored, B * 16)
            sp.wait_ge(xhl_made, B * KD)
            sp.wait_ge(logits_made, B)
            load_expert(E - 1, last_gu, last_dn)
            for u in range(2):
                store_shared(2 * B - 2 + u)

            def store_routed(i):
                sp.wait_ge(y_made, (2 * B + i + 2) * TT)
                sp.dma_start(y_d[bass.ds(i * TW, TW), :].rearrange("(t p) d -> p t d", p=P),
                             ysb[:, :].rearrange("p (t d) -> p t d", t=TT)).then_inc(y_stored, 16)

            with sp.Fori(0, NTILE) as i:
                store_routed(i)

            def load_rows(g, r, first):
                if not first:
                    sp.wait_ge(out_stored[r], 16 * g)
                for a, src in ((2, sh_d), (3, x2_d)):
                    sp.dma_start(cmb[:, r, a], src[bass.ds((2 * g + r) * 2 * P, 2 * P), :].rearrange("(t p) d -> p t d", p=P)).then_inc(cmb_loaded[r], 16)

            def store_out(g, r):
                sp.wait_ge(out_made, 2 * g + r + 1)
                sp.dma_start(of[bass.ds((2 * g + r) * 2 * P, 2 * P), :].rearrange("(t p) d -> p t d", p=P), cmb[:, r, 3]).then_inc(out_stored[r], 16)

            NGRP = NTB // 4
            sp.wait_ge(y_stored, 16 * (2 * B + NTILE + 1))
            load_rows(0, 0, True)
            load_rows(0, 1, True)
            with sp.Fori(0, NGRP - 1) as g:
                store_out(g, 0)
                load_rows(g + 1, 0, False)
                store_out(g, 1)
                load_rows(g + 1, 1, False)
            store_out(NGRP - 1, 0)
            store_out(NGRP - 1, 1)
            for r in range(2):
                sp.wait_ge(out_stored[r], 16 * NGRP)

        @block.gpsimd
        def _(pool):
            g = nc.gpsimd
            g.memset(ident[:, :], 0.0).then_inc(link_p, 1)
            g.memset(ones[:, :], 1.0).then_inc(link_p, 1)
            g.memset(upper[:, :], 1.0).then_inc(link_p, 1)
            g.memset(mask[:, :], 1.0).then_inc(link_p, 1)
            g.memset(mhalf[:, :], -0.5).then_inc(link_p, 1)
            g.iota(iota_i, pattern=[[1, P]], base=0, channel_multiplier=0).then_inc(link_p, 1)
            pool.wait_ge(link_p, 6)
            g.affine_select(out=ident[:, :], in_=ident[:, :], compare_op=ALU.not_equal, fill=1.0, base=0,
                            pattern=[[-1, P]], channel_multiplier=1).then_inc(const_made, 1)
            g.affine_select(out=upper[:, :], in_=upper[:, :], compare_op=ALU.is_gt, fill=0.0, base=0,
                            pattern=[[1, P]], channel_multiplier=-1).then_inc(const_made, 1)
            m3 = mask[:, :].rearrange("p (h c) -> p h c", c=HD)
            g.affine_select(out=m3, in_=m3, compare_op=ALU.is_ge, fill=0.0, base=0,
                            pattern=[[-HD, P // HD], [0, HD]], channel_multiplier=1).then_inc(link_p, 1)
            pool.wait_ge(link_p, 7)
            g.affine_select(out=m3, in_=m3, compare_op=ALU.is_ge, fill=0.0, base=HD - 1,
                            pattern=[[HD, P // HD], [0, HD]], channel_multiplier=-1).then_inc(const_made, 1)
            g.tensor_copy(iota[:, :], iota_i).then_inc(const_made, 1)
            g.iota(lohi_i[:, 0:NTB], pattern=[[P, NTB]], base=0, channel_multiplier=1).then_inc(link_p, 1)
            g.iota(posi[:, 0:E], pattern=[[-1, E]], base=E, channel_multiplier=0).then_inc(link_p, 1)
            pool.wait_ge(link_p, 9)
            g.tensor_copy(tokf[:, :], lohi_i[:, 0:NTB]).then_inc(const_made, 1)
            g.tensor_copy(rev[:, :], posi[:, 0:E]).then_inc(const_made, 1)

            def root(n, cols):
                pool.wait_ge(ve_made, n + 1)
                g.tensor_tensor(rstd[:, 0:cols], ve[:, 0:cols], mhalf[:, 0:cols], ALU.pow).then_inc(rstd_made, 1)

            def prep_scale(s):
                pool.wait_ge(max_made, s + 1)
                passed(pool)
                g.partition_all_reduce(mxa[:, :], mx[:, :], P, bass.bass_isa.ReduceOp.max).then_inc(maxall_made, 1)

            def batch(b):
                for step in ORDER:
                    if step[0] == "ln1":
                        root(4 * b, NT)
                    if step[0] == "prep_scale":
                        prep_scale(b)
                    if step[0] == "ctx_norm":
                        root(4 * b + 1, KD)
                    if step[0] == "lno":
                        root(4 * b + 2, NT)
                        root(4 * b + 3, NT)

            batch(0)
            with pool.Fori(1, B) as b:
                batch(b)
            prep_scale(B)

            pool.wait_ge(idx_made, 1)
            pool.wait_ge(xn2_stored, B * 16)

            def gather_x(i, r, first):
                if not first:
                    pool.wait_ge(xg_turned, i - 1)
                    pool.wait_ge(xg_loaded[r], 16 * (i - r))
                g.tensor_copy(idxc[:, 2 * r:2 * r + 2], idx[:, bass.ds(i * TT, TT)]).then_inc(idxc_made, 1)
                pool.wait_ge(idxc_made, i + 1)
                passed(pool)
                for t in range(TT):
                    g.indirect_dma_start(xg[:, r, t, :], None, xn2_d,
                                         bass.IndirectOffsetOnAxis(ap=idxc[:, 2 * r + t:2 * r + t + 1], axis=0)).then_inc(xg_loaded[r], 16)

            gather_x(0, 0, True)
            gather_x(1, 1, True)
            with pool.Fori(2, NTILE - 1, 2) as i:
                gather_x(i, 0, False)
                gather_x(i + 1, 1, False)
            gather_x(NTILE - 1, 0, False)

            pool.wait_ge(y_stored, 16 * (2 * B + NTILE + 1))
            for r in range(2):
                pool.wait_ge(xg_loaded[r], 32 * ((NTILE + 1 - r) // 2))

            def gather_y(g2, r, first):
                if not first:
                    pool.wait_ge(out_stored[r], 16 * g2)
                for a in range(2):
                    for t in range(2):
                        g.tensor_copy(idxc[:, t:t + 1], posi[:, bass.ds(a * NTB + (2 * g2 + r) * 2 + t, 1)]).then_inc(idxc_made, 1)
                    n = NTILE + (2 * g2 + r) * 4 + 2 * a + 2
                    pool.wait_ge(idxc_made, n)
                    passed(pool)
                    for t in range(2):
                        g.indirect_dma_start(cmb[:, r, a, t, :], None, y_d,
                                             bass.IndirectOffsetOnAxis(ap=idxc[:, t:t + 1], axis=0)).then_inc(gath[r], 16)
                    pool.wait_ge(gath[r], g2 * 64 + a * 32 + 32)

            gather_y(0, 0, True)
            gather_y(0, 1, True)
            with pool.Fori(1, NTB // 4) as g2:
                gather_y(g2, 0, False)
                gather_y(g2, 1, False)

        @block.scalar
        def _(act):
            a = nc.scalar
            act.sem_inc(y_made, TT)
            act.sem_inc(y_stored, 16)

            for n in range(8):
                act.wait_ge(setup_turned, n + 1)
                src = att_bank(n)
                if n < 6:
                    k, j = n // 3, 2 * (n % 3)
                    a.copy(wqkvT[:, k, j * P:(j + 2) * P], src[:, 0:256]).then_inc(setup_copied, 1)
                elif n == 6:
                    a.copy(attw[:, 1536:2048], src[:, :]).then_inc(setup_copied, 1)
                else:
                    a.copy(gateT[:, :], src[:, 0:16]).then_inc(link_v, 1)
                    a.copy(colv[:, 0:6], src[:, 16:22]).then_inc(setup_copied, 1)

            def gate_up(t, c, slot):
                q = t * FC + c
                act.wait_ge(gu_done, q + 1)
                passed(act)
                if c < FC - 1:
                    a.activation(silu[:, c % 2 * TW:(c % 2 + 1) * TW], gu_ps[c % 2][:, 0:TW], ACT.Silu,
                                 scale=scale_of(slot, 0)).then_inc(silu_made, 1)
                else:
                    a.activation(silu[64:P, TW:2 * TW], gu_ps[1][0:64, 0:TW], ACT.Silu,
                                 scale=scale_of(slot, 0, 0, 64)).then_inc(silu_made, 1)

            def hidden_hi(t, c):
                q = t * FC + c
                act.wait_ge(h_made, q + 3)
                act.wait_ge(dn_done, q + 1)
                h = hf[:, c % 2 * TW:(c % 2 + 1) * TW]
                o = hT[:, c * 2 * TW:c * 2 * TW + TW]
                if c < FC - 1:
                    a.copy(o, h).then_inc(hi_made, 1)
                else:
                    a.copy(o[0:64], h[64:P])
                    a.copy(o[64:P], h[64:P]).then_inc(hi_made, 1)

            def y_out(t, slot):
                act.wait_ge(dn_done, FC + (t + 1) * FC)
                act.wait_ge(y_stored, 16 * (t + 1))
                passed(act)
                for tt in range(TT):
                    ins = a.activation(ysb[:, tt * D:(tt + 1) * D], y_ps[tt][:, 0:D], ACT.Copy, scale=scale_of(slot, 2))
                    ins.then_inc(y_made, 1)

            def ffn_step(kind, n, t0, slot):
                t, c = t0 + n // FC, n % FC
                if kind == "G":
                    gate_up(t, c, slot)
                    if n > 0:
                        hidden_hi(t0 + (n - 1) // FC, (n - 1) % FC)
                    if n == 2 * FC - 1:
                        hidden_hi(t, c)
                elif c == FC - 1:
                    y_out(t, slot)

            def prep(s, n):
                what, k, j, w = GROUPS[n]
                act.wait_ge(prep_turned, s * NG + n + 1)
                act.wait_ge(scale_made, s + 1)
                passed(act)
                src = prep_ps[n % 2]
                if what == "gu":
                    a.activation(slot_gu(s, 0, k, j, w), src[:, 0:w * P], ACT.Copy, scale=pw[:, 4:5]).then_inc(prep_hi, 1)
                else:
                    dst = wdn[:, bass.ds(s * SLOT_DN + j * 2 * D, 4 * D)].rearrange("p (c h d) -> p c h d", c=2, h=2)[:, :, 0, :]
                    a.activation(dst, src[:, :].rearrange("p (c d) -> p c d", c=2), ACT.Copy, scale=pw[:, 5:6]).then_inc(prep_hi, 1)

            def batch(b):
                for step in ORDER:
                    kind = step[0]
                    if kind in "GD" and not isinstance(b, int):
                        ffn_step(kind, step[1], 2 * b - 2, 0)
                    if kind == "turn1":
                        use_done(act, b, TURN1)
                        a.copy(xT[:, 0, :], att_bank(TURN1)[:, :]).then_inc(xTa_made, 1)
                    if kind == "q":
                        for m in range(KD):
                            use_done(act, b, QU + m)
                            a.activation(qT[:, m, :], att_bank(QU + m)[:, :], ACT.Identity, bias=colv[:, m:m + 1]).then_inc(q_made, 1)
                    if kind == "ctx":
                        for m in range(KD):
                            use_done(act, b, CTX + m)
                            a.copy(xT[:, m, :], att_bank(CTX + m)[:, :]).then_inc(ctx_made, 1)
                    if kind == "prep":
                        prep(b, step[1])
                    if kind == "lno":
                        act.wait_ge(nmr_made, b + 1)
                        for t in range(NT):
                            a.activation(orow[:, t, :], orow[:, t, :], ACT.Identity, bias=nmr[:, t:t + 1], scale=rstd[:, t:t + 1]).then_inc(o_scaled, 1)
                    if kind == "turn2":
                        use_done(act, b, TURN2)
                        a.copy(xT[:, 0, :], att_bank(TURN2)[:, :]).then_inc(xTa_made, 1)
                        act.wait_ge(xTa_made, 2 * b + 2)
                        act.wait_ge(xTb_made, 2 * b + 2)
                        for k in range(KD):
                            a.activation(xhl_v[:, 0, k, :], xT[:, k, :], ACT.Copy, scale=X_SCALE).then_inc(hi_x_made, 1)
                    if kind == "logits":
                        use_done(act, b, LOGIT)
                        a.copy(logits[:, bass.ds(b * NT * E, NT * E)], att_bank(LOGIT)[:, 0:NT * E]).then_inc(logits_made, 1)

            batch(0)
            with act.Fori(1, B) as b:
                batch(b)
            for step in TAIL:
                if step[0] in "GD":
                    ffn_step(step[0], step[1], 2 * B - 2, 0)
                if step[0] == "prep":
                    prep(B, step[1])
                if step[0] == "route_probs":
                    act.wait_ge(diff_made, 1)
                    a.activation(r_p, r_t, ACT.Exp).then_inc(exp_made, 1)

            act.wait_ge(eid_made, 1)

            def turned_x(i, r):
                act.wait_ge(xg_turned, i + 1)
                a.activation(xt16[:, r, 0], xg_ps(r), ACT.Copy, scale=X_SCALE).then_inc(xt_hi, 1)

            def routed(i, r, slot, before, turn=True):
                t = 2 * B + i
                gate_up(t, 0, slot)
                if before is not None:
                    hidden_hi(t - 1, 5)
                gate_up(t, 1, slot)
                hidden_hi(t, 0)
                if before is not None:
                    y_out(t - 1, before)
                gate_up(t, 2, slot)
                hidden_hi(t, 1)
                gate_up(t, 3, slot)
                hidden_hi(t, 2)
                if turn:
                    turned_x(i + 1, 1 - r)
                gate_up(t, 4, slot)
                hidden_hi(t, 3)
                gate_up(t, 5, slot)
                hidden_hi(t, 4)

            turned_x(0, 0)
            slot0 = act.value_load(eid[0:1, 0:1], min_val=1, max_val=E)
            routed(0, 0, slot0, None)
            with act.Fori(1, NTILE - 2, 2) as i:
                s0 = act.value_load(eid[0:1, bass.ds(i - 1, 1)], min_val=1, max_val=E)
                s1 = act.value_load(eid[0:1, bass.ds(i, 1)], min_val=1, max_val=E)
                routed(i, 1, s1, s0)
                s2 = act.value_load(eid[0:1, bass.ds(i + 1, 1)], min_val=1, max_val=E)
                routed(i + 1, 0, s2, s1)
            s0 = act.value_load(eid[0:1, NTILE - 3:NTILE - 2], min_val=1, max_val=E)
            s1 = act.value_load(eid[0:1, NTILE - 2:NTILE - 1], min_val=1, max_val=E)
            routed(NTILE - 2, 1, s1, s0)
            s2 = act.value_load(eid[0:1, NTILE - 1:NTILE], min_val=1, max_val=E)
            routed(NTILE - 1, 0, s2, s1, turn=False)
            hidden_hi(2 * B + NTILE - 1, 5)
            sl = act.value_load(eid[0:1, NTILE - 1:NTILE], min_val=1, max_val=E)
            y_out(2 * B + NTILE - 1, sl)

            def combine(g, r):
                n = 2 * g + r
                act.wait_ge(cmb_ve, n + 1)
                a.activation(small[:, 16:18], small[:, 12:14], ACT.Sqrt).then_inc(cmb_sd, 1)
                act.wait_ge(cmb_nmr, n + 1)
                for t in range(2):
                    a.activation(cmb[:, r, 2, t, :], cmb[:, r, 2, t, :], ACT.Identity, bias=small[:, 24 + t:25 + t],
                                 scale=small[:, 20 + t:21 + t]).then_inc(cmb_norm, 1)

            with act.Fori(0, NTB // 4) as g:
                combine(g, 0)
                combine(g, 1)

        @block.tensor
        def _(pe):
            te = nc.tensor
            pe.sem_inc(dn_done, FC)
            pe.wait_ge(const_made, 6)
            pe.wait_ge(wqkv_staged, 96)
            for n in range(8):
                wait(pe, setup_copied, n - 1)
                dst = att_bank(n)
                if n < 6:
                    k, j = n // 3, 2 * (n % 3)
                    for jj in range(2):
                        src = att[:, (j + jj) * D + k * P:(j + jj) * D + (k + 1) * P]
                        ins = te.transpose(dst[:, jj * P:(jj + 1) * P], src, ident[:, :])
                elif n == 6:
                    for k in range(KD):
                        for j in range(2):
                            src = att[:, 1536 + j * D + k * P:1536 + j * D + (k + 1) * P]
                            ins = te.transpose(dst[:, k * D + j * P:k * D + (j + 1) * P], src, ident[:, :])
                else:
                    for k in range(KD):
                        te.transpose(dst[:, k * E:(k + 1) * E], att[0:E, 2048 + k * P:2048 + (k + 1) * P], ident[0:E, 0:E])
                    for v in range(3):
                        ins = te.transpose(dst[:, 16 + 2 * v:18 + 2 * v], att[0:2, 2304 + v * P:2304 + (v + 1) * P], ident[0:2, 0:2])
                ins.then_inc(setup_turned, 1)
            pe.wait_ge(setup_copied, 8)

            def gate_up(t, c, slot, x, x_sem, x_count):
                q = t * FC + c
                if c == 0:
                    pe.wait_ge(x_sem, x_count)
                pe.wait_ge(h_made, q + 1)
                halves = ((c, 0), (5 + c, TW)) if c < FC - 1 else ((GJ - 1, 0),)
                for j, at in halves:
                    o = gu_ps[c % 2][:, at:at + TW]
                    n = 0
                    for k in range(KD):
                        for hw, hx in ((0, 0), (0, 1), (1, 0)):
                            ins = te.matmul(o, slot_gu(slot, hw, k, j), x(hx, k), start=(n == 0), stop=(n == 5))
                            n += 1
                ins.then_inc(gu_done, 1)

            def down(t, c, slot):
                q = t * FC + c
                if c == 0:
                    pe.wait_ge(y_made, (t + 1) * TT)
                pe.wait_ge(lo_made, q + 3)
                for tt in range(TT):
                    def h(hl):
                        at = (c * 2 + hl) * TW + tt * P
                        return hT[:, at:at + P]
                    pairs = ((0, 0), (0, 1), (1, 0)) if c < FC - 1 else ((0, 0), (0, 1))
                    for n, (hh, hw) in enumerate(pairs):
                        ins = te.matmul(y_ps[tt][:, 0:D], h(hh), slot_dn(slot, c, hw), start=(c == 0 and n == 0),
                                        stop=(c == FC - 1 and n == 1))
                ins.then_inc(dn_done, 1)

            def ffn_step(kind, n, t0, b):
                t, c = t0 + n // FC, n % FC
                if kind == "G":
                    u = n // FC
                    gate_up(t, c, 0, lambda h, k: xhl_v[:, h, k, u * TW:(u + 1) * TW], xhl_made, b * KD)
                else:
                    down(t, c, 0)

            def prep(s, n, gu, dn):
                what, k, j, w = GROUPS[n]
                if n == 0:
                    pe.wait_ge(stage_loaded, 96 * (s + 1))
                wait(pe, prep_lo, s * NG + n - 1)
                dst = prep_ps[n % 2]
                if what == "gu":
                    for jj in range(w):
                        ins = te.transpose(dst[:, jj * P:(jj + 1) * P], gu[:, j + jj, k * P:(k + 1) * P], ident[:, :])
                else:
                    for cc in range(w):
                        for t in range(KD):
                            ins = te.transpose(dst[:, cc * D + t * P:cc * D + (t + 1) * P], dn[:, t, (j + cc) * P:(j + cc + 1) * P], ident[:, :])
                ins.then_inc(prep_turned, 1)

            def turn(b, n, made, count):
                pe.wait_ge(made, count)
                for k in range(KD):
                    bank_ready(pe, b, n + k)
                    for t in range(NT):
                        ins = te.transpose(att_bank(n + k)[:, t * P:(t + 1) * P], xn[:, t, k * P:(k + 1) * P], ident[:, :])
                    ins.then_inc(att_done, 1)

            def batch(b):
                for step in ORDER:
                    kind = step[0]
                    if kind in "GD" and not isinstance(b, int):
                        ffn_step(kind, step[1], 2 * b - 2, b)
                    if kind == "turn1":
                        turn(b, TURN1, xn_made, b + 1)
                    if kind == "q":
                        pe.wait_ge(xTa_made, 2 * b + 1)
                        pe.wait_ge(xTb_made, 2 * b + 1)
                        for m in range(KD):
                            bank_ready(pe, b, QU + m)
                            for k in range(KD):
                                ins = te.matmul(att_bank(QU + m)[:, :], wqkvT[:, k, m * P:(m + 1) * P], xT[:, k, :], start=(k == 0), stop=(k == KD - 1))
                            ins.then_inc(att_done, 1)
                    if kind == "kv":
                        for t in range(NT):
                            bank_ready(pe, b, KVU + t)
                            for k in range(KD):
                                ins = te.matmul(att_bank(KVU + t)[:, :], xT[:, k, t * P:(t + 1) * P], wqkvT[:, k, D:3 * D], start=(k == 0), stop=(k == KD - 1))
                            ins.then_inc(att_done, 1)
                    if kind == "state":
                        pe.wait_ge(kv_made, NT * (b + 1))
                        bank_ready(pe, b, STATE)
                        for m in range(KD):
                            for t in range(NT):
                                ins = te.matmul(att_bank(STATE)[:, m * P:(m + 1) * P], kv[:, t, m * P:(m + 1) * P],
                                                kv[:, t, D + m * P:D + (m + 1) * P], start=(t == 0), stop=(t == NT - 1))
                        ins.then_inc(att_done, 1)
                    if kind == "ctx":
                        pe.wait_ge(state_made, b + 1)
                        pe.wait_ge(q_made, KD * (b + 1))
                        for m in range(KD):
                            bank_ready(pe, b, CTX + m)
                            te.matmul(att_bank(CTX + m)[:, :], state[:, m * P:(m + 1) * P], qT[:, m, :], start=True, stop=True).then_inc(att_done, 1)
                    if kind == "group_mean":
                        pe.wait_ge(gstat_made, 2 * b + 1)
                        bank_ready(pe, b, GMEAN)
                        te.matmul(att_bank(GMEAN)[:, 0:4], mask[:, :], gst[:, 0:4], start=True, stop=True).then_inc(att_done, 1)
                    if kind == "group_var":
                        pe.wait_ge(gstat_made, 2 * b + 2)
                        bank_ready(pe, b, GVAR)
                        te.matmul(att_bank(GVAR)[:, 0:2], mask[:, :], gst[:, 8:10], start=True, stop=True).then_inc(att_done, 1)
                    if kind == "out":
                        pe.wait_ge(ctxn_made, KD * (b + 1))
                        for h in range(2):
                            bank_ready(pe, b, OUT + h)
                            for t in (2 * h, 2 * h + 1):
                                for k in range(KD):
                                    ins = te.matmul(att_bank(OUT + h)[:, (t % 2) * D:(t % 2 + 1) * D], xT[:, k, t * P:(t + 1) * P], woT[:, k, :],
                                                    start=(k == 0), stop=(k == KD - 1))
                            ins.then_inc(att_done, 1)
                    if kind == "prep":
                        prep(b, step[1], stg_gu, stg_dn)
                    if kind == "turn2":
                        turn(b, TURN2, xn2_made, b + 1)
                    if kind == "logits":
                        pe.wait_ge(xTa_made, 2 * b + 2)
                        pe.wait_ge(xTb_made, 2 * b + 2)
                        bank_ready(pe, b, LOGIT)
                        for t in range(NT):
                            for k in range(KD):
                                ins = te.matmul(att_bank(LOGIT)[:, t * E:(t + 1) * E], xT[:, k, t * P:(t + 1) * P], gateT[:, k * E:(k + 1) * E],
                                                start=(k == 0), stop=(k == KD - 1))
                        ins.then_inc(att_done, 1)

            batch(0)
            with pe.Fori(1, B) as b:
                batch(b)
            for step in TAIL:
                kind = step[0]
                if kind in "GD":
                    ffn_step(kind, step[1], 2 * B - 2, B)
                if kind == "prep":
                    prep(B, step[1], last_gu, last_dn)
                if kind == "route_slots":
                    pe.wait_ge(m_made, 1)
                    pe.wait_ge(xTb_made, 2 * B)
                    te.matmul(att_ps[0][:, 0:256], upper[:, :], r_m, start=True, stop=True)
                    te.matmul(att_ps[0][:, 256:512], ones[:, :], r_m, start=True, stop=True).then_inc(counted, 1)
                if kind == "route_invert":
                    pe.wait_ge(logits_made, B)

                    def invert(n, r, start, stop):
                        pe.wait_ge(onehot_made, n + 1)
                        return te.matmul(att_ps[1][:, 0:NCOL], oh_lo[:, r, :], oh_hi[:, r, 0:NCOL], start=start, stop=stop)
                    invert(0, 0, True, False).then_inc(onehot_used, 1)
                    invert(1, 1, False, False).then_inc(onehot_used, 1)
                    with pe.Fori(2, 2 * NTB - 2, 2) as n:
                        invert(n, 0, False, False).then_inc(onehot_used, 1)
                        invert(n + 1, 1, False, False).then_inc(onehot_used, 1)
                    invert(2 * NTB - 2, 0, False, False).then_inc(onehot_used, 1)
                    invert(2 * NTB - 1, 1, False, True).then_inc(inverted, 1)

            pe.wait_ge(eid_made, 1)

            def turn_x(i, r, first):
                pe.wait_ge(xg_loaded[r], 16 * (i + 2 - r))
                if not first:
                    pe.wait_ge(xt_lo, i - 1)
                for k in range(KD):
                    for t in range(TT):
                        ins = te.transpose(xg_ps(r)[:, k, t * P:(t + 1) * P], xg[:, r, t, k * P:(k + 1) * P], ident[:, :])
                ins.then_inc(xg_turned, 1)

            def routed(i, r, slot, before, turn=True):
                t = 2 * B + i

                def gu(c):
                    gate_up(t, c, slot, lambda h, k: xt16[:, r, h, k, :], xt_lo, i + 1)
                gu(0)
                if before is not None:
                    down(t - 1, 4, before)
                gu(1)
                if before is not None:
                    down(t - 1, 5, before)
                gu(2)
                down(t, 0, slot)
                if turn:
                    turn_x(i + 1, 1 - r, isinstance(i, int) and i == 0)
                gu(3)
                down(t, 1, slot)
                gu(4)
                down(t, 2, slot)
                gu(5)
                down(t, 3, slot)

            pe.wait_ge(prep_lo, NSLOT * NG)
            turn_x(0, 0, True)
            slot0 = pe.value_load(eid[0:1, 0:1], min_val=1, max_val=E)
            routed(0, 0, slot0, None)
            with pe.Fori(1, NTILE - 2, 2) as i:
                s0 = pe.value_load(eid[0:1, bass.ds(i - 1, 1)], min_val=1, max_val=E)
                s1 = pe.value_load(eid[0:1, bass.ds(i, 1)], min_val=1, max_val=E)
                routed(i, 1, s1, s0)
                s2 = pe.value_load(eid[0:1, bass.ds(i + 1, 1)], min_val=1, max_val=E)
                routed(i + 1, 0, s2, s1)
            s0 = pe.value_load(eid[0:1, NTILE - 3:NTILE - 2], min_val=1, max_val=E)
            s1 = pe.value_load(eid[0:1, NTILE - 2:NTILE - 1], min_val=1, max_val=E)
            routed(NTILE - 2, 1, s1, s0)
            s2 = pe.value_load(eid[0:1, NTILE - 1:NTILE], min_val=1, max_val=E)
            routed(NTILE - 1, 0, s2, s1, turn=False)
            sl = pe.value_load(eid[0:1, NTILE - 1:NTILE], min_val=1, max_val=E)
            down(2 * B + NTILE - 1, 4, sl)
            down(2 * B + NTILE - 1, 5, sl)

        @block.vector
        def _(dve):
            v = nc.vector
            dve.sem_inc(h_made, 2)
            dve.sem_inc(lo_made, 2)
            dve.wait_ge(setup_copied, 8)
            dve.wait_ge(setup_loaded, 32)
            dve.wait_ge(const_made, 6)
            LINKS = 15
            links = [0]

            def linked(ins, b):
                ins.then_inc(link_v, 1)
                links[0] += 1
                dve.wait_ge(link_v, 1 + b * LINKS + links[0])

            def stats(src, b, n):
                for t in range(NT):
                    ins = v.bn_stats(st6[:, 6 * t:6 * t + 6], src[:, t, :])
                linked(ins, b)
                passed(dve)
                for t in range(NT):
                    ins = v.bn_aggr(mv[:, 2 * t:2 * t + 2], st6[:, 6 * t:6 * t + 6])
                linked(ins, b)
                v.tensor_scalar(ve[:, :], mv[:, :].rearrange("p (t s) -> p t s", s=2)[:, :, 1], EPS, None, ALU.add).then_inc(ve_made, 1)
                dve.wait_ge(rstd_made, 4 * b + n + 1)

            def normalise(dst, src):
                for t in range(NT):
                    ins = v.tensor_scalar(dst[:, t, :], src[:, t, :], mv[:, 2 * t:2 * t + 1], rstd[:, t:t + 1], ALU.subtract, ALU.mult)
                return ins

            def gate_up(t, c, slot):
                q = t * FC + c
                dve.wait_ge(silu_made, q + 1)
                dve.wait_ge(lo_made, q + 1)
                lo = 0 if c < FC - 1 else 64
                up = gu_ps[c % 2][:, TW:2 * TW] if c < FC - 1 else gu_ps[1][64:P, 0:TW]
                v.scalar_tensor_tensor(out=hf[lo:P, c % 2 * TW:(c % 2 + 1) * TW], in0=up, scalar=scale_of(slot, 1, lo, P),
                                       in1=silu[lo:P, c % 2 * TW:(c % 2 + 1) * TW], op0=ALU.mult, op1=ALU.mult).then_inc(h_made, 1)

            def hidden_lo(t, c):
                q = t * FC + c
                dve.wait_ge(hi_made, q + 1)
                h = hf[:, c % 2 * TW:(c % 2 + 1) * TW]
                hi = hT[:, c * 2 * TW:c * 2 * TW + TW]
                lo = hT[:, c * 2 * TW + TW:(c + 1) * 2 * TW]
                if c < FC - 1:
                    v.tensor_tensor(lo, h, hi, ALU.subtract).then_inc(lo_made, 1)
                else:
                    v.tensor_tensor(hi[64:P], h[64:P], hi[64:P], ALU.subtract).then_inc(lo_made, 1)

            def ffn_step(kind, n, t0, slot):
                if kind == "G":
                    gate_up(t0 + n // FC, n % FC, slot)
                    if n > 0:
                        hidden_lo(t0 + (n - 1) // FC, (n - 1) % FC)
                    if n == 2 * FC - 1:
                        hidden_lo(t0 + n // FC, n % FC)

            def prep_scale(s, gu, dn):
                dve.wait_ge(stage_loaded, 96 * (s + 1))
                v.tensor_reduce(mx[:, 0:1], gu, AX.XY, ALU.max, apply_absolute_value=True)
                v.tensor_reduce(mx[:, 1:2], dn, AX.XY, ALU.max, apply_absolute_value=True).then_inc(max_made, 1)
                dve.wait_ge(maxall_made, s + 1)
                base = 1 + B * LINKS if isinstance(s, int) and s == B else None

                def l2(ins):
                    linked(ins, s)
                l2(v.tensor_scalar(pw[:, 0:2], mxa[:, :], 2.0 ** -30, None, ALU.max))
                l2(v.tensor_scalar(pw[:, 2:4].bitcast(I32), pw[:, 0:2].bitcast(I32), 0x7F800000, None, ALU.bitwise_and))
                l2(v.reciprocal(pw[:, 0:2], pw[:, 2:4]))
                v.tensor_scalar(pw[:, 4:6], pw[:, 0:2], 2.0 ** 14, None, ALU.mult)
                v.tensor_scalar(scale_of(s, 0), pw[:, 2:3], 2.0 ** -14 / X_SCALE, None, ALU.mult)
                v.tensor_scalar(scale_of(s, 1), pw[:, 0:1], 2.0 ** -17 / X_SCALE, None, ALU.mult)
                l2(v.scalar_tensor_tensor(out=pw[:, 6:7], in0=pw[:, 2:3], scalar=pw[:, 2:3], in1=pw[:, 3:4], op0=ALU.mult, op1=ALU.mult))
                v.tensor_scalar(scale_of(s, 2), pw[:, 6:7], 2.0 ** -11, None, ALU.mult).then_inc(scale_made, 1)

            def prep(s, n):
                what, k, j, w = GROUPS[n]
                dve.wait_ge(prep_hi, s * NG + n + 1)
                if what == "gu":
                    v.scalar_tensor_tensor(out=slot_gu(s, 1, k, j, w), in0=prep_ps[n % 2][:, 0:w * P], scalar=pw[:, 4:5],
                                           in1=slot_gu(s, 0, k, j, w), op0=ALU.mult, op1=ALU.subtract).then_inc(prep_lo, 1)
                else:
                    dst = wdn[:, bass.ds(s * SLOT_DN + j * 2 * D, 4 * D)].rearrange("p (c h d) -> p c h d", c=2, h=2)
                    v.scalar_tensor_tensor(out=dst[:, :, 1, :], in0=prep_ps[n % 2][:, :].rearrange("p (c d) -> p c d", c=2), scalar=pw[:, 5:6],
                                           in1=dst[:, :, 0, :], op0=ALU.mult, op1=ALU.subtract).then_inc(prep_lo, 1)

            def batch(b):
                links[0] = 0
                for step in ORDER:
                    kind = step[0]
                    if kind in "GD" and not isinstance(b, int):
                        ffn_step(kind, step[1], 2 * b - 2, 0)
                    if kind == "ln1":
                        dve.wait_ge(x_loaded, 16 * (b + 1))
                        stats(xres, b, 0)
                        if not isinstance(b, int):
                            dve.wait_ge(xn2_stored, 16 * b)
                            dve.wait_ge(att_done, USES * b)
                        normalise(xn, xres).then_inc(xn_made, 1)
                    if kind == "turn1":
                        use_done(dve, b, TURN1 + 1)
                        v.tensor_copy(xT[:, 1, :], att_bank(TURN1 + 1)[:, :]).then_inc(xTb_made, 1)
                    if kind == "kv":
                        for t in range(NT):
                            use_done(dve, b, KVU + t)
                            v.tensor_tensor(kv[:, t, :], att_bank(KVU + t)[:, :], kvb, ALU.add).then_inc(kv_made, 1)
                    if kind == "state":
                        use_done(dve, b, STATE)
                        for m in range(KD):
                            ins = v.tensor_tensor(state[:, m * P:(m + 1) * P], att_bank(STATE)[:, m * P:(m + 1) * P], mask[:, :], ALU.mult)
                        ins.then_inc(state_made, 1)
                    if kind == "prep_scale":
                        prep_scale(b, stg_gu, stg_dn)
                    if kind == "prep":
                        prep(b, step[1])
                    if kind == "group_mean":
                        dve.wait_ge(ctx_made, KD * (b + 1))
                        for m in range(KD):
                            ins = v.bn_stats(st6[:, 6 * m:6 * m + 6], xT[:, m, :])
                        linked(ins, b)
                        passed(dve)
                        for m in range(KD):
                            ins = v.bn_aggr(gst[:, 2 * m:2 * m + 2], st6[:, 6 * m:6 * m + 6])
                        ins.then_inc(gstat_made, 1)
                        use_done(dve, b, GMEAN)
                        v.tensor_scalar(gst[:, 4:8], att_bank(GMEAN)[:, 0:4], 1.0 / HD, None, ALU.mult).then_inc(gmean_made, 1)
                        dve.wait_ge(gmean_made, b + 1)
                        g3 = gst[:, 0:8].rearrange("p (w m s) -> p w m s", w=2, s=2)
                        linked(v.tensor_tensor(gst[:, 10:12], g3[:, 0, :, 0], g3[:, 1, :, 0], ALU.subtract), b)
                        v.tensor_tensor(gst[:, 8:10], gst[:, 10:12], gst[:, 10:12], ALU.mult).then_inc(gstat_made, 1)
                    if kind == "ctx_norm":
                        use_done(dve, b, GVAR)
                        g3 = gst[:, 0:8].rearrange("p (w m s) -> p w m s", w=2, s=2)
                        v.scalar_tensor_tensor(out=gst[:, 12:14], in0=att_bank(GVAR)[:, 0:2], scalar=1.0 / HD, in1=g3[:, 1, :, 1],
                                               op0=ALU.mult, op1=ALU.add).then_inc(gvar_made, 1)
                        dve.wait_ge(gvar_made, b + 1)
                        v.tensor_scalar(ve[:, 0:KD], gst[:, 12:14], EPS, None, ALU.add).then_inc(ve_made, 1)
                        dve.wait_ge(rstd_made, 4 * b + 2)
                        linked(v.tensor_tensor(gst[:, 12:14], rstd[:, 0:KD], colv[:, 2:4], ALU.mult), b)
                        linked(v.tensor_tensor(gst[:, 14:16], g3[:, 1, :, 0], gst[:, 12:14], ALU.mult), b)
                        linked(v.tensor_tensor(gst[:, 10:12], colv[:, 4:6], gst[:, 14:16], ALU.subtract), b)
                        for m in range(KD):
                            v.tensor_scalar(xT[:, m, :], xT[:, m, :], gst[:, 12 + m:13 + m], gst[:, 10 + m:11 + m], ALU.mult, ALU.add).then_inc(ctxn_made, 1)
                    if kind == "out":
                        for h in range(2):
                            use_done(dve, b, OUT + h)
                            for t in (2 * h, 2 * h + 1):
                                ins = v.tensor_tensor(orow[:, t, :], att_bank(OUT + h)[:, (t % 2) * D:(t % 2 + 1) * D], outb, ALU.add)
                            ins.then_inc(o_made, 1)
                    if kind == "lno":
                        dve.wait_ge(o_made, 2 * (b + 1))
                        stats(orow, b, 2)
                        v.scalar_tensor_tensor(out=nmr[:, :], in0=mv[:, :].rearrange("p (t s) -> p t s", s=2)[:, :, 0], scalar=-1.0,
                                               in1=rstd[:, :], op0=ALU.mult, op1=ALU.mult).then_inc(nmr_made, 1)
                        dve.wait_ge(o_scaled, NT * (b + 1))
                        v.tensor_tensor(att[:, 0:1024], att[:, 0:1024], att[:, 2048:3072], ALU.add).then_inc(x2_made, 1)
                        dve.wait_ge(x2_made, b + 1)
                        stats(xres, b, 3)
                        normalise(xn, xres).then_inc(xn2_made, 1)
                    if kind == "turn2":
                        use_done(dve, b, TURN2 + 1)
                        v.tensor_copy(xT[:, 1, :], att_bank(TURN2 + 1)[:, :]).then_inc(xTb_made, 1)
                        for k in range(KD):
                            dve.wait_ge(xTb_made, 2 * b + 2)
                            dve.wait_ge(hi_x_made, KD * b + k + 1)
                            v.scalar_tensor_tensor(out=xhl_v[:, 1, k, :], in0=xT[:, k, :], scalar=X_SCALE, in1=xhl_v[:, 0, k, :],
                                                   op0=ALU.mult, op1=ALU.subtract).then_inc(xhl_made, 1)
                assert links[0] == LINKS, links[0]

            batch(0)
            with dve.Fori(1, B) as b:
                batch(b)

            rlinks = [0]

            def rl(ins):
                ins.then_inc(rt_link, 1)
                rlinks[0] += 1
                dve.wait_ge(rt_link, rlinks[0])

            def te8(a):
                return a.rearrange("p (t e) -> p t e", e=E)

            def by_tile(a):
                return a.rearrange("p (t o) -> p t o", o=1).to_broadcast([P, NTB, E])

            rev_b = rev[:, :].rearrange("p (o e) -> p o e", o=1).to_broadcast([P, NTB, E])
            m1, m2, mr, ms = (small[:, 32 * n:32 * n + 32] for n in range(4))
            ends, tiles, tiles_i, base_, n255 = (small[:, 128 + 8 * n:136 + 8 * n] for n in range(5))
            one8 = small[:, 168:176]

            def first_of(dst, top):
                rl(v.tensor_reduce(top, te8(r_p), AX.X, ALU.max))
                rl(v.tensor_tensor(te8(r_x), te8(r_p), by_tile(top), ALU.is_equal))
                rl(v.tensor_tensor(te8(r_x), te8(r_x), rev_b, ALU.mult))
                rl(v.tensor_reduce(mr, te8(r_x), AX.X, ALU.max))
                rl(v.tensor_tensor(te8(dst), rev_b, by_tile(mr), ALU.is_equal))

            links[0] = 0
            for step in TAIL:
                kind = step[0]
                if kind in "GD":
                    ffn_step(kind, step[1], 2 * B - 2, 0)
                if kind == "prep_scale":
                    prep_scale(B, last_gu, last_dn)
                if kind == "prep":
                    prep(B, step[1])
                if kind == "route_probs":
                    dve.wait_ge(logits_made, B)
                    rl(v.tensor_reduce(ms, te8(logits[:, :]), AX.X, ALU.max))
                    v.tensor_tensor(te8(r_t), te8(logits[:, :]), by_tile(ms), ALU.subtract).then_inc(diff_made, 1)
                if kind == "route_top1":
                    dve.wait_ge(exp_made, 1)
                    rl(v.tensor_reduce(ms, te8(r_p), AX.X, ALU.add))
                    rl(v.reciprocal(mr, ms))
                    rl(v.tensor_tensor(te8(r_p), te8(r_p), by_tile(mr), ALU.mult))
                    first_of(r_o1, m1)
                if kind == "route_top2":
                    rl(v.scalar_tensor_tensor(out=r_p, in0=r_o1, scalar=-2.0, in1=r_p, op0=ALU.mult, op1=ALU.add))
                    first_of(r_o2, m2)
                    v.tensor_tensor(r_m, r_o1, r_o2, ALU.add).then_inc(m_made, 1)
                    rl(v.tensor_tensor(ms, m1, m2, ALU.add))
                    rl(v.tensor_scalar(ms, ms, 1e-20, None, ALU.add))
                    rl(v.reciprocal(mr, ms))
                    v.tensor_tensor(wts[:, 0:NTB], m1, mr, ALU.mult)
                    v.tensor_tensor(wts[:, NTB:2 * NTB], m2, mr, ALU.mult)
                    rl(v.memset(one8, 1.0))
                if kind == "route_slots":
                    dve.wait_ge(counted, 1)
                    rl(v.tensor_copy(r_c, att_ps[0][:, 256:512]))
                    for e in range(E):
                        ins = v.tensor_tensor_scan(te8(r_s)[:, :, e], ones[:, 0:NTB], te8(r_c)[:, :, e], 0.0, ALU.mult, ALU.add)
                    rl(ins)
                    rl(v.tensor_tensor(r_x, r_s, r_c, ALU.subtract))
                    rl(v.tensor_tensor(r_x, r_x, att_ps[0][:, 0:256], ALU.add))
                    rl(v.tensor_scalar(n255.bitcast(I32), te8(r_s)[:, NTB - 1, :], float(TW - 1), None, ALU.add))
                    rl(v.tensor_scalar(tiles_i.bitcast(I32), n255.bitcast(I32), 8, None, ALU.logical_shift_right))
                    rl(v.tensor_copy(tiles, tiles_i.bitcast(I32)))
                    rl(v.tensor_tensor_scan(ends, one8, tiles, 0.0, ALU.mult, ALU.add))
                    rl(v.tensor_tensor(base_, ends, tiles, ALU.subtract))
                    rl(v.tensor_scalar(base_, base_, float(TW), None, ALU.mult))
                    rl(v.tensor_tensor(te8(r_x), te8(r_x), base_.rearrange("p (o e) -> p o e", o=1).to_broadcast([P, NTB, E]), ALU.add))
                if kind == "route_positions":
                    for n, oh in enumerate((r_o1, r_o2)):
                        rl(v.tensor_tensor(r_c, oh, r_x, ALU.mult))
                        rl(v.tensor_reduce(posf[:, n * NTB:(n + 1) * NTB], te8(r_c), AX.X, ALU.add))
                    e3 = attw[:, 0:NTILE * E].rearrange("p (i e) -> p i e", e=E)
                    rl(v.tensor_tensor(e3, iota[:, 0:NTILE].rearrange("p (i o) -> p i o", o=1).to_broadcast([P, NTILE, E]),
                                       ends.rearrange("p (o e) -> p o e", o=1).to_broadcast([P, NTILE, E]), ALU.is_ge))
                    rl(v.tensor_reduce(attw[:, 512:512 + NTILE], e3, AX.X, ALU.add))
                    v.tensor_scalar(eid[:, :], attw[:, 512:512 + NTILE], float(E - 1), 1.0, ALU.min, ALU.add).then_inc(eid_made, 1)
                    rl(v.tensor_copy(posi[:, :], posf))
                    rl(v.tensor_scalar(lohi_i[:, :], posi[:, :], P - 1, None, ALU.bitwise_and))
                    rl(v.tensor_copy(lof, lohi_i[:, :]))
                    rl(v.tensor_scalar(lohi_i[:, :], posi[:, :], 7, None, ALU.logical_shift_right))
                    rl(v.tensor_copy(hif, lohi_i[:, :]))
                if kind == "route_invert":
                    def onehots(half, j, r, n, first):
                        if not first:
                            dve.wait_ge(onehot_used, n - 1)
                        v.tensor_scalar(oh_lo[:, r, :], iota[:, :], lof[:, bass.ds(half * NTB + j, 1)], None, ALU.is_equal)
                        v.tensor_scalar(oh_hi[:, r, 0:NCOL], iota[:, 0:NCOL], hif[:, bass.ds(half * NTB + j, 1)],
                                        tokf[:, bass.ds(j, 1)], ALU.is_equal, ALU.mult).then_inc(onehot_made, 1)
                    onehots(0, 0, 0, 0, True)
                    onehots(1, 0, 1, 1, True)
                    with dve.Fori(1, NTB) as j:
                        onehots(0, j, 0, 2 * j, False)
                        onehots(1, j, 1, 2 * j + 1, False)
                    dve.wait_ge(inverted, 1)
                    v.tensor_copy(idx[:, :], att_ps[1][:, 0:NCOL]).then_inc(idx_made, 1)

            def turned_x(i, r):
                dve.wait_ge(xt_hi, i + 1)
                v.scalar_tensor_tensor(out=xt16[:, r, 1].rearrange("p k s -> p (k s)"), in0=ps[6 + r][:, :], scalar=X_SCALE,
                                       in1=xt16[:, r, 0].rearrange("p k s -> p (k s)"), op0=ALU.mult, op1=ALU.subtract).then_inc(xt_lo, 1)

            def routed(i, r, slot, before, turn=True):
                t = 2 * B + i

                def gu(c):
                    gate_up(t, c, slot)
                gu(0)
                if before:
                    hidden_lo(t - 1, 5)
                gu(1)
                hidden_lo(t, 0)
                gu(2)
                hidden_lo(t, 1)
                gu(3)
                hidden_lo(t, 2)
                if turn:
                    turned_x(i + 1, 1 - r)
                gu(4)
                hidden_lo(t, 3)
                gu(5)
                hidden_lo(t, 4)

            turned_x(0, 0)
            slot0 = dve.value_load(eid[0:1, 0:1], min_val=1, max_val=E)
            routed(0, 0, slot0, False)
            with dve.Fori(1, NTILE - 2, 2) as i:
                s1 = dve.value_load(eid[0:1, bass.ds(i, 1)], min_val=1, max_val=E)
                routed(i, 1, s1, True)
                s2 = dve.value_load(eid[0:1, bass.ds(i + 1, 1)], min_val=1, max_val=E)
                routed(i + 1, 0, s2, True)
            s1 = dve.value_load(eid[0:1, NTILE - 2:NTILE - 1], min_val=1, max_val=E)
            routed(NTILE - 2, 1, s1, True)
            s2 = dve.value_load(eid[0:1, NTILE - 1:NTILE], min_val=1, max_val=E)
            routed(NTILE - 1, 0, s2, True, turn=False)
            hidden_lo(2 * B + NTILE - 1, 5)

            CL = 5

            def combine(g, r):
                n = 2 * g + r
                k = [0]

                def cl(ins):
                    ins.then_inc(cmb_link, 1)
                    k[0] += 1
                    dve.wait_ge(cmb_link, n * CL + k[0])
                dve.wait_ge(gath[r], 64 * (g + 1))
                dve.wait_ge(cmb_loaded[r], 32 * (g + 1))
                for a in range(2):
                    for t in range(2):
                        ins = v.scalar_tensor_tensor(out=cmb[:, r, 2, t, :], in0=cmb[:, r, a, t, :], scalar=wts[:, bass.ds(a * NTB + 2 * n + t, 1)],
                                                     in1=cmb[:, r, 2, t, :], op0=ALU.mult, op1=ALU.add)
                    cl(ins)
                for t in range(2):
                    ins = v.bn_stats(st6[:, 6 * t:6 * t + 6], cmb[:, r, 2, t, :])
                cl(ins)
                passed(dve)
                for t in range(2):
                    ins = v.bn_aggr(mv[:, 2 * t:2 * t + 2], st6[:, 6 * t:6 * t + 6])
                cl(ins)
                m3 = mv[:, 0:4].rearrange("p (t s) -> p t s", s=2)
                v.tensor_scalar(small[:, 12:14], m3[:, :, 1], EPS, None, ALU.add).then_inc(cmb_ve, 1)
                dve.wait_ge(cmb_sd, n + 1)
                cl(v.reciprocal(small[:, 20:22], small[:, 16:18]))
                v.scalar_tensor_tensor(out=small[:, 24:26], in0=m3[:, :, 0], scalar=-1.0, in1=small[:, 20:22], op0=ALU.mult, op1=ALU.mult).then_inc(cmb_nmr, 1)
                dve.wait_ge(cmb_norm, 2 * n + 2)
                v.tensor_tensor(cmb[:, r, 3], cmb[:, r, 3], cmb[:, r, 2], ALU.add).then_inc(out_made, 1)
                assert k[0] == CL

            with dve.Fori(0, NTB // 4) as g:
                combine(g, 0)
                combine(g, 1)


_INS = ["L0_attn_x", "L0_attn_Wqkv_w", "L0_attn_Wqkv_b", "L0_attn_gn_w", "L0_attn_gn_b", "L0_attn_out_w", "L0_attn_out_b",
        "L0_ffn_gate_w", "L0_ffn_expert_gate", "L0_ffn_expert_up", "L0_ffn_expert_down", "L0_ffn_shared_gate", "L0_ffn_shared_up",
        "L0_ffn_shared_down"]


def kernel(**inputs):
    import numpy as _np
    import concourse.bacc as _bacc
    from concourse.bass_utils import run_bass_kernel_spmd as _run

    nc = _bacc.Bacc("TRN2", target_bir_lowering=False, num_devices=1)
    arrays, args = {}, []
    for name in _INS:
        a = _np.ascontiguousarray(inputs[name])
        arrays[f"in_{name}"] = a
        args.append(nc.dram_tensor(f"in_{name}", a.shape, mybir.dt.from_np(a.dtype), kind="ExternalInput").ap())
    args.append(nc.dram_tensor("out_x", (B, S, D), F32, kind="ExternalOutput").ap())
    build(nc, *args)
    r = _run(nc, [arrays], core_ids=[0])
    return r.results[0]["out_x"]
```

```python
from contextlib import ExitStack

import concourse.bass as bass
from concourse import mybir

F32 = mybir.dt.float32
F16 = mybir.dt.float16
I32 = mybir.dt.int32
ALU = mybir.AluOpType
ACT = mybir.ActivationFunctionType
AX = mybir.AxisListType

P = 128
B, S, D = 8, 512, 256
HD = 8
TOK = B * S
NT = S // P
KD = D // P
E = 8
F = 704
FC = 6
GU = 2 * F
GJ = GU // P
TW = 256
TT = TW // P
NTILE = 2 * TOK // TW + E - 1
NCOL = NTILE * TT
NTB = TOK // P
EPS = 1e-5
X_SCALE = 2.0 ** 11
SLOT_GU = 2 * KD * GU
SLOT_DN = FC * 2 * D
NSLOT = E + 1

ORDER = [("ln1_stats",), ("G", 0), ("H", 0), ("ctx",), ("ctx_out",), ("G", 1), ("channel_stats",), ("H", 1), ("prep_end", 4), ("G", 2),
         ("group_mean",), ("D", 0), ("H", 2), ("group_var",), ("G", 3), ("D", 1), ("H", 3), ("prep_end", 5), ("ctx_norm",), ("G", 4), ("D", 2), ("H", 4),
         ("ln1_apply",), ("out",), ("out_out",), ("prep_end", 6), ("G", 5), ("D", 3), ("H", 5), ("turn1",), ("turn1_out",), ("lno_stats",),
         ("prep_end", 7), ("G", 6), ("D", 4), ("H", 6), ("q",), ("lno_apply",), ("q_out",), ("prep_end", 8), ("G", 7), ("D", 5), ("H", 7),
         ("kv", 0), ("kv_out", 0), ("x2",), ("G", 8), ("D", 6), ("H", 8), ("kv", 1), ("kv_out", 1), ("prep_max", 0), ("kv", 2), ("kv_out", 2),
         ("G", 9), ("D", 7), ("H", 9), ("prep_max", 1), ("ln2_apply",), ("kv", 3), ("kv_out", 3), ("prep_max", 2), ("G", 10), ("D", 8), ("H", 10),
         ("turn2",), ("turn2_out",), ("prep_max", 3), ("state",), ("state_out",), ("prep_scale",), ("logits",), ("logits_out",),
         ("G", 11), ("D", 9), ("H", 11), ("prep", 0), ("prep", 1), ("xhl",), ("D", 10), ("prep", 2), ("D", 11), ("prep", 3)]
FIRST_HALF = ("ln1_stats", "ln1_apply", "turn1", "turn1_out", "q", "q_out", "kv", "kv_out", "state", "state_out")
LAST_ORDER = [("route_probs", 0), ("G", 0), ("H", 0), ("ctx",), ("ctx_out",), ("G", 1), ("channel_stats",), ("H", 1), ("prep_end", 4), ("G", 2),
              ("group_mean",), ("D", 0), ("H", 2), ("group_var",), ("G", 3), ("D", 1), ("ctx_norm",), ("H", 3), ("prep_end", 5), ("out",), ("out_out",),
              ("G", 4), ("D", 2), ("H", 4), ("lno_stats",), ("prep_end", 6), ("G", 5), ("D", 3), ("H", 5), ("lno_apply",), ("prep_end", 7),
              ("G", 6), ("D", 4), ("H", 6), ("x2",), ("prep_end", 8), ("G", 7), ("D", 5), ("H", 7), ("route_top1", 0), ("G", 8), ("D", 6), ("H", 8),
              ("ln2_apply",), ("G", 9), ("D", 7), ("H", 9), ("turn2",), ("turn2_out",), ("G", 10), ("D", 8), ("H", 10), ("G", 11), ("H", 11), ("xhl",),
              ("logits",), ("logits_out",), ("route_top2", 0), ("D", 9), ("D", 10), ("route_probs", 1), ("D", 11)]
TAIL = [("G", 0), ("H", 0), ("G", 1), ("route_top1", 1), ("H", 1), ("G", 2), ("D", 0), ("H", 2), ("route_top2", 1), ("G", 3), ("D", 1), ("H", 3),
        ("prep_max", 0), ("route_slots",), ("prep_max", 1), ("G", 4), ("D", 2), ("H", 4), ("prep_max", 2), ("G", 5), ("route_positions",), ("prep_max", 3),
        ("one_hots", 0), ("G", 6), ("H", 5), ("invert", 0), ("D", 3), ("prep_scale",), ("one_hots", 1), ("prep", 0), ("G", 7), ("H", 6), ("invert", 1), ("D", 4),
        ("one_hots", 2), ("prep", 1), ("G", 8), ("H", 7), ("invert", 2), ("D", 5), ("one_hots", 3), ("prep", 2), ("G", 9), ("H", 8), ("invert", 3), ("D", 6),
        ("one_hots", 4), ("prep", 3), ("G", 10), ("H", 9), ("invert", 4), ("D", 7), ("one_hots", 5), ("prep", 4), ("G", 11), ("H", 10), ("invert", 5), ("D", 8),
        ("one_hots", 6), ("prep", 5), ("H", 11), ("invert", 6), ("D", 9), ("one_hots", 7), ("D", 10), ("invert", 7), ("D", 11), ("route_indices",),
        ("prep", 6), ("prep", 7), ("prep", 8)]

CTX, GMEAN, GVAR, OUT, TURN1, QU, TURN2, STATE, LOGIT = 0, 2, 3, 4, 6, 8, 14, 16, 17
KV_USES = [10, 11, 12, 13]
USES_FIRST = [TURN1, TURN1 + 1, QU, QU + 1] + KV_USES + [STATE]
USES_SECOND = [CTX, CTX + 1, GMEAN, GVAR, OUT, OUT + 1, TURN2, TURN2 + 1, LOGIT]


def uses(b):
    first = USES_FIRST if not isinstance(b, int) or b < B - 1 else []
    second = USES_SECOND if not isinstance(b, int) or b >= 0 else []
    return sorted(first + second)


def build(nc, x_in, Wqkv, bqkv, gn_w, gn_b, Wout, bout, gate_w, eg, eu, ed, sg, su, sd, out):
    xf = x_in.rearrange("b s d -> (b s) d")
    of = out.rearrange("b s d -> (b s) d")
    with ExitStack() as ctx:
        def sb(name, cols, dt=F32, parts=P):
            return ctx.enter_context(nc.sbuf_tensor(name, [parts, cols], dt))

        def sem(name):
            return ctx.enter_context(nc.semaphore(name))

        xn2_d = nc.dram_tensor("xn2_d", (TOK, D + E), F32, kind="Internal").ap()
        x2_d = nc.dram_tensor("x2_d", (TOK, D), F32, kind="Internal").ap()
        acc_d = nc.dram_tensor("acc_d", (TOK + P, D), F32, kind="Internal").ap()

        wgu = sb("wgu", NSLOT * SLOT_GU, F16)
        wdn = sb("wdn", NSLOT * SLOT_DN, F16)
        att = sb("att", 5120)
        xres = att[:, 0:1024].rearrange("p (t d) -> p t d", t=NT)
        xn = att[:, 1024:2048].rearrange("p (t d) -> p t d", t=NT)
        kv = att[:, 1024:3072].rearrange("p (t c) -> p t c", t=NT)
        orow = att[:, 2048:3072].rearrange("p (t d) -> p t d", t=NT)
        xT = att[:, 3072:4096].rearrange("p (k s) -> p k s", k=KD)
        qT = att[:, 4096:5120].rearrange("p (k s) -> p k s", k=KD)
        xhl = sb("xhl", 2 * KD * S, F16)
        xhl_v = xhl[:, :].rearrange("p (h k s) -> p h k s", h=2, k=KD)
        attw = sb("attw", 2816)
        wqkvT = attw[:, 0:1536].rearrange("p (k c) -> p k c", k=KD)
        woT = attw[:, 1536:2048].rearrange("p (k c) -> p k c", k=KD)
        kvb = attw[:, 2048:2560]
        outb = attw[:, 2560:2816]
        silu = sb("silu", 2 * TW)
        hf = sb("hf", 2 * TW)
        hT = sb("hT", FC * 2 * TW, F16)
        ysb = sb("ysb", TT * D)
        ident = sb("ident", P)
        mask = sb("mask", P)
        upper = sb("upper", P)
        ones = sb("ones", P)
        iota = sb("iota", P)
        iota_i = silu[:, 0:P].bitcast(I32)
        rev = sb("rev", E)
        state = sb("state", KD * P)
        logits = sb("logits", NTB * E)
        gateT = sb("gateT", KD * E)
        sc = sb("sc", NSLOT * 4)
        colv = sb("colv", 8)
        LN1, GN, LNO, LN2 = range(4)
        st6a, mva, vea, rstda = (sb(f"{name}", 4 * NT * w) for name, w in (("st6", 6), ("mv", 2), ("ve", 1), ("rstd", 1)))
        st6, mv, ve, rstd = ([arr[:, NT * w * n:NT * w * (n + 1)] for n in range(4)] for arr, w in ((st6a, 6), (mva, 2), (vea, 1), (rstda, 1)))
        nmr = sb("nmr", NT)
        mhalf = sb("mhalf", NT)
        gst = sb("gst", 16)
        mx = sb("mx", 4)
        mxa = sb("mxa", 4)
        pw = sb("pw", 8)
        small = sb("small", 176)
        tokf = sb("tokf", NTB)
        posi = sb("posi", 2 * NTB, I32)
        wts = sb("wts", 2 * NTB)
        lohi_i = sb("lohi_i", 2 * NTB, I32)
        idx = sb("idx", NCOL, I32)
        idxc = sb("idxc", 8, I32)
        yw = sb("yw", 4)
        eid = sb("eid", NTILE, I32)

        stg_gu = wgu[:, E * SLOT_GU:].bitcast(F32).rearrange("p (j d) -> p j d", j=GJ)
        stg_dn = wdn[:, E * SLOT_DN:].bitcast(F32).rearrange("p (t f) -> p t f", t=KD)
        last_gu = att[:, 0:2816].rearrange("p (j d) -> p j d", j=GJ)
        last_dn = att[:, 2816:4352].rearrange("p (t f) -> p t f", t=KD)

        def rt(n):
            return attw[:, 256 * n:256 * n + 256]
        r_p, r_t, r_o1, r_o2, r_m, r_c, r_s, r_x = (rt(n) for n in range(8))
        PART = ((0, NTB - NT), (NTB - NT, NTB))

        def part_of(a, n, per=E):
            return a[:, PART[n][0] * per:PART[n][1] * per]

        OHB = 4
        oh_lo = attw[:, 2048:2560].bitcast(F16).rearrange("p (h m c) -> p h m c", h=OHB, m=2)
        oh_hi = att[:, 4352:4672].bitcast(F16).rearrange("p (h m c) -> p h m c", h=OHB, m=2)
        iota16 = att[:, 4672:4736].bitcast(F16)
        posf, lof, hif = (attw[:, 2560 + 2 * NTB * n:2560 + 2 * NTB * (n + 1)] for n in range(3))
        cmb_dev = [small[:, NT * r:NT * (r + 1)] for r in range(4)]
        cmb_shift = [small[:, 16 + NT * r:16 + NT * (r + 1)] for r in range(4)]
        idx_s = ones[:, 0:NCOL].bitcast(I32)
        xg = attw[:, 0:2 * TT * (D + E)].rearrange("p (r t d) -> p r t d", r=2, t=TT)
        xt16 = att[:, 0:1024].bitcast(F16).rearrange("p (r h k s) -> p r h k s", r=2, h=2, k=KD)
        GB = 4
        NGRP = B // GB
        y_rows = wgu[:, 0:B * 2048].bitcast(F32).rearrange("p (n t d) -> p n t d", n=B, t=NT)
        x2_rows = wdn[:, 0:B * 2048].bitcast(F32).rearrange("p (n t d) -> p n t d", n=B, t=NT)

        def rows_of(arr, g, r):
            return arr[:, bass.ds(GB * g + r, 1)].rearrange("p n t d -> p (n t) d")

        ps = [ctx.enter_context(nc.psum_tensor(f"ps{i}", [P, 512], F32)) for i in range(8)]
        gu_ps, y_ps, att_ps, prep_ps = ps[0:2], ps[2:4], ps[4:6], ps[6:8]

        const_made = sem("const_made")
        wait_passed = sem("wait_passed")
        setup_loaded = sem("setup_loaded")
        wqkv_staged = sem("wqkv_staged")
        setup_turned = sem("setup_turned")
        setup_copied = sem("setup_copied")
        x_loaded = sem("x_loaded")
        stage_loaded = sem("stage_loaded")
        x2_made = sem("x2_made")
        xn2_made = sem("xn2_made")
        x2_stored = sem("x2_stored")
        xn2_stored = sem("xn2_stored")
        xn_made = sem("xn_made")
        ve_made = [sem(f"ve_made{n}") for n in range(4)]
        rstd_made = [sem(f"rstd_made{n}") for n in range(4)]
        xres_loaded = sem("xres_loaded")
        att_done = sem("att_done")
        link_v = sem("link_v")
        link_p = sem("link_p")
        xT1a_made = sem("xT1a_made")
        xT1b_made = sem("xT1b_made")
        xT2a_made = sem("xT2a_made")
        xT2b_made = sem("xT2b_made")
        gmean_made = sem("gmean_made")
        gvar_made = sem("gvar_made")
        o_made = sem("o_made")
        q_made = sem("q_made")
        kv_made = sem("kv_made")
        state_made = sem("state_made")
        ctx_made = sem("ctx_made")
        gstat_made = sem("gstat_made")
        ctxn_made = sem("ctxn_made")
        nmr_made = sem("nmr_made")
        o_scaled = sem("o_scaled")
        xhl_made = sem("xhl_made")
        hi_x_made = sem("hi_x_made")
        logits_made = sem("logits_made")
        max_made = sem("max_made")
        maxall_made = sem("maxall_made")
        scale_made = sem("scale_made")
        prep_turned = sem("prep_turned")
        prep_hi = sem("prep_hi")
        prep_lo = sem("prep_lo")
        gu_done = sem("gu_done")
        silu_made = sem("silu_made")
        h_made = sem("h_made")
        hi_made = sem("hi_made")
        lo_made = sem("lo_made")
        dn_done = sem("dn_done")
        y_made = sem("y_made")
        y_stored = sem("y_stored")
        rt_link = sem("rt_link")
        diff_made = sem("diff_made")
        exp_made = sem("exp_made")
        m_made = sem("m_made")
        counted = sem("counted")
        eid_made = sem("eid_made")
        onehot_made = sem("onehot_made")
        comb_made = sem("comb_made")
        comb_stored = sem("comb_stored")
        onehot_used = sem("onehot_used")
        idx_made = sem("idx_made")
        idxc_made = sem("idxc_made")
        xg_loaded = [sem("xg_loaded0"), sem("xg_loaded1")]
        xg_turned = sem("xg_turned")
        xt_hi = sem("xt_hi")
        xt_lo = sem("xt_lo")
        idxs_made = sem("idxs_made")
        yw_made = sem("yw_made")
        scattered = sem("scattered")
        y_added = sem("y_added")
        x2_loaded = [sem(f"x2_loaded{r}") for r in range(4)]
        acc_loaded = [sem(f"acc_loaded{r}") for r in range(4)]
        cmb_link = sem("cmb_link")
        cmb_ve = sem("cmb_ve")
        cmb_sd = sem("cmb_sd")
        cmb_nmr = sem("cmb_nmr")
        cmb_norm = sem("cmb_norm")
        out_made = sem("out_made")
        out_stored = sem("out_stored")

        def wait(eng, s, value):
            if not (isinstance(value, int) and value <= 0):
                eng.wait_ge(s, value)

        def slot_gu(slot, h, k, j, n=1):
            return wgu[:, bass.ds(slot * SLOT_GU + ((h * KD + k) * GJ + j) * P, n * P)]

        def slot_dn(slot, c, h):
            return wdn[:, bass.ds(slot * SLOT_DN + (c * 2 + h) * D, D)]

        def scale_of(slot, n, lo=0, hi=P):
            return sc[lo:hi, bass.ds(slot * 4 + n, 1)]

        def passed(eng):
            eng.sem_inc(wait_passed, 1)

        READ = {LOGIT: (logits_made, 1, 1), STATE: (state_made, 1, 1), GMEAN: (gmean_made, 1, 1), GVAR: (gvar_made, 1, 1)}
        for k, (s1, s2) in enumerate(((xT1a_made, xT2a_made), (xT1b_made, xT2b_made))):
            READ |= {TURN1 + k: (s1, 1, 1), TURN2 + k: (s2, 1, 1), QU + k: (q_made, KD, k + 1), CTX + k: (ctx_made, KD, k + 1), OUT + k: (o_made, 2, k + 1)}
        READ |= {KV_USES[t]: (kv_made, NT, t + 1) for t in range(NT)}

        def y_bank(u, tt):
            return (y_ps, att_ps)[u][tt][:, 0:D]

        def att_bank(n):
            return att_ps[n % 2]

        def bank_ready(pe, b, n):
            here = [m for m in uses(b) if m < n and m % 2 == n % 2]
            if not here and isinstance(b, int) and b < 0:
                return
            rnd, m = (b, here[-1]) if here else (b - 1, [m for m in uses(b - 1) if m % 2 == n % 2][-1])
            s, per, count = READ[m]
            pe.wait_ge(s, (rnd + 1 if m in USES_FIRST else rnd) * per + count)

        def use_done(eng, b, n):
            before = 0 if isinstance(b, int) and b < 0 else len(USES_FIRST) + b * (len(USES_FIRST) + len(USES_SECOND))
            eng.wait_ge(att_done, before + uses(b).index(n) + 1)

        def steps(b):
            if isinstance(b, int) and b == B - 1:
                yield from LAST_ORDER
                return
            for step in ORDER:
                kind = step[0]
                prepares = kind in ("prep_max", "prep_scale", "prep")
                if isinstance(b, int) and b < 0 and kind not in FIRST_HALF and not prepares:
                    continue
                if isinstance(b, int) and b <= 0 and kind in ("G", "D", "H", "prep_end"):
                    continue
                yield step
            if isinstance(b, int) and b < 0:
                for n in range(4, 9):
                    yield "prep", n

        def xg_ps(r):
            return ps[6 + r][:, :].rearrange("p (k s) -> p k s", k=KD)

        GROUPS = [("gu", k, j, min(4, GJ - j)) for k in range(KD) for j in (0, 4, 8)] + [("dn", 0, c, 2) for c in (0, 2, 4)]
        NG = len(GROUPS)

        block = ctx.enter_context(nc.Block())

        @block.sync
        def _(sp):
            sp.dma_start(att[:, 0:1536].rearrange("p (j d) -> p j d", j=6), Wqkv.rearrange("(j p) d -> p j d", p=P)).then_inc(wqkv_staged, 16)
            sp.dma_start(att[:, 1536:2048].rearrange("p (j d) -> p j d", j=2), Wout.rearrange("(j p) d -> p j d", p=P)).then_inc(wqkv_staged, 16)
            sp.dma_start(att[0:E, 2048:2304], gate_w).then_inc(wqkv_staged, 16)
            sp.dma_start(att[0:2, 2304:2432], bqkv[0:D].rearrange("(k p) -> k p", p=P)).then_inc(wqkv_staged, 16)
            sp.dma_start(att[0:2, 2432:2560], gn_w.rearrange("(k p) -> k p", p=P)).then_inc(wqkv_staged, 16)
            sp.dma_start(att[0:2, 2560:2688], gn_b.rearrange("(k p) -> k p", p=P)).then_inc(wqkv_staged, 16)
            sp.dma_start(kvb, bqkv[D:3 * D].rearrange("(o n) -> o n", o=1).to_broadcast([P, 2 * D])).then_inc(setup_loaded, 16)
            sp.dma_start(outb, bout.rearrange("(o n) -> o n", o=1).to_broadcast([P, D])).then_inc(setup_loaded, 16)

            def load_stage(g_src, u_src, d_src, gu, dn):
                n5 = 5 * P
                sp.dma_start(gu[:, 0:5, :], g_src[0:n5].rearrange("(j p) d -> p j d", p=P)).then_inc(stage_loaded, 16)
                sp.dma_start(gu[:, 5:10, :], u_src[0:n5].rearrange("(j p) d -> p j d", p=P)).then_inc(stage_loaded, 16)
                sp.dma_start(gu[0:64, 10, :], g_src[n5:F]).then_inc(stage_loaded, 16)
                sp.dma_start(gu[64:P, 10, :], u_src[n5:F]).then_inc(stage_loaded, 16)
                sp.dma_start(dn[:, :, 0:F], d_src.rearrange("(t p) f -> p t f", p=P)).then_inc(stage_loaded, 16)
                sp.dma_start(dn[:, :, F:F + 64], d_src[:, n5:F].rearrange("(t p) f -> p t f", p=P)).then_inc(stage_loaded, 16)

            def load_expert(e, gu, dn):
                load_stage(eg[bass.ds(e, 1)].rearrange("e f d -> (e f) d"), eu[bass.ds(e, 1)].rearrange("e f d -> (e f) d"),
                           ed[bass.ds(e, 1)].rearrange("e d f -> (e d) f"), gu, dn)

            def load_x(b):
                sp.dma_start(xn, xf[bass.ds(b * S, S), :].rearrange("(t p) d -> p t d", p=P)).then_inc(x_loaded, 16)

            def stage_slot(s):
                sp.wait_ge(prep_turned, s * NG)
                load_expert(s - 1, stg_gu, stg_dn)

            def batch(b):
                if not isinstance(b, int) or b > 0:
                    sp.wait_ge(xn2_stored, b * 16)
                    use_done(sp, b - 1, TURN2 + 1)
                sp.dma_start(xres, xf[bass.ds(b * S, S), :].rearrange("(t p) d -> p t d", p=P)).then_inc(xres_loaded, 16)
                if not isinstance(b, int) or 0 < b < B - 1:
                    stage_slot(b + 1)
                sp.wait_ge(x2_made, b + 1)
                sp.dma_start(x2_d[bass.ds(b * S, S), :].rearrange("(t p) d -> p t d", p=P), xres).then_inc(x2_stored, 16)
                if not isinstance(b, int) or b > 0:
                    store_shared(2 * b - 2)
                sp.wait_ge(xn2_made, b + 1)
                sp.dma_start(xn2_d[bass.ds(b * S, S), 0:D].rearrange("(t p) d -> p t d", p=P), xres).then_inc(xn2_stored, 16)
                if not isinstance(b, int) or b < B - 1:
                    if not isinstance(b, int) or b < B - 2:
                        use_done(sp, b, STATE)
                        load_x(b + 2)
                if not isinstance(b, int) or b > 0:
                    store_shared(2 * b - 1)

            def store_shared(t):
                sp.wait_ge(y_made, (t + 3) * TT)
                sp.dma_start(acc_d[bass.ds(t * TW, TW), :].rearrange("(t p) d -> p t d", p=P),
                             ysb[:, :].rearrange("p (t d) -> p t d", t=TT)).then_inc(y_stored, 16)

            sp.dma_start(acc_d[TOK:TOK + P, :], xf[0:P, :]).then_inc(setup_loaded, 16)
            sp.wait_ge(setup_turned, 8)
            load_x(0)
            load_stage(sg, su, sd, stg_gu, stg_dn)
            use_done(sp, -1, STATE)
            load_x(1)
            stage_slot(1)
            batch(0)
            with sp.Fori(1, B - 2) as b:
                batch(b)
            batch(B - 2)
            batch(B - 1)
            sp.wait_ge(x2_stored, B * 16)
            sp.wait_ge(xn2_stored, B * 16)
            sp.wait_ge(xhl_made, B * KD)
            sp.wait_ge(logits_made, B)
            sp.wait_ge(prep_lo, B * NG)
            load_expert(E - 1, last_gu, last_dn)
            sp.wait_ge(comb_made, 2)
            sp.dma_start(xn2_d[:, D:D + E].rearrange("(t p) e -> p t e", p=P), r_t.rearrange("p (t e) -> p t e", e=E)).then_inc(comb_stored, 16)
            for u in range(2):
                store_shared(2 * B - 2 + u)

            def load_rows(arr, src, loaded):
                for n in range(B):
                    if n >= GB:
                        sp.wait_ge(loaded[n - GB], 16)
                    sp.dma_start(arr[:, n], src[n * S:(n + 1) * S, :].rearrange("(t p) d -> p t d", p=P)).then_inc(loaded[n % GB], 16)

            sp.wait_ge(dn_done, FC * (2 * B + NTILE + 1))
            load_rows(x2_rows, x2_d, x2_loaded)
            sp.wait_ge(scattered, 16 * TT * NTILE)
            load_rows(y_rows, acc_d, acc_loaded)
            with sp.Fori(0, B) as n:
                sp.wait_ge(out_made, n + 1)
                sp.dma_start(of[bass.ds(n * S, S), :].rearrange("(t p) d -> p t d", p=P), rows_of(x2_rows, 0, n)).then_inc(out_stored, 16)
            sp.wait_ge(out_stored, 16 * B)

        @block.gpsimd
        def _(pool):
            g = nc.gpsimd
            g.memset(ident[:, :], 0.0).then_inc(link_p, 1)
            g.memset(ones[:, :], 1.0).then_inc(link_p, 1)
            g.memset(upper[:, :], 1.0).then_inc(link_p, 1)
            g.memset(mask[:, :], 1.0).then_inc(link_p, 1)
            g.memset(mhalf[:, :], -0.5).then_inc(link_p, 1)
            g.iota(iota_i, pattern=[[1, P]], base=0, channel_multiplier=0).then_inc(link_p, 1)
            pool.wait_ge(link_p, 6)
            g.affine_select(out=ident[:, :], in_=ident[:, :], compare_op=ALU.not_equal, fill=1.0, base=0,
                            pattern=[[-1, P]], channel_multiplier=1).then_inc(const_made, 1)
            g.affine_select(out=upper[:, :], in_=upper[:, :], compare_op=ALU.is_gt, fill=0.0, base=0,
                            pattern=[[1, P]], channel_multiplier=-1).then_inc(const_made, 1)
            m3 = mask[:, :].rearrange("p (h c) -> p h c", c=HD)
            g.affine_select(out=m3, in_=m3, compare_op=ALU.is_ge, fill=0.0, base=0,
                            pattern=[[-HD, P // HD], [0, HD]], channel_multiplier=1).then_inc(link_p, 1)
            pool.wait_ge(link_p, 7)
            g.affine_select(out=m3, in_=m3, compare_op=ALU.is_ge, fill=0.0, base=HD - 1,
                            pattern=[[HD, P // HD], [0, HD]], channel_multiplier=-1).then_inc(const_made, 1)
            g.tensor_copy(iota[:, :], iota_i).then_inc(const_made, 1)
            g.iota(lohi_i[:, 0:NTB], pattern=[[P, NTB]], base=0, channel_multiplier=1).then_inc(link_p, 1)
            g.iota(posi[:, 0:E], pattern=[[-1, E]], base=E, channel_multiplier=0).then_inc(link_p, 1)
            pool.wait_ge(link_p, 9)
            g.tensor_copy(tokf[:, :], lohi_i[:, 0:NTB]).then_inc(const_made, 1)
            g.tensor_copy(rev[:, :], posi[:, 0:E]).then_inc(const_made, 1)

            def root(n, b, cols):
                pool.wait_ge(ve_made[n], b + 1)
                g.tensor_tensor(rstd[n][:, 0:cols], ve[n][:, 0:cols], mhalf[:, 0:cols], ALU.pow).then_inc(rstd_made[n], 1)

            def prep_scale(s):
                pool.wait_ge(max_made, 4 * s + 4)
                passed(pool)
                g.partition_all_reduce(mxa[:, :], mx[:, :], P, bass.bass_isa.ReduceOp.max).then_inc(maxall_made, 1)

            def batch(b):
                for step in steps(b):
                    if step[0] == "ln1_stats":
                        root(LN1, b + 1, NT)
                    if step[0] == "prep_scale":
                        prep_scale(b + 1)
                    if step[0] == "ctx_norm":
                        root(GN, b, KD)
                    if step[0] == "lno_stats":
                        root(LNO, b, NT)
                    if step[0] == "x2":
                        root(LN2, b, NT)

            batch(-1)
            batch(0)
            with pool.Fori(1, B - 1) as b:
                batch(b)
            batch(B - 1)

            prep_scale(B)

            pool.wait_ge(idx_made, 2)
            pool.wait_ge(xn2_stored, B * 16)
            pool.wait_ge(comb_stored, 16)

            def gather_x(i, r, first):
                if not first:
                    pool.wait_ge(xg_turned, i - 1)
                    pool.wait_ge(yw_made, i - 1)
                    pool.wait_ge(xg_loaded[r], 16 * (i - r))
                g.tensor_copy(idxc[:, 2 * r:2 * r + 2], idx[:, bass.ds(i * TT, TT)]).then_inc(idxc_made, 1)
                pool.wait_ge(idxc_made, i + 1)
                passed(pool)
                for t in range(TT):
                    g.indirect_dma_start(xg[:, r, t, :], None, xn2_d[:, :],
                                         bass.IndirectOffsetOnAxis(ap=idxc[:, 2 * r + t:2 * r + t + 1], axis=0)).then_inc(xg_loaded[r], 16)

            def scatter(i, r, ahead=True):
                pool.wait_ge(y_made, (2 * B + i + 3) * TT)
                g.tensor_copy(idxc[:, 4:6], idx_s[:, bass.ds(i * TT, TT)]).then_inc(idxs_made, 1)
                pool.wait_ge(idxs_made, i + 1)
                passed(pool)
                for t in range(TT):
                    g.indirect_dma_start(acc_d, bass.IndirectOffsetOnAxis(ap=idxc[:, 4 + t:5 + t], axis=0), ysb[:, t * D:(t + 1) * D], None,
                                         compute_op=ALU.add).then_inc(scattered, 16)
                    if t == 0 and ahead:
                        gather_x(i + 3, r, False)
                    pool.wait_ge(scattered, 16 * (TT * i + t + 1))
                    passed(pool)
                pool.sem_inc(y_added, 1)

            gather_x(0, 0, True)
            gather_x(1, 1, True)
            pool.wait_ge(y_stored, 16 * (2 * B + 1))
            pool.wait_ge(setup_loaded, 48)
            gather_x(2, 0, False)
            with pool.Fori(0, (NTILE - 3) // 2) as pair:
                scatter(2 * pair, 1)
                scatter(2 * pair + 1, 0)
            for i in range(NTILE - 3, NTILE):
                scatter(i, 0, False)

        @block.scalar
        def _(act):
            a = nc.scalar
            act.sem_inc(y_made, 2 * TT)
            act.sem_inc(y_stored, 16)
            act.sem_inc(y_added, 1)

            for n in range(8):
                act.wait_ge(setup_turned, n + 1)
                src = att_bank(n)
                if n < 6:
                    k, j = n // 3, 2 * (n % 3)
                    a.copy(wqkvT[:, k, j * P:(j + 2) * P], src[:, 0:256]).then_inc(setup_copied, 1)
                elif n == 6:
                    a.copy(attw[:, 1536:2048], src[:, :]).then_inc(setup_copied, 1)
                else:
                    a.copy(gateT[:, :], src[:, 0:16]).then_inc(link_v, 1)
                    a.copy(colv[:, 0:6], src[:, 16:22]).then_inc(setup_copied, 1)

            def gate_up(t, c, slot):
                q = t * FC + c
                act.wait_ge(gu_done, q + 1)
                passed(act)
                if c < FC - 1:
                    a.activation(silu[:, c % 2 * TW:(c % 2 + 1) * TW], gu_ps[c % 2][:, 0:TW], ACT.Silu,
                                 scale=scale_of(slot, 0)).then_inc(silu_made, 1)
                else:
                    a.activation(silu[64:P, TW:2 * TW], gu_ps[1][0:64, 0:TW], ACT.Silu,
                                 scale=scale_of(slot, 0, 0, 64)).then_inc(silu_made, 1)

            def hidden_hi(t, c):
                q = t * FC + c
                act.wait_ge(h_made, q + 3)
                act.wait_ge(dn_done, q + 1)
                h = hf[:, c % 2 * TW:(c % 2 + 1) * TW]
                o = hT[:, c * 2 * TW:c * 2 * TW + TW]
                if c < FC - 1:
                    a.copy(o, h).then_inc(hi_made, 1)
                else:
                    a.copy(o[0:64], h[64:P])
                    a.copy(o[64:P], h[64:P]).then_inc(hi_made, 1)

            def y_out(t, u, slot, routed=None):
                act.wait_ge(dn_done, FC + (t + 1) * FC)
                if routed is None:
                    act.wait_ge(y_stored, 16 * (t + 1))
                else:
                    act.wait_ge(y_added, routed + 1)
                    act.wait_ge(yw_made, routed + 1)
                passed(act)
                for tt in range(TT):
                    by = scale_of(slot, 2) if routed is None else yw[:, TT * u + tt:TT * u + tt + 1]
                    ins = a.activation(ysb[:, tt * D:(tt + 1) * D], y_bank(u, tt), ACT.Copy, scale=by)
                    ins.then_inc(y_made, 1)

            def ffn_step(kind, n, t0, slot):
                t, c = t0 + n // FC, n % FC
                if kind == "H":
                    gate_up(t, c, slot)
                    if n > 0:
                        hidden_hi(t0 + (n - 1) // FC, (n - 1) % FC)
                    if n == 2 * FC - 1:
                        hidden_hi(t, c)
                elif kind == "D" and c == FC - 1:
                    y_out(t, 0, slot)

            def prep(s, n):
                what, k, j, w = GROUPS[n]
                act.wait_ge(prep_turned, s * NG + n + 1)
                act.wait_ge(scale_made, s + 1)
                passed(act)
                src = prep_ps[n % 2]
                if what == "gu":
                    a.activation(slot_gu(s, 0, k, j, w), src[:, 0:w * P], ACT.Copy, scale=pw[:, 4:5]).then_inc(prep_hi, 1)
                else:
                    dst = wdn[:, bass.ds(s * SLOT_DN + j * 2 * D, 4 * D)].rearrange("p (c h d) -> p c h d", c=2, h=2)[:, :, 0, :]
                    a.activation(dst, src[:, :].rearrange("p (c d) -> p c d", c=2), ACT.Copy, scale=pw[:, 5:6]).then_inc(prep_hi, 1)

            def route_probs(n):
                act.wait_ge(diff_made, n + 1)
                a.activation(part_of(r_p, n), part_of(r_t, n), ACT.Exp).then_inc(exp_made, 1)

            def batch(b):
                for step in steps(b):
                    kind = step[0]
                    if kind in "GDH":
                        ffn_step(kind, step[1], 2 * b - 2, 0)
                    if kind == "route_probs":
                        route_probs(step[1])
                    if kind == "turn1_out":
                        use_done(act, b, TURN1)
                        a.copy(xT[:, 0, :], att_bank(TURN1)[:, :]).then_inc(xT1a_made, 1)
                    if kind == "q_out":
                        for m in range(KD):
                            use_done(act, b, QU + m)
                            a.activation(qT[:, m, :], att_bank(QU + m)[:, :], ACT.Identity, bias=colv[:, m:m + 1]).then_inc(q_made, 1)
                    if kind == "ctx_out":
                        for m in range(KD):
                            use_done(act, b, CTX + m)
                            a.copy(qT[:, m, :], att_bank(CTX + m)[:, :]).then_inc(ctx_made, 1)
                    if kind == "prep":
                        prep(b + 1, step[1])
                    if kind == "prep_end":
                        prep(b, step[1])
                    if kind == "lno_apply":
                        act.wait_ge(nmr_made, b + 1)
                        for t in range(NT):
                            a.activation(orow[:, t, :], orow[:, t, :], ACT.Identity, bias=nmr[:, t:t + 1], scale=rstd[LNO][:, t:t + 1]).then_inc(o_scaled, 1)
                    if kind == "turn2_out":
                        use_done(act, b, TURN2)
                        a.copy(xT[:, 0, :], att_bank(TURN2)[:, :]).then_inc(xT2a_made, 1)
                    if kind == "xhl":
                        act.wait_ge(xT2a_made, b + 1)
                        act.wait_ge(xT2b_made, b + 1)
                        for k in range(KD):
                            if k == 0:
                                wait(act, gu_done, 2 * FC * b)
                            a.activation(xhl_v[:, 0, k, :], xT[:, k, :], ACT.Copy, scale=X_SCALE).then_inc(hi_x_made, 1)
                    if kind == "logits_out":
                        use_done(act, b, LOGIT)
                        a.copy(logits[:, bass.ds(b * NT * E, NT * E)], att_bank(LOGIT)[:, 0:NT * E]).then_inc(logits_made, 1)

            batch(-1)
            batch(0)
            with act.Fori(1, B - 1) as b:
                batch(b)
            batch(B - 1)
            for step in TAIL:
                if step[0] in "GDH":
                    ffn_step(step[0], step[1], 2 * B - 2, 0)
                if step[0] == "prep":
                    prep(B, step[1])

            act.wait_ge(eid_made, 1)

            def turned_x(i, r):
                act.wait_ge(xg_turned, i + 1)
                a.activation(xt16[:, r, 0], xg_ps(r), ACT.Copy, scale=X_SCALE).then_inc(xt_hi, 1)

            def routed(i, r, slot, before, turn=True):
                t = 2 * B + i
                gate_up(t, 0, slot)
                if before is not None:
                    hidden_hi(t - 1, 5)
                gate_up(t, 1, slot)
                hidden_hi(t, 0)
                gate_up(t, 2, slot)
                hidden_hi(t, 1)
                gate_up(t, 3, slot)
                hidden_hi(t, 2)
                if before is not None:
                    y_out(t - 1, 1 - r, before, i - 1)
                if turn:
                    turned_x(i + 1, 1 - r)
                gate_up(t, 4, slot)
                hidden_hi(t, 3)
                gate_up(t, 5, slot)
                hidden_hi(t, 4)

            turned_x(0, 0)
            slot0 = act.value_load(eid[0:1, 0:1], min_val=1, max_val=E)
            routed(0, 0, slot0, None)
            act.wait_ge(y_stored, 16 * (2 * B + 1))
            with act.Fori(1, NTILE - 2, 2) as i:
                s1 = act.value_load(eid[0:1, bass.ds(i, 1)], min_val=1, max_val=E)
                routed(i, 1, s1, True)
                s2 = act.value_load(eid[0:1, bass.ds(i + 1, 1)], min_val=1, max_val=E)
                routed(i + 1, 0, s2, True)
            s1 = act.value_load(eid[0:1, NTILE - 2:NTILE - 1], min_val=1, max_val=E)
            routed(NTILE - 2, 1, s1, True)
            s2 = act.value_load(eid[0:1, NTILE - 1:NTILE], min_val=1, max_val=E)
            routed(NTILE - 1, 0, s2, True, turn=False)
            hidden_hi(2 * B + NTILE - 1, 5)
            y_out(2 * B + NTILE - 1, 0, None, NTILE - 1)

            def deviation(g, r):
                act.wait_ge(cmb_ve, GB * g + r + 1)
                a.activation(cmb_dev[r], ve[r][:, :], ACT.Sqrt).then_inc(cmb_sd, 1)

            def scaling(g, r):
                act.wait_ge(cmb_nmr, GB * g + r + 1)
                passed(act)
                rows = rows_of(y_rows, g, r)
                for t in range(NT):
                    a.activation(rows[:, t, :], rows[:, t, :], ACT.Identity, bias=cmb_shift[r][:, t:t + 1],
                                 scale=rstd[r][:, t:t + 1]).then_inc(cmb_norm, 1)

            with act.Fori(0, NGRP) as g:
                for r in range(GB):
                    deviation(g, r)
                    scaling(g, r)

        @block.tensor
        def _(pe):
            te = nc.tensor
            pe.sem_inc(dn_done, FC)
            pe.wait_ge(const_made, 6)
            pe.wait_ge(wqkv_staged, 96)
            for n in range(8):
                wait(pe, setup_copied, n - 1)
                dst = att_bank(n)
                if n < 6:
                    k, j = n // 3, 2 * (n % 3)
                    for jj in range(2):
                        src = att[:, (j + jj) * D + k * P:(j + jj) * D + (k + 1) * P]
                        ins = te.transpose(dst[:, jj * P:(jj + 1) * P], src, ident[:, :])
                elif n == 6:
                    for k in range(KD):
                        for j in range(2):
                            src = att[:, 1536 + j * D + k * P:1536 + j * D + (k + 1) * P]
                            ins = te.transpose(dst[:, k * D + j * P:k * D + (j + 1) * P], src, ident[:, :])
                else:
                    for k in range(KD):
                        te.transpose(dst[:, k * E:(k + 1) * E], att[0:E, 2048 + k * P:2048 + (k + 1) * P], ident[0:E, 0:E])
                    for v in range(3):
                        ins = te.transpose(dst[:, 16 + 2 * v:18 + 2 * v], att[0:2, 2304 + v * P:2304 + (v + 1) * P], ident[0:2, 0:2])
                ins.then_inc(setup_turned, 1)
            pe.wait_ge(setup_copied, 8)

            def gate_up(t, c, slot, x, x_sem, x_count):
                q = t * FC + c
                if c == 0:
                    pe.wait_ge(x_sem, x_count)
                pe.wait_ge(h_made, q + 1)
                halves = ((c, 0), (5 + c, TW)) if c < FC - 1 else ((GJ - 1, 0),)
                for j, at in halves:
                    o = gu_ps[c % 2][:, at:at + TW]
                    n = 0
                    for k in range(KD):
                        for hw, hx in ((0, 0), (0, 1), (1, 0)):
                            ins = te.matmul(o, slot_gu(slot, hw, k, j), x(hx, k), start=(n == 0), stop=(n == 5))
                            n += 1
                ins.then_inc(gu_done, 1)

            def down(t, u, c, slot, tiles_out=2):
                q = t * FC + c
                if c == 0:
                    pe.wait_ge(y_made, (t + tiles_out) * TT)
                pe.wait_ge(lo_made, q + 3)
                for tt in range(TT):
                    def h(hl):
                        at = (c * 2 + hl) * TW + tt * P
                        return hT[:, at:at + P]
                    pairs = ((0, 0), (0, 1), (1, 0)) if c < FC - 1 else ((0, 0), (0, 1))
                    for n, (hh, hw) in enumerate(pairs):
                        ins = te.matmul(y_bank(u, tt), h(hh), slot_dn(slot, c, hw), start=(c == 0 and n == 0),
                                        stop=(c == FC - 1 and n == 1))
                ins.then_inc(dn_done, 1)

            def ffn_step(kind, n, t0, b):
                t, c = t0 + n // FC, n % FC
                if kind == "G":
                    u = n // FC
                    gate_up(t, c, 0, lambda h, k: xhl_v[:, h, k, u * TW:(u + 1) * TW], xhl_made, b * KD)
                elif kind == "D":
                    down(t, 0, c, 0)

            def prep(s, n, gu, dn):
                what, k, j, w = GROUPS[n]
                if n == 0:
                    pe.wait_ge(stage_loaded, 96 * (s + 1))
                wait(pe, prep_lo, s * NG + max(n - 1, 0))
                dst = prep_ps[n % 2]
                if what == "gu":
                    for jj in range(w):
                        ins = te.transpose(dst[:, jj * P:(jj + 1) * P], gu[:, j + jj, k * P:(k + 1) * P], ident[:, :])
                else:
                    for cc in range(w):
                        for t in range(KD):
                            ins = te.transpose(dst[:, cc * D + t * P:cc * D + (t + 1) * P], dn[:, t, (j + cc) * P:(j + cc + 1) * P], ident[:, :])
                ins.then_inc(prep_turned, 1)

            def turn(b, n, rows, made, count):
                pe.wait_ge(made, count)
                for k in range(KD):
                    bank_ready(pe, b, n + k)
                    for t in range(NT):
                        ins = te.transpose(att_bank(n + k)[:, t * P:(t + 1) * P], rows[:, t, k * P:(k + 1) * P], ident[:, :])
                    ins.then_inc(att_done, 1)

            def batch(b):
                for step in steps(b):
                    kind = step[0]
                    if kind in "GDH":
                        ffn_step(kind, step[1], 2 * b - 2, b)
                    if kind == "turn1":
                        turn(b, TURN1, xn, xn_made, b + 2)
                    if kind == "q":
                        pe.wait_ge(xT1a_made, b + 2)
                        pe.wait_ge(xT1b_made, b + 2)
                        for m in range(KD):
                            bank_ready(pe, b, QU + m)
                            for k in range(KD):
                                ins = te.matmul(att_bank(QU + m)[:, :], wqkvT[:, k, m * P:(m + 1) * P], xT[:, k, :], start=(k == 0), stop=(k == KD - 1))
                            ins.then_inc(att_done, 1)
                    if kind == "kv":
                        t = step[1]
                        bank_ready(pe, b, KV_USES[t])
                        for k in range(KD):
                            ins = te.matmul(att_bank(KV_USES[t])[:, :], xT[:, k, t * P:(t + 1) * P], wqkvT[:, k, D:3 * D], start=(k == 0), stop=(k == KD - 1))
                        ins.then_inc(att_done, 1)
                    if kind == "state":
                        pe.wait_ge(kv_made, NT * (b + 2))
                        bank_ready(pe, b, STATE)
                        for m in range(KD):
                            for t in range(NT):
                                ins = te.matmul(att_bank(STATE)[:, m * P:(m + 1) * P], kv[:, t, m * P:(m + 1) * P],
                                                kv[:, t, D + m * P:D + (m + 1) * P], start=(t == 0), stop=(t == NT - 1))
                        ins.then_inc(att_done, 1)
                    if kind == "ctx":
                        pe.wait_ge(state_made, b + 1)
                        pe.wait_ge(q_made, KD * (b + 1))
                        for m in range(KD):
                            bank_ready(pe, b, CTX + m)
                            te.matmul(att_bank(CTX + m)[:, :], state[:, m * P:(m + 1) * P], qT[:, m, :], start=True, stop=True).then_inc(att_done, 1)
                    if kind == "group_mean":
                        pe.wait_ge(gstat_made, 2 * b + 1)
                        bank_ready(pe, b, GMEAN)
                        te.matmul(att_bank(GMEAN)[:, 0:4], mask[:, :], gst[:, 0:4], start=True, stop=True).then_inc(att_done, 1)
                    if kind == "group_var":
                        pe.wait_ge(gstat_made, 2 * b + 2)
                        bank_ready(pe, b, GVAR)
                        te.matmul(att_bank(GVAR)[:, 0:2], mask[:, :], gst[:, 8:10], start=True, stop=True).then_inc(att_done, 1)
                    if kind == "out":
                        pe.wait_ge(ctxn_made, KD * (b + 1))
                        for h in range(2):
                            bank_ready(pe, b, OUT + h)
                            for t in (2 * h, 2 * h + 1):
                                for k in range(KD):
                                    ins = te.matmul(att_bank(OUT + h)[:, (t % 2) * D:(t % 2 + 1) * D], qT[:, k, t * P:(t + 1) * P], woT[:, k, :],
                                                    start=(k == 0), stop=(k == KD - 1))
                            ins.then_inc(att_done, 1)
                    if kind == "prep":
                        prep(b + 1, step[1], stg_gu, stg_dn)
                    if kind == "prep_end":
                        prep(b, step[1], stg_gu, stg_dn)
                    if kind == "turn2":
                        turn(b, TURN2, xres, xn2_made, b + 1)
                    if kind == "logits":
                        pe.wait_ge(xT2a_made, b + 1)
                        pe.wait_ge(xT2b_made, b + 1)
                        bank_ready(pe, b, LOGIT)
                        for t in range(NT):
                            for k in range(KD):
                                ins = te.matmul(att_bank(LOGIT)[:, t * E:(t + 1) * E], xT[:, k, t * P:(t + 1) * P], gateT[:, k * E:(k + 1) * E],
                                                start=(k == 0), stop=(k == KD - 1))
                        ins.then_inc(att_done, 1)

            batch(-1)
            batch(0)
            with pe.Fori(1, B - 1) as b:
                batch(b)
            batch(B - 1)
            for step in TAIL:
                kind = step[0]
                if kind in "GDH":
                    ffn_step(kind, step[1], 2 * B - 2, B)
                if kind == "prep":
                    prep(B, step[1], last_gu, last_dn)
                if kind == "route_slots":
                    pe.wait_ge(m_made, 2)
                    pe.wait_ge(xT2b_made, B)
                    te.matmul(att_ps[0][:, 0:256], upper[:, :], r_m, start=True, stop=True)
                    te.matmul(att_ps[0][:, 256:512], ones[:, :], r_m, start=True, stop=True).then_inc(counted, 1)
                if kind == "invert":
                    for h in range(OHB):
                        j = OHB * step[1] + h
                        pe.wait_ge(onehot_made, j + 1)
                        for m in range(2):
                            ins = te.matmul(att_ps[1][:, 0:80], oh_lo[:, h, m, :], oh_hi[:, h, m, :], start=(j == 0 and m == 0), stop=(j == NTB - 1 and m == 1))
                        ins.then_inc(onehot_used, 1)

            pe.wait_ge(eid_made, 1)

            def turn_x(i, r, first):
                pe.wait_ge(xg_loaded[r], 16 * (i + 2 - r))
                if not first:
                    pe.wait_ge(xt_lo, i - 1)
                for k in range(KD):
                    for t in range(TT):
                        ins = te.transpose(xg_ps(r)[:, k, t * P:(t + 1) * P], xg[:, r, t, k * P:(k + 1) * P], ident[:, :])
                ins.then_inc(xg_turned, 1)

            def routed(i, r, slot, before, turn=True, later=None):
                t = 2 * B + i

                def gu(c):
                    gate_up(t, c, slot, lambda h, k: xt16[:, r, h, k, :], xt_lo, i + 1)
                gu(0)
                if before is not None:
                    down(t - 1, 1 - r, 3, before)
                gu(1)
                if before is not None:
                    down(t - 1, 1 - r, 4, before)
                gu(2)
                if before is not None:
                    down(t - 1, 1 - r, 5, before)
                after = later() if later else None
                gu(3)
                down(t, r, 0, slot, 2 if isinstance(i, int) and i == 0 else 1)
                if turn:
                    turn_x(i + 1, 1 - r, isinstance(i, int) and i == 0)
                gu(4)
                down(t, r, 1, slot)
                gu(5)
                down(t, r, 2, slot)
                return after

            def expert_of(i):
                return pe.value_load(eid[0:1, bass.ds(i, 1)], min_val=1, max_val=E)

            pe.wait_ge(prep_lo, NSLOT * NG)
            turn_x(0, 0, True)
            slot0 = expert_of(0)
            slot_before, slot_next = pe.alloc_register("slot_before"), pe.alloc_register("slot_next")
            nxt = routed(0, 0, slot0, None, later=lambda: expert_of(1))
            pe.reg_mov(slot_before, slot0)
            pe.reg_mov(slot_next, nxt)
            with pe.Fori(1, NTILE - 2, 2) as i:
                s0 = pe.snap(slot_before, min_val=1, max_val=E)
                s1 = pe.snap(slot_next, min_val=1, max_val=E)
                s2 = routed(i, 1, s1, s0, later=lambda: expert_of(i + 1))
                s3 = routed(i + 1, 0, s2, s1, later=lambda: expert_of(i + 2))
                pe.reg_mov(slot_before, s2)
                pe.reg_mov(slot_next, s3)
            s0 = pe.snap(slot_before, min_val=1, max_val=E)
            s1 = pe.snap(slot_next, min_val=1, max_val=E)
            s2 = routed(NTILE - 2, 1, s1, s0, later=lambda: expert_of(NTILE - 1))
            routed(NTILE - 1, 0, s2, s1, turn=False)
            for c in (3, 4, 5):
                down(2 * B + NTILE - 1, 0, c, s2)

        @block.vector
        def _(dve):
            v = nc.vector
            dve.sem_inc(h_made, 2)
            dve.sem_inc(lo_made, 2)
            dve.wait_ge(setup_copied, 8)
            dve.wait_ge(setup_loaded, 48)
            dve.wait_ge(const_made, 6)
            L_FIRST, L_SECOND, L_PREP = 2, 9, 5
            links = [0]

            def linked(ins, base):
                ins.then_inc(link_v, 1)
                links[0] += 1
                dve.wait_ge(link_v, base + links[0])

            def link_base(b):
                return 1 if isinstance(b, int) and b < 0 else 1 + L_FIRST + L_PREP + b * (L_FIRST + L_SECOND + L_PREP)

            def stats(src, b, n, base):
                for t in range(NT):
                    ins = v.bn_stats(st6[n][:, 6 * t:6 * t + 6], src[:, t, :])
                linked(ins, base)
                passed(dve)
                for t in range(NT):
                    ins = v.bn_aggr(mv[n][:, 2 * t:2 * t + 2], st6[n][:, 6 * t:6 * t + 6])
                linked(ins, base)
                v.tensor_scalar(ve[n][:, :], mv[n].rearrange("p (t s) -> p t s", s=2)[:, :, 1], EPS, None, ALU.add).then_inc(ve_made[n], 1)

            def normalise(rows, n):
                for t in range(NT):
                    ins = v.tensor_scalar(rows[:, t, :], rows[:, t, :], mv[n][:, 2 * t:2 * t + 1], rstd[n][:, t:t + 1], ALU.subtract, ALU.mult)
                return ins

            def gate_up(t, c, slot):
                q = t * FC + c
                dve.wait_ge(silu_made, q + 1)
                dve.wait_ge(lo_made, q + 1)
                lo = 0 if c < FC - 1 else 64
                up = gu_ps[c % 2][:, TW:2 * TW] if c < FC - 1 else gu_ps[1][64:P, 0:TW]
                v.scalar_tensor_tensor(out=hf[lo:P, c % 2 * TW:(c % 2 + 1) * TW], in0=up, scalar=scale_of(slot, 1, lo, P),
                                       in1=silu[lo:P, c % 2 * TW:(c % 2 + 1) * TW], op0=ALU.mult, op1=ALU.mult).then_inc(h_made, 1)

            def hidden_lo(t, c):
                q = t * FC + c
                dve.wait_ge(hi_made, q + 1)
                h = hf[:, c % 2 * TW:(c % 2 + 1) * TW]
                hi = hT[:, c * 2 * TW:c * 2 * TW + TW]
                lo = hT[:, c * 2 * TW + TW:(c + 1) * 2 * TW]
                if c < FC - 1:
                    v.tensor_tensor(lo, h, hi, ALU.subtract).then_inc(lo_made, 1)
                else:
                    v.tensor_tensor(hi[64:P], h[64:P], hi[64:P], ALU.subtract).then_inc(lo_made, 1)

            def ffn_step(kind, n, t0, slot):
                if kind == "H":
                    gate_up(t0 + n // FC, n % FC, slot)
                    if n > 0:
                        hidden_lo(t0 + (n - 1) // FC, (n - 1) % FC)
                    if n == 2 * FC - 1:
                        hidden_lo(t0 + n // FC, n % FC)

            def prep_max(s, n, gu, dn):
                dve.wait_ge(stage_loaded, 96 * (s + 1))
                part = gu[:, 4 * n:min(4 * n + 4, GJ), :] if n < 3 else dn
                v.tensor_reduce(mx[:, n:n + 1], part, AX.XY, ALU.max, apply_absolute_value=True).then_inc(max_made, 1)

            def prep_scale(s, base):
                dve.wait_ge(maxall_made, s + 1)

                def l2(ins):
                    linked(ins, base)
                l2(v.tensor_reduce(mxa[:, 0:1], mxa[:, 0:3], AX.X, ALU.max))
                l2(v.tensor_scalar(pw[:, 0:2], mxa[:, 0:4:3], 2.0 ** -30, None, ALU.max))
                l2(v.tensor_scalar(pw[:, 2:4].bitcast(I32), pw[:, 0:2].bitcast(I32), 0x7F800000, None, ALU.bitwise_and))
                l2(v.reciprocal(pw[:, 0:2], pw[:, 2:4]))
                v.tensor_scalar(pw[:, 4:6], pw[:, 0:2], 2.0 ** 14, None, ALU.mult)
                v.tensor_scalar(scale_of(s, 0), pw[:, 2:3], 2.0 ** -14 / X_SCALE, None, ALU.mult)
                v.tensor_scalar(scale_of(s, 1), pw[:, 0:1], 2.0 ** -17 / X_SCALE, None, ALU.mult)
                l2(v.scalar_tensor_tensor(out=pw[:, 6:7], in0=pw[:, 2:3], scalar=pw[:, 2:3], in1=pw[:, 3:4], op0=ALU.mult, op1=ALU.mult))
                v.tensor_scalar(scale_of(s, 2), pw[:, 6:7], 2.0 ** -11, None, ALU.mult).then_inc(scale_made, 1)

            def prep(s, n):
                what, k, j, w = GROUPS[n]
                dve.wait_ge(prep_hi, s * NG + n + 1)
                if what == "gu":
                    v.scalar_tensor_tensor(out=slot_gu(s, 1, k, j, w), in0=prep_ps[n % 2][:, 0:w * P], scalar=pw[:, 4:5],
                                           in1=slot_gu(s, 0, k, j, w), op0=ALU.mult, op1=ALU.subtract).then_inc(prep_lo, 1)
                else:
                    dst = wdn[:, bass.ds(s * SLOT_DN + j * 2 * D, 4 * D)].rearrange("p (c h d) -> p c h d", c=2, h=2)
                    v.scalar_tensor_tensor(out=dst[:, :, 1, :], in0=prep_ps[n % 2][:, :].rearrange("p (c d) -> p c d", c=2), scalar=pw[:, 5:6],
                                           in1=dst[:, :, 0, :], op0=ALU.mult, op1=ALU.subtract).then_inc(prep_lo, 1)

            rlinks = [0]

            def rl(ins):
                ins.then_inc(rt_link, 1)
                rlinks[0] += 1
                dve.wait_ge(rt_link, rlinks[0])

            def te8(a):
                return a.rearrange("p (t e) -> p t e", e=E)

            def by_tile(a):
                return a.rearrange("p (t o) -> p t o", o=1).to_broadcast([P, a.shape[-1], E])

            ends, tiles, tiles_i, base_, n255 = (small[:, 128 + 8 * n:136 + 8 * n] for n in range(5))
            one8 = small[:, 168:176]

            def route(kind, n):
                count = PART[n][1] - PART[n][0]
                lg, pr, df, o1, o2, mm, cc, xx = (part_of(arr, n) for arr in (logits[:, :], r_p, r_t, r_o1, r_o2, r_m, r_c, r_x))
                m1, m2, mr, ms = (part_of(small[:, NTB * m:NTB * (m + 1)], n, 1) for m in range(4))
                w1, w2 = (part_of(wts[:, NTB * m:NTB * (m + 1)], n, 1) for m in range(2))
                rev_b = rev[:, :].rearrange("p (o e) -> p o e", o=1).to_broadcast([P, count, E])

                def first_of(dst, top):
                    rl(v.tensor_reduce(top, te8(pr), AX.X, ALU.max))
                    rl(v.tensor_tensor(te8(xx), te8(pr), by_tile(top), ALU.is_equal))
                    rl(v.tensor_tensor(te8(xx), te8(xx), rev_b, ALU.mult))
                    rl(v.tensor_reduce(mr, te8(xx), AX.X, ALU.max))
                    rl(v.tensor_tensor(te8(dst), rev_b, by_tile(mr), ALU.is_equal))

                if kind == "route_probs":
                    dve.wait_ge(logits_made, B - 1 + n)
                    rl(v.tensor_reduce(ms, te8(lg), AX.X, ALU.max))
                    v.tensor_tensor(te8(df), te8(lg), by_tile(ms), ALU.subtract).then_inc(diff_made, 1)
                if kind == "route_top1":
                    dve.wait_ge(exp_made, n + 1)
                    rl(v.tensor_reduce(ms, te8(pr), AX.X, ALU.add))
                    rl(v.reciprocal(mr, ms))
                    rl(v.tensor_tensor(te8(pr), te8(pr), by_tile(mr), ALU.mult))
                    first_of(o1, m1)
                if kind == "route_top2":
                    rl(v.scalar_tensor_tensor(out=pr, in0=o1, scalar=-2.0, in1=pr, op0=ALU.mult, op1=ALU.add))
                    first_of(o2, m2)
                    v.tensor_tensor(mm, o1, o2, ALU.add).then_inc(m_made, 1)
                    rl(v.tensor_tensor(ms, m1, m2, ALU.add))
                    rl(v.tensor_scalar(ms, ms, 1e-20, None, ALU.add))
                    rl(v.reciprocal(mr, ms))
                    v.tensor_tensor(w1, m1, mr, ALU.mult)
                    rl(v.tensor_tensor(w2, m2, mr, ALU.mult))
                    v.tensor_tensor(te8(df), te8(o1), by_tile(w1), ALU.mult)
                    rl(v.tensor_tensor(te8(cc), te8(o2), by_tile(w2), ALU.mult))
                    v.tensor_tensor(df, df, cc, ALU.add).then_inc(comb_made, 1)
                    if n == 0:
                        v.tensor_copy(iota16, iota[:, :])
                        v.tensor_scalar(tokf[:, 0:NTB // 2], tokf[:, 0:NTB // 2], -float(TOK // 2), None, ALU.add)
                        v.tensor_scalar(tokf[:, NTB // 2:], tokf[:, NTB // 2:], 1.0 - TOK // 2, None, ALU.add)
                        rl(v.memset(one8, 1.0))

            def batch(b):
                links[0] = 0
                base = link_base(b)
                g3 = gst[:, 0:8].rearrange("p (w m s) -> p w m s", w=2, s=2)
                for step in steps(b):
                    kind = step[0]
                    if kind in "GDH":
                        ffn_step(kind, step[1], 2 * b - 2, 0)
                    if kind == "ln1_stats":
                        dve.wait_ge(x_loaded, 16 * (b + 2))
                        stats(xn, b, LN1, base)
                    if kind == "ln1_apply":
                        dve.wait_ge(rstd_made[LN1], b + 2)
                        normalise(xn, LN1).then_inc(xn_made, 1)
                    if kind == "turn1_out":
                        use_done(dve, b, TURN1 + 1)
                        v.tensor_copy(xT[:, 1, :], att_bank(TURN1 + 1)[:, :]).then_inc(xT1b_made, 1)
                    if kind == "kv_out":
                        t = step[1]
                        use_done(dve, b, KV_USES[t])
                        v.tensor_tensor(kv[:, t, :], att_bank(KV_USES[t])[:, :], kvb, ALU.add).then_inc(kv_made, 1)
                    if kind == "state_out":
                        use_done(dve, b, STATE)
                        for m in range(KD):
                            ins = v.tensor_tensor(state[:, m * P:(m + 1) * P], att_bank(STATE)[:, m * P:(m + 1) * P], mask[:, :], ALU.mult)
                        ins.then_inc(state_made, 1)
                    if kind.startswith("route"):
                        route(kind, step[1])
                    if kind == "prep_max":
                        prep_max(b + 1, step[1], stg_gu, stg_dn)
                    if kind == "prep_scale":
                        prep_scale(b + 1, base)
                    if kind == "prep":
                        prep(b + 1, step[1])
                    if kind == "prep_end":
                        prep(b, step[1])
                    if kind == "channel_stats":
                        dve.wait_ge(ctx_made, KD * (b + 1))
                        for m in range(KD):
                            ins = v.bn_stats(st6[GN][:, 6 * m:6 * m + 6], qT[:, m, :])
                        linked(ins, base)
                        passed(dve)
                        for m in range(KD):
                            ins = v.bn_aggr(gst[:, 2 * m:2 * m + 2], st6[GN][:, 6 * m:6 * m + 6])
                        ins.then_inc(gstat_made, 1)
                    if kind == "group_mean":
                        use_done(dve, b, GMEAN)
                        v.tensor_scalar(gst[:, 4:8], att_bank(GMEAN)[:, 0:4], 1.0 / HD, None, ALU.mult).then_inc(gmean_made, 1)
                        dve.wait_ge(gmean_made, b + 1)
                        linked(v.tensor_tensor(gst[:, 10:12], g3[:, 0, :, 0], g3[:, 1, :, 0], ALU.subtract), base)
                        v.tensor_tensor(gst[:, 8:10], gst[:, 10:12], gst[:, 10:12], ALU.mult).then_inc(gstat_made, 1)
                    if kind == "group_var":
                        use_done(dve, b, GVAR)
                        v.scalar_tensor_tensor(out=gst[:, 12:14], in0=att_bank(GVAR)[:, 0:2], scalar=1.0 / HD, in1=g3[:, 1, :, 1],
                                               op0=ALU.mult, op1=ALU.add).then_inc(gvar_made, 1)
                        dve.wait_ge(gvar_made, b + 1)
                        v.tensor_scalar(ve[GN][:, 0:KD], gst[:, 12:14], EPS, None, ALU.add).then_inc(ve_made[GN], 1)
                    if kind == "ctx_norm":
                        dve.wait_ge(rstd_made[GN], b + 1)
                        linked(v.tensor_tensor(gst[:, 12:14], rstd[GN][:, 0:KD], colv[:, 2:4], ALU.mult), base)
                        linked(v.tensor_tensor(gst[:, 14:16], g3[:, 1, :, 0], gst[:, 12:14], ALU.mult), base)
                        linked(v.tensor_tensor(gst[:, 10:12], colv[:, 4:6], gst[:, 14:16], ALU.subtract), base)
                        for m in range(KD):
                            v.tensor_scalar(qT[:, m, :], qT[:, m, :], gst[:, 12 + m:13 + m], gst[:, 10 + m:11 + m], ALU.mult, ALU.add).then_inc(ctxn_made, 1)
                    if kind == "out_out":
                        for h in range(2):
                            use_done(dve, b, OUT + h)
                            for t in (2 * h, 2 * h + 1):
                                ins = v.tensor_tensor(orow[:, t, :], att_bank(OUT + h)[:, (t % 2) * D:(t % 2 + 1) * D], outb, ALU.add)
                            ins.then_inc(o_made, 1)
                    if kind == "lno_stats":
                        dve.wait_ge(o_made, 2 * (b + 1))
                        stats(orow, b, LNO, base)
                    if kind == "lno_apply":
                        dve.wait_ge(rstd_made[LNO], b + 1)
                        v.scalar_tensor_tensor(out=nmr[:, :], in0=mv[LNO].rearrange("p (t s) -> p t s", s=2)[:, :, 0], scalar=-1.0,
                                               in1=rstd[LNO][:, :], op0=ALU.mult, op1=ALU.mult).then_inc(nmr_made, 1)
                    if kind == "x2":
                        dve.wait_ge(o_scaled, NT * (b + 1))
                        dve.wait_ge(xres_loaded, 16 * (b + 1))
                        v.tensor_tensor(att[:, 0:1024], att[:, 0:1024], att[:, 2048:3072], ALU.add).then_inc(x2_made, 1)
                        dve.wait_ge(x2_made, b + 1)
                        stats(xres, b, LN2, base)
                    if kind == "ln2_apply":
                        dve.wait_ge(rstd_made[LN2], b + 1)
                        dve.wait_ge(x2_stored, 16 * (b + 1))
                        normalise(xres, LN2).then_inc(xn2_made, 1)
                    if kind == "turn2_out":
                        use_done(dve, b, TURN2 + 1)
                        v.tensor_copy(xT[:, 1, :], att_bank(TURN2 + 1)[:, :]).then_inc(xT2b_made, 1)
                    if kind == "xhl":
                        dve.wait_ge(xT2b_made, b + 1)
                        for k in range(KD):
                            dve.wait_ge(hi_x_made, KD * b + k + 1)
                            v.scalar_tensor_tensor(out=xhl_v[:, 1, k, :], in0=xT[:, k, :], scalar=X_SCALE, in1=xhl_v[:, 0, k, :],
                                                   op0=ALU.mult, op1=ALU.subtract).then_inc(xhl_made, 1)
                return links[0]

            assert batch(-1) == L_FIRST + L_PREP
            n = batch(0)
            assert n == L_FIRST + L_SECOND + L_PREP, n
            with dve.Fori(1, B - 1) as b:
                batch(b)
            batch(B - 1)

            links[0] = 0
            tail_base = link_base(B - 1) + L_SECOND
            for step in TAIL:
                kind = step[0]
                if kind in "GDH":
                    ffn_step(kind, step[1], 2 * B - 2, 0)
                if kind == "prep_max":
                    prep_max(B, step[1], last_gu, last_dn)
                if kind == "prep_scale":
                    prep_scale(B, tail_base)
                if kind == "prep":
                    prep(B, step[1])
                if kind in ("route_top1", "route_top2"):
                    route(kind, step[1])
                if kind == "route_slots":
                    dve.wait_ge(counted, 1)
                    dve.wait_ge(comb_made, 2)
                    rl(v.tensor_copy(r_c, att_ps[0][:, 256:512]))
                    for e in range(E):
                        ins = v.tensor_tensor_scan(te8(r_s)[:, :, e], ones[:, 0:NTB], te8(r_c)[:, :, e], 0.0, ALU.mult, ALU.add)
                    rl(ins)
                    rl(v.tensor_tensor(r_x, r_s, r_c, ALU.subtract))
                    rl(v.tensor_tensor(r_x, r_x, att_ps[0][:, 0:256], ALU.add))
                    rl(v.tensor_scalar(n255.bitcast(I32), te8(r_s)[:, NTB - 1, :], float(TW - 1), None, ALU.add))
                    rl(v.tensor_scalar(tiles_i.bitcast(I32), n255.bitcast(I32), 8, None, ALU.logical_shift_right))
                    rl(v.tensor_copy(tiles, tiles_i.bitcast(I32)))
                    rl(v.tensor_tensor_scan(ends, one8, tiles, 0.0, ALU.mult, ALU.add))
                    rl(v.tensor_tensor(base_, ends, tiles, ALU.subtract))
                    rl(v.tensor_scalar(base_, base_, float(TW), None, ALU.mult))
                    rl(v.tensor_tensor(te8(r_x), te8(r_x), base_.rearrange("p (o e) -> p o e", o=1).to_broadcast([P, NTB, E]), ALU.add))
                if kind == "route_positions":
                    for n, oh in enumerate((r_o1, r_o2)):
                        rl(v.tensor_tensor(r_c, oh, r_x, ALU.mult))
                        rl(v.tensor_reduce(posf[:, n * NTB:(n + 1) * NTB], te8(r_c), AX.X, ALU.add))
                    dve.wait_ge(comb_stored, 16)
                    e3 = attw[:, 0:NTILE * E].rearrange("p (i e) -> p i e", e=E)
                    rl(v.tensor_tensor(e3, iota[:, 0:NTILE].rearrange("p (i o) -> p i o", o=1).to_broadcast([P, NTILE, E]),
                                       ends.rearrange("p (o e) -> p o e", o=1).to_broadcast([P, NTILE, E]), ALU.is_ge))
                    rl(v.tensor_reduce(attw[:, 512:512 + NTILE], e3, AX.X, ALU.add))
                    v.tensor_scalar(eid[:, :], attw[:, 512:512 + NTILE], float(E - 1), 1.0, ALU.min, ALU.add).then_inc(eid_made, 1)
                    rl(v.tensor_copy(posi[:, :], posf))
                    rl(v.tensor_scalar(lohi_i[:, :], posi[:, :], P - 1, None, ALU.bitwise_and))
                    rl(v.tensor_copy(lof, lohi_i[:, :]))
                    rl(v.tensor_scalar(lohi_i[:, :], posi[:, :], 7, None, ALU.logical_shift_right))
                    rl(v.tensor_copy(hif, lohi_i[:, :]))
                if kind == "one_hots":
                    for h in range(OHB):
                        j = OHB * step[1] + h
                        wait(dve, onehot_used, j - OHB + 1)
                        for m in range(2):
                            n = m * NTB + j
                            v.tensor_scalar(oh_lo[:, h, m, :], iota16, lof[:, n:n + 1], None, ALU.is_equal)
                            ins = v.tensor_scalar(oh_hi[:, h, m, :], iota16[:, 0:80], hif[:, n:n + 1], tokf[:, j:j + 1], ALU.is_equal, ALU.mult)
                        ins.then_inc(onehot_made, 1)
                if kind == "route_indices":
                    dve.wait_ge(onehot_used, NTB)
                    nums, empty, late = (attw[:, 128 * n:128 * n + NCOL] for n in range(3))
                    rl(v.tensor_copy(nums, att_ps[1][:, 0:NCOL]))
                    v.tensor_scalar(late, nums, 0.0, -1.0, ALU.is_gt, ALU.mult)
                    rl(v.tensor_scalar(empty, nums, 0.0, None, ALU.is_equal))
                    v.tensor_scalar(small[:, 0:1], tokf[:, 0:1], float(TOK), None, ALU.add)
                    rl(v.scalar_tensor_tensor(out=nums, in0=nums, scalar=float(TOK // 2), in1=late, op0=ALU.add, op1=ALU.add))
                    rl(v.tensor_scalar(late, empty, small[:, 0:1], None, ALU.mult))
                    v.tensor_tensor(idx_s, nums, late, ALU.add).then_inc(idx_made, 1)
                    v.scalar_tensor_tensor(out=idx[:, :], in0=empty, scalar=-float(TOK // 2), in1=nums, op0=ALU.mult, op1=ALU.add).then_inc(idx_made, 1)

            def turned_x(i, r):
                dve.wait_ge(xt_hi, i + 1)
                v.scalar_tensor_tensor(out=xt16[:, r, 1].rearrange("p k s -> p (k s)"), in0=ps[6 + r][:, :], scalar=X_SCALE,
                                       in1=xt16[:, r, 0].rearrange("p k s -> p (k s)"), op0=ALU.mult, op1=ALU.subtract).then_inc(xt_lo, 1)

            def routed(i, r, slot, before, turn=True):
                t = 2 * B + i

                def gu(c):
                    gate_up(t, c, slot)
                gu(0)
                dve.wait_ge(y_made, (t + 1) * TT)
                passed(dve)
                v.tensor_scalar(yw[:, TT * r:TT * (r + 1)], xg[:, r, :, bass.ds(slot + (D - 1), 1)].rearrange("p t o -> p (t o)"), scale_of(slot, 2), None,
                                ALU.mult).then_inc(yw_made, 1)
                if before:
                    hidden_lo(t - 1, 5)
                gu(1)
                hidden_lo(t, 0)
                gu(2)
                hidden_lo(t, 1)
                gu(3)
                hidden_lo(t, 2)
                if turn:
                    turned_x(i + 1, 1 - r)
                gu(4)
                hidden_lo(t, 3)
                gu(5)
                hidden_lo(t, 4)

            turned_x(0, 0)
            slot0 = dve.value_load(eid[0:1, 0:1], min_val=1, max_val=E)
            routed(0, 0, slot0, False)
            with dve.Fori(1, NTILE - 2, 2) as i:
                s1 = dve.value_load(eid[0:1, bass.ds(i, 1)], min_val=1, max_val=E)
                routed(i, 1, s1, True)
                s2 = dve.value_load(eid[0:1, bass.ds(i + 1, 1)], min_val=1, max_val=E)
                routed(i + 1, 0, s2, True)
            s1 = dve.value_load(eid[0:1, NTILE - 2:NTILE - 1], min_val=1, max_val=E)
            routed(NTILE - 2, 1, s1, True)
            s2 = dve.value_load(eid[0:1, NTILE - 1:NTILE], min_val=1, max_val=E)
            routed(NTILE - 1, 0, s2, True, turn=False)
            hidden_lo(2 * B + NTILE - 1, 5)

            CL = 3

            def group_stats(g, r):
                n = GB * g + r
                dve.wait_ge(acc_loaded[r], 16 * (g + 1))
                passed(dve)
                rows = rows_of(y_rows, g, r)
                for t in range(NT):
                    ins = v.bn_stats(st6[r][:, 6 * t:6 * t + 6], rows[:, t, :])
                ins.then_inc(cmb_link, 1)
                dve.wait_ge(cmb_link, n * CL + 1)
                passed(dve)
                for t in range(NT):
                    ins = v.bn_aggr(mv[r][:, 2 * t:2 * t + 2], st6[r][:, 6 * t:6 * t + 6])
                ins.then_inc(cmb_link, 1)
                dve.wait_ge(cmb_link, n * CL + 2)
                v.tensor_scalar(ve[r][:, :], mv[r].rearrange("p (t s) -> p t s", s=2)[:, :, 1], EPS, None, ALU.add).then_inc(cmb_ve, 1)

            def group_shift(g, r):
                n = GB * g + r
                dve.wait_ge(cmb_sd, n + 1)
                v.reciprocal(rstd[r][:, :], cmb_dev[r]).then_inc(cmb_link, 1)
                dve.wait_ge(cmb_link, n * CL + 3)
                v.scalar_tensor_tensor(out=cmb_shift[r], in0=mv[r].rearrange("p (t s) -> p t s", s=2)[:, :, 0], scalar=-1.0, in1=rstd[r][:, :],
                                       op0=ALU.mult, op1=ALU.mult).then_inc(cmb_nmr, 1)

            def group_sum(g, r):
                n = GB * g + r
                dve.wait_ge(cmb_norm, NT * (n + 1))
                dve.wait_ge(x2_loaded[r], 16 * (g + 1))
                passed(dve)
                v.tensor_tensor(rows_of(x2_rows, g, r), rows_of(x2_rows, g, r), rows_of(y_rows, g, r), ALU.add).then_inc(out_made, 1)

            with dve.Fori(0, NGRP) as g:
                for r in range(GB):
                    group_stats(g, r)
                    if r > 0:
                        group_sum(g, r - 1)
                    group_shift(g, r)
                group_sum(g, GB - 1)


_INS = ["L0_attn_x", "L0_attn_Wqkv_w", "L0_attn_Wqkv_b", "L0_attn_gn_w", "L0_attn_gn_b", "L0_attn_out_w", "L0_attn_out_b",
        "L0_ffn_gate_w", "L0_ffn_expert_gate", "L0_ffn_expert_up", "L0_ffn_expert_down", "L0_ffn_shared_gate", "L0_ffn_shared_up",
        "L0_ffn_shared_down"]


def kernel(**inputs):
    import numpy as _np
    import concourse.bacc as _bacc
    from concourse.bass_utils import run_bass_kernel_spmd as _run

    nc = _bacc.Bacc("TRN2", target_bir_lowering=False, num_devices=1)
    arrays, args = {}, []
    for name in _INS:
        a = _np.ascontiguousarray(inputs[name])
        arrays[f"in_{name}"] = a
        args.append(nc.dram_tensor(f"in_{name}", a.shape, mybir.dt.from_np(a.dtype), kind="ExternalInput").ap())
    args.append(nc.dram_tensor("out_x", (B, S, D), F32, kind="ExternalOutput").ap())
    build(nc, *args)
    r = _run(nc, [arrays], core_ids=[0])
    return r.results[0]["out_x"]
```

```python
from contextlib import ExitStack

import concourse.bass as bass
from concourse import mybir

F32 = mybir.dt.float32
F16 = mybir.dt.float16
I32 = mybir.dt.int32
ALU = mybir.AluOpType
ACT = mybir.ActivationFunctionType
AX = mybir.AxisListType

P = 128
B, S, D = 8, 512, 256
HD = 8
TOK = B * S
NT = S // P
KD = D // P
E = 8
F = 704
FC = 6
GU = 2 * F
GJ = GU // P
TW = 256
TT = TW // P
NTILE = 2 * TOK // TW + E - 1
NCOL = NTILE * TT
NTB = TOK // P
EPS = 1e-5
X_SCALE = 2.0 ** 11
SLOT_GU = 2 * KD * GU
SLOT_DN = FC * 2 * D
NSLOT = E + 1

ORDER = [("G", 0), ("ln1_stats",), ("H", 0), ("ctx",), ("G", 1), ("ctx_out",), ("channel_stats",), ("H", 1), ("G", 2), ("group_mean",), ("H", 2),
         ("G", 3), ("group_var",), ("G", 4), ("H", 3), ("ctx_norm",), ("G", 5), ("D", 0), ("D", 1), ("ln1_apply",), ("D", 2), ("out",), ("H", 4),
         ("H", 5), ("D", 3), ("prep_max", 0), ("out_out",), ("turn1",), ("turn1_out",), ("prep_max", 1), ("prep_max", 2), ("G", 6), ("D", 4),
         ("H", 6), ("lno_stats",), ("q",), ("q_out",), ("prep_max", 3), ("G", 7), ("D", 5), ("H", 7), ("lno_apply",), ("kv", 0), ("prep_scale",),
         ("kv_out", 0), ("x2",), ("G", 8), ("D", 6), ("H", 8), ("kv", 1), ("kv_out", 1), ("prep", 0), ("kv", 2), ("kv_out", 2), ("prep", 1),
         ("G", 9), ("D", 7), ("G", 10), ("H", 9), ("ln2_apply",), ("kv", 3), ("kv_out", 3), ("prep", 2), ("H", 10), ("prep", 3), ("D", 8), ("G", 11),
         ("turn2",), ("turn2_out",), ("prep", 4), ("H", 11), ("state",), ("state_out",), ("xhl",), ("prep", 5), ("logits",), ("D", 9), ("prep", 6),
         ("logits_out",), ("D", 10), ("prep", 7), ("D", 11), ("prep", 8)]
FIRST_HALF = ("ln1_stats", "ln1_apply", "turn1", "turn1_out", "q", "q_out", "kv", "kv_out", "state", "state_out")
LAST_ORDER = [("G", 0), ("ctx",), ("H", 0), ("route_probs", 0), ("ctx_out",), ("G", 1), ("channel_stats",), ("H", 1), ("G", 2), ("group_mean",),
              ("H", 2), ("G", 3), ("group_var",), ("G", 4), ("H", 3), ("ctx_norm",), ("D", 0), ("D", 1), ("out",), ("out_out",), ("D", 2), ("G", 5),
              ("H", 4), ("lno_stats",), ("prep_max", 0), ("prep_max", 1), ("H", 5), ("lno_apply",), ("G", 6), ("prep_max", 2), ("D", 3),
              ("prep_max", 3), ("D", 4), ("H", 6), ("x2",), ("D", 5), ("G", 7), ("H", 7), ("prep_scale",), ("prep", 0), ("prep", 1), ("G", 8),
              ("D", 6), ("H", 8), ("ln2_apply",), ("G", 9), ("route_top1", 0), ("H", 9), ("D", 7), ("prep", 2), ("turn2",), ("turn2_out",),
              ("prep", 3), ("G", 10), ("D", 8), ("H", 10), ("prep", 4), ("G", 11), ("H", 11), ("xhl",), ("prep", 5), ("prep", 6), ("logits",),
              ("logits_out",), ("route_top2", 0), ("route_probs", 1), ("D", 9), ("D", 10), ("prep", 7), ("prep", 8), ("D", 11)]
TAIL = [("G", 0), ("G", 1), ("H", 0), ("H", 1), ("G", 2), ("D", 0), ("route_top1", 1), ("H", 2), ("route_top2", 1), ("D", 1), ("prep_max", 0),
        ("route_slots",), ("G", 3), ("prep_max", 1), ("G", 4), ("H", 3), ("H", 4), ("prep_max", 2), ("D", 2), ("G", 5), ("route_positions",),
        ("prep_max", 3), ("one_hots", 0), ("G", 6), ("invert", 0), ("D", 3), ("prep_scale",), ("H", 5), ("G", 7), ("one_hots", 1), ("H", 6),
        ("prep", 0), ("D", 4), ("invert", 1), ("one_hots", 2), ("prep", 1), ("H", 7), ("G", 8), ("invert", 2), ("one_hots", 3), ("D", 5),
        ("prep", 2), ("G", 9), ("prep", 3), ("H", 8), ("invert", 3), ("D", 6), ("one_hots", 4), ("G", 10), ("H", 9), ("invert", 4), ("one_hots", 5),
        ("D", 7), ("prep", 4), ("G", 11), ("H", 10), ("invert", 5), ("D", 8), ("one_hots", 6), ("invert", 6), ("D", 9), ("H", 11), ("D", 10),
        ("one_hots", 7), ("prep", 5), ("invert", 7), ("D", 11), ("route_indices",), ("prep", 6), ("prep", 7), ("prep", 8)]

CTX, GMEAN, GVAR, OUT, TURN1, QU, TURN2, STATE, LOGIT = 0, 2, 3, 4, 6, 8, 14, 16, 17
KV_USES = [10, 11, 12, 13]
USES_FIRST = [TURN1, TURN1 + 1, QU, QU + 1] + KV_USES + [STATE]
USES_SECOND = [CTX, CTX + 1, GMEAN, GVAR, OUT, OUT + 1, TURN2, TURN2 + 1, LOGIT]


TERMS = [(k, hw, hx) for k in range(KD) for hw, hx in ((0, 0), (0, 1), (1, 0))]


def uses(b):
    first = USES_FIRST if not isinstance(b, int) or b < B - 1 else []
    second = USES_SECOND if not isinstance(b, int) or b >= 0 else []
    return sorted(first + second)


def build(nc, x_in, Wqkv, bqkv, gn_w, gn_b, Wout, bout, gate_w, eg, eu, ed, sg, su, sd, out):
    xf = x_in.rearrange("b s d -> (b s) d")
    of = out.rearrange("b s d -> (b s) d")
    with ExitStack() as ctx:
        def sb(name, cols, dt=F32, parts=P):
            return ctx.enter_context(nc.sbuf_tensor(name, [parts, cols], dt))

        def sem(name):
            return ctx.enter_context(nc.semaphore(name))

        xn2_d = nc.dram_tensor("xn2_d", (TOK, D + E), F32, kind="Internal").ap()
        x2_d = nc.dram_tensor("x2_d", (TOK, D), F32, kind="Internal").ap()
        acc_d = nc.dram_tensor("acc_d", (TOK + P, D), F32, kind="Internal").ap()

        wgu = sb("wgu", NSLOT * SLOT_GU, F16)
        wdn = sb("wdn", NSLOT * SLOT_DN, F16)
        att = sb("att", 5120)
        xres = att[:, 0:1024].rearrange("p (t d) -> p t d", t=NT)
        xn = att[:, 1024:2048].rearrange("p (t d) -> p t d", t=NT)
        kv = att[:, 1024:3072].rearrange("p (t c) -> p t c", t=NT)
        orow = att[:, 2048:3072].rearrange("p (t d) -> p t d", t=NT)
        xT = att[:, 3072:4096].rearrange("p (k s) -> p k s", k=KD)
        xq = att[:, 3072:4096].bitcast(F16).rearrange("p (h k s) -> p h k s", h=2, k=KD)
        qT = att[:, 4096:5120].rearrange("p (k s) -> p k s", k=KD)
        xhl = sb("xhl", 2 * KD * S, F16)
        xhl_v = xhl[:, :].rearrange("p (h k s) -> p h k s", h=2, k=KD)
        attw = sb("attw", 2816)
        wqkvT = attw[:, 0:1536].bitcast(F16).rearrange("p (h k c) -> p h k c", h=2, k=KD)
        woT = attw[:, 1536:2048].rearrange("p (k c) -> p k c", k=KD)
        kvb = attw[:, 2048:2560]
        outb = attw[:, 2560:2816]
        silu = sb("silu", 2 * TW)
        hf = sb("hf", 2 * TW)
        hT = sb("hT", FC * 2 * TW, F16)
        ysb = sb("ysb", TT * D)
        ident = sb("ident", P)
        mask = sb("mask", P)
        upper = sb("upper", P)
        ones = sb("ones", P)
        iota = sb("iota", P)
        iota_i = silu[:, 0:P].bitcast(I32)
        rev = sb("rev", E)
        state = sb("state", KD * P)
        logits = sb("logits", NTB * E)
        gateT = sb("gateT", KD * E)
        sc = sb("sc", NSLOT * 4)
        colv = sb("colv", 8)
        early = wgu[:, SLOT_GU:].bitcast(F32)
        LN1, GN, LNO, LN2 = range(4)
        st6a, mva, vea, rstda = (sb(f"{name}", 4 * NT * w) for name, w in (("st6", 6), ("mv", 2), ("ve", 1), ("rstd", 1)))
        st6, mv, ve, rstd = ([arr[:, NT * w * n:NT * w * (n + 1)] for n in range(4)] for arr, w in ((st6a, 6), (mva, 2), (vea, 1), (rstda, 1)))
        nmr = sb("nmr", NT)
        mhalf = sb("mhalf", NT)
        gst = sb("gst", 16)
        mx = sb("mx", 4)
        mxa = sb("mxa", 4)
        pw = sb("pw", 8)
        small = sb("small", 176)
        tokf = sb("tokf", NTB)
        posi = sb("posi", 2 * NTB, I32)
        wts = sb("wts", 2 * NTB)
        lohi_i = sb("lohi_i", 2 * NTB, I32)
        idx = sb("idx", NCOL, I32)
        idxc = sb("idxc", 8, I32)
        yw = sb("yw", 4)
        eid = sb("eid", NTILE, I32)

        stg_gu = wgu[:, E * SLOT_GU:].bitcast(F32).rearrange("p (j d) -> p j d", j=GJ)
        stg_dn = wdn[:, E * SLOT_DN:].bitcast(F32).rearrange("p (t f) -> p t f", t=KD)
        last_gu = att[:, 0:2816].rearrange("p (j d) -> p j d", j=GJ)
        last_dn = att[:, 2816:4352].rearrange("p (t f) -> p t f", t=KD)

        def rt(n):
            return attw[:, 256 * n:256 * n + 256]
        r_p, r_t, r_o1, r_o2, r_m, r_c, r_s, r_x = (rt(n) for n in range(8))
        PART = ((0, NTB - NT), (NTB - NT, NTB))

        def part_of(a, n, per=E):
            return a[:, PART[n][0] * per:PART[n][1] * per]

        OHB = 4
        oh_lo = attw[:, 2048:2560].bitcast(F16).rearrange("p (h m c) -> p h m c", h=OHB, m=2)
        oh_hi = att[:, 4352:4672].bitcast(F16).rearrange("p (h m c) -> p h m c", h=OHB, m=2)
        iota16 = att[:, 4672:4736].bitcast(F16)
        posf, lof, hif = (attw[:, 2560 + 2 * NTB * n:2560 + 2 * NTB * (n + 1)] for n in range(3))
        cmb_dev = [small[:, NT * r:NT * (r + 1)] for r in range(4)]
        cmb_shift = [small[:, 16 + NT * r:16 + NT * (r + 1)] for r in range(4)]
        idx_s = ones[:, 0:NCOL].bitcast(I32)
        xg = attw[:, 0:2 * TT * (D + E)].rearrange("p (r t d) -> p r t d", r=2, t=TT)
        xt16 = att[:, 0:1024].bitcast(F16).rearrange("p (r h k s) -> p r h k s", r=2, h=2, k=KD)
        GB = 4
        NGRP = B // GB
        y_rows = wdn[:, 0:B * 2048].bitcast(F32).rearrange("p (n t d) -> p n t d", n=B, t=NT)
        x2_rows = wgu[:, 0:B * 2048].bitcast(F32).rearrange("p (n t d) -> p n t d", n=B, t=NT)

        def rows_of(arr, g, r):
            return arr[:, bass.ds(GB * g + r, 1)].rearrange("p n t d -> p (n t) d")

        ps = [ctx.enter_context(nc.psum_tensor(f"ps{i}", [P, 512], F32)) for i in range(8)]
        gu_ps, y_ps, att_ps, prep_ps = ps[0:2], ps[2:4], ps[4:6], ps[6:8]

        const_made = sem("const_made")
        wait_passed = sem("wait_passed")
        setup_loaded = sem("setup_loaded")
        wqkv_staged = sem("wqkv_staged")
        setup_turned = sem("setup_turned")
        setup_copied = sem("setup_copied")
        setup_link = sem("setup_link")
        wmax_made = sem("wmax_made")
        wmaxall_made = sem("wmaxall_made")
        wscale_made = sem("wscale_made")
        w_hi_made = sem("w_hi_made")
        w_lo_made = sem("w_lo_made")
        x_loaded = sem("x_loaded")
        stage_loaded = sem("stage_loaded")
        x2_made = sem("x2_made")
        xn2_made = sem("xn2_made")
        x2_stored = sem("x2_stored")
        xn2_stored = sem("xn2_stored")
        xn_made = sem("xn_made")
        ve_made = [sem(f"ve_made{n}") for n in range(4)]
        rstd_made = [sem(f"rstd_made{n}") for n in range(4)]
        xres_loaded = sem("xres_loaded")
        att_done = sem("att_done")
        link_v = sem("link_v")
        link_p = sem("link_p")
        xq_hi = sem("xq_hi")
        xq_lo = sem("xq_lo")
        xT2a_made = sem("xT2a_made")
        xT2b_made = sem("xT2b_made")
        gmean_made = sem("gmean_made")
        gvar_made = sem("gvar_made")
        o_made = sem("o_made")
        q_made = sem("q_made")
        kv_made = sem("kv_made")
        state_made = sem("state_made")
        ctx_made = sem("ctx_made")
        gstat_made = sem("gstat_made")
        ctxn_made = sem("ctxn_made")
        nmr_made = sem("nmr_made")
        o_scaled = sem("o_scaled")
        xhl_made = sem("xhl_made")
        hi_x_made = sem("hi_x_made")
        logits_made = sem("logits_made")
        max_made = sem("max_made")
        maxall_made = sem("maxall_made")
        scale_made = sem("scale_made")
        prep_turned = sem("prep_turned")
        prep_hi = sem("prep_hi")
        prep_lo = sem("prep_lo")
        gu_done = sem("gu_done")
        silu_made = sem("silu_made")
        h_made = sem("h_made")
        hi_made = sem("hi_made")
        lo_made = sem("lo_made")
        dn_done = sem("dn_done")
        y_made = sem("y_made")
        y_stored = sem("y_stored")
        rt_link = sem("rt_link")
        diff_made = sem("diff_made")
        exp_made = sem("exp_made")
        m_made = sem("m_made")
        counted = sem("counted")
        eid_made = sem("eid_made")
        onehot_made = sem("onehot_made")
        onehot_lo_made = sem("onehot_lo_made")
        remainders_made = sem("remainders_made")
        comb_made = sem("comb_made")
        comb_stored = sem("comb_stored")
        onehot_used = sem("onehot_used")
        idx_made = sem("idx_made")
        idxc_made = sem("idxc_made")
        xg_loaded = [sem("xg_loaded0"), sem("xg_loaded1")]
        xg_turned = sem("xg_turned")
        xt_hi = sem("xt_hi")
        xt_lo = sem("xt_lo")
        idxs_made = sem("idxs_made")
        yw_made = sem("yw_made")
        scattered = sem("scattered")
        y_added = sem("y_added")
        x2_loaded = [sem(f"x2_loaded{r}") for r in range(4)]
        acc_loaded = [sem(f"acc_loaded{r}") for r in range(4)]
        cmb_stats = sem("cmb_stats")
        cmb_mean = sem("cmb_mean")
        cmb_rstd = sem("cmb_rstd")
        cmb_ve = sem("cmb_ve")
        cmb_sd = sem("cmb_sd")
        cmb_nmr = sem("cmb_nmr")
        cmb_norm = sem("cmb_norm")
        out_made = sem("out_made")
        out_stored = sem("out_stored")

        def wait(eng, s, value):
            if not (isinstance(value, int) and value <= 0):
                eng.wait_ge(s, value)

        def slot_gu(slot, h, k, j, n=1):
            return wgu[:, bass.ds(slot * SLOT_GU + ((h * KD + k) * GJ + j) * P, n * P)]

        def slot_dn(slot, c, h):
            return wdn[:, bass.ds(slot * SLOT_DN + (c * 2 + h) * D, D)]

        def scale_of(slot, n, lo=0, hi=P):
            return sc[lo:hi, bass.ds(slot * 4 + n, 1)]

        def passed(eng):
            eng.sem_inc(wait_passed, 1)

        READ = {LOGIT: (logits_made, 1, 1), STATE: (state_made, 1, 1), GMEAN: (gmean_made, 1, 1), GVAR: (gvar_made, 1, 1)}
        for k, s2 in enumerate((xT2a_made, xT2b_made)):
            READ |= {TURN1 + k: (xq_lo, KD, k + 1), TURN2 + k: (s2, 1, 1), QU + k: (q_made, KD, k + 1), CTX + k: (ctx_made, KD, k + 1), OUT + k: (o_made, 2, k + 1)}
        READ |= {KV_USES[t]: (kv_made, NT, t + 1) for t in range(NT)}

        def y_bank(u, tt):
            return (y_ps, att_ps)[u][tt][:, 0:D]

        def setup_bank(n):
            return ps[(0, 1, 2, 3, 6, 7)[n]]

        def att_bank(n):
            return att_ps[n % 2]

        def bank_ready(pe, b, n):
            here = [m for m in uses(b) if m < n and m % 2 == n % 2]
            if not here and isinstance(b, int) and b < 0:
                return
            rnd, m = (b, here[-1]) if here else (b - 1, [m for m in uses(b - 1) if m % 2 == n % 2][-1])
            s, per, count = READ[m]
            pe.wait_ge(s, (rnd + 1 if m in USES_FIRST else rnd) * per + count)

        def use_done(eng, b, n):
            before = 0 if isinstance(b, int) and b < 0 else len(USES_FIRST) + b * (len(USES_FIRST) + len(USES_SECOND))
            eng.wait_ge(att_done, before + uses(b).index(n) + 1)

        def steps(b):
            if isinstance(b, int) and b == B - 1:
                yield from LAST_ORDER
                return
            for step in ORDER:
                kind = step[0]
                if isinstance(b, int) and b < 0 and kind not in FIRST_HALF or isinstance(b, int) and b == 0 and kind in ("G", "D", "H"):
                    continue
                yield step

        def xg_ps(r):
            return ps[6 + r][:, :].rearrange("p (k s) -> p k s", k=KD)

        GROUPS = [("gu", k, j, min(4, GJ - j)) for k in range(KD) for j in (0, 4, 8)] + [("dn", 0, c, 2) for c in (0, 2, 4)]
        NG = len(GROUPS)

        block = ctx.enter_context(nc.Block())

        @block.sync
        def _(sp):
            def load_x(b):
                sp.dma_start(xn, xf[bass.ds(b * S, S), :].rearrange("(t p) d -> p t d", p=P)).then_inc(x_loaded, 16)

            load_x(0)
            sp.dma_start(early[:, 0:1536].rearrange("p (j d) -> p j d", j=6), Wqkv.rearrange("(j p) d -> p j d", p=P)).then_inc(wqkv_staged, 16)
            sp.dma_start(early[:, 1536:2048].rearrange("p (j d) -> p j d", j=2), Wout.rearrange("(j p) d -> p j d", p=P)).then_inc(wqkv_staged, 16)
            sp.dma_start(early[0:E, 2048:2304], gate_w).then_inc(wqkv_staged, 16)
            for n, vec in enumerate((bqkv[0:D], gn_w, gn_b)):
                sp.dma_start(early[0:KD, 2304 + n * P:2304 + (n + 1) * P], vec.rearrange("(k p) -> k p", p=P)).then_inc(wqkv_staged, 16)
            sp.dma_start(kvb, bqkv[D:3 * D].rearrange("(o n) -> o n", o=1).to_broadcast([P, 2 * D])).then_inc(setup_loaded, 16)
            sp.dma_start(outb, bout.rearrange("(o n) -> o n", o=1).to_broadcast([P, D])).then_inc(setup_loaded, 16)

            def load_stage(g_src, u_src, d_src, gu, dn):
                n5 = 5 * P
                sp.dma_start(gu[:, 0:5, :], g_src[0:n5].rearrange("(j p) d -> p j d", p=P)).then_inc(stage_loaded, 16)
                sp.dma_start(gu[:, 5:10, :], u_src[0:n5].rearrange("(j p) d -> p j d", p=P)).then_inc(stage_loaded, 16)
                sp.dma_start(gu[0:64, 10, :], g_src[n5:F]).then_inc(stage_loaded, 16)
                sp.dma_start(gu[64:P, 10, :], u_src[n5:F]).then_inc(stage_loaded, 16)
                sp.dma_start(dn[:, :, 0:F], d_src.rearrange("(t p) f -> p t f", p=P)).then_inc(stage_loaded, 16)
                sp.dma_start(dn[:, :, F:F + 64], d_src[:, n5:F].rearrange("(t p) f -> p t f", p=P)).then_inc(stage_loaded, 16)

            def load_expert(e, gu, dn):
                load_stage(eg[bass.ds(e, 1)].rearrange("e f d -> (e f) d"), eu[bass.ds(e, 1)].rearrange("e f d -> (e f) d"),
                           ed[bass.ds(e, 1)].rearrange("e d f -> (e d) f"), gu, dn)

            def stage_slot(s):
                sp.wait_ge(prep_turned, s * NG)
                load_expert(s - 1, stg_gu, stg_dn)

            def batch(b):
                if not isinstance(b, int) or b > 0:
                    sp.wait_ge(xn2_stored, b * 16)
                    use_done(sp, b - 1, TURN2 + 1)
                sp.dma_start(xres, xf[bass.ds(b * S, S), :].rearrange("(t p) d -> p t d", p=P)).then_inc(xres_loaded, 16)
                sp.wait_ge(x2_made, b + 1)
                sp.dma_start(x2_d[bass.ds(b * S, S), :].rearrange("(t p) d -> p t d", p=P), xres).then_inc(x2_stored, 16)
                if not isinstance(b, int) or b > 0:
                    store_shared(2 * b - 2)
                sp.wait_ge(xn2_made, b + 1)
                sp.dma_start(xn2_d[bass.ds(b * S, S), 0:D].rearrange("(t p) d -> p t d", p=P), xres).then_inc(xn2_stored, 16)
                if not isinstance(b, int) or b < B - 1:
                    if not isinstance(b, int) or b < B - 2:
                        use_done(sp, b, STATE)
                        load_x(b + 2)
                    stage_slot(b + 1)
                if not isinstance(b, int) or b > 0:
                    store_shared(2 * b - 1)

            def store_shared(t):
                sp.wait_ge(y_made, (t + 3) * TT)
                sp.dma_start(acc_d[bass.ds(t * TW, TW), :].rearrange("(t p) d -> p t d", p=P),
                             ysb[:, :].rearrange("p (t d) -> p t d", t=TT)).then_inc(y_stored, 16)

            sp.dma_start(acc_d[TOK:TOK + P, :], xf[0:P, :]).then_inc(setup_loaded, 16)
            load_stage(sg, su, sd, stg_gu, stg_dn)
            use_done(sp, -1, STATE)
            load_x(1)
            batch(0)
            with sp.Fori(1, B - 2) as b:
                batch(b)
            batch(B - 2)
            batch(B - 1)
            sp.wait_ge(x2_stored, B * 16)
            sp.wait_ge(xn2_stored, B * 16)
            sp.wait_ge(xhl_made, B * KD)
            sp.wait_ge(logits_made, B)
            load_expert(E - 1, last_gu, last_dn)
            sp.wait_ge(comb_made, 2)
            sp.dma_start(xn2_d[:, D:D + E].rearrange("(t p) e -> p t e", p=P), r_t.rearrange("p (t e) -> p t e", e=E)).then_inc(comb_stored, 16)
            for u in range(2):
                store_shared(2 * B - 2 + u)

            def load_rows(arr, src, loaded, flying):
                for n in range(B):
                    if n >= flying:
                        sp.wait_ge(loaded[(n - flying) % GB], 16 * ((n - flying) // GB + 1))
                    sp.dma_start(arr[:, n], src[n * S:(n + 1) * S, :].rearrange("(t p) d -> p t d", p=P)).then_inc(loaded[n % GB], 16)

            sp.wait_ge(gu_done, FC * (2 * B + NTILE))
            load_rows(x2_rows, x2_d, x2_loaded, 2)
            sp.wait_ge(dn_done, FC * (2 * B + NTILE + 1))
            sp.wait_ge(scattered, 16 * TT * NTILE)
            load_rows(y_rows, acc_d, acc_loaded, GB)
            with sp.Fori(0, B) as n:
                sp.wait_ge(out_made, n + 1)
                sp.dma_start(of[bass.ds(n * S, S), :].rearrange("(t p) d -> p t d", p=P), rows_of(x2_rows, 0, n)).then_inc(out_stored, 16)
            sp.wait_ge(out_stored, 16 * B)

        @block.gpsimd
        def _(pool):
            g = nc.gpsimd
            g.memset(ident[:, :], 0.0).then_inc(link_p, 1)
            g.memset(ones[:, :], 1.0).then_inc(link_p, 1)
            g.memset(upper[:, :], 1.0).then_inc(link_p, 1)
            g.memset(mask[:, :], 1.0).then_inc(link_p, 1)
            g.memset(mhalf[:, :], -0.5).then_inc(link_p, 1)
            g.iota(iota_i, pattern=[[1, P]], base=0, channel_multiplier=0).then_inc(link_p, 1)
            pool.wait_ge(link_p, 6)
            g.affine_select(out=ident[:, :], in_=ident[:, :], compare_op=ALU.not_equal, fill=1.0, base=0,
                            pattern=[[-1, P]], channel_multiplier=1).then_inc(const_made, 1)
            g.affine_select(out=upper[:, :], in_=upper[:, :], compare_op=ALU.is_gt, fill=0.0, base=0,
                            pattern=[[1, P]], channel_multiplier=-1).then_inc(const_made, 1)
            m3 = mask[:, :].rearrange("p (h c) -> p h c", c=HD)
            g.affine_select(out=m3, in_=m3, compare_op=ALU.is_ge, fill=0.0, base=0,
                            pattern=[[-HD, P // HD], [0, HD]], channel_multiplier=1).then_inc(link_p, 1)
            pool.wait_ge(link_p, 7)
            g.affine_select(out=m3, in_=m3, compare_op=ALU.is_ge, fill=0.0, base=HD - 1,
                            pattern=[[HD, P // HD], [0, HD]], channel_multiplier=-1).then_inc(const_made, 1)
            g.tensor_copy(iota[:, :], iota_i).then_inc(const_made, 1)
            g.iota(lohi_i[:, 0:NTB], pattern=[[P, NTB]], base=0, channel_multiplier=1).then_inc(link_p, 1)
            g.iota(posi[:, 0:E], pattern=[[-1, E]], base=E, channel_multiplier=0).then_inc(link_p, 1)
            pool.wait_ge(link_p, 9)
            g.tensor_copy(tokf[:, :], lohi_i[:, 0:NTB]).then_inc(const_made, 1)
            g.tensor_copy(rev[:, :], posi[:, 0:E]).then_inc(const_made, 1)

            def root(n, b, cols):
                pool.wait_ge(ve_made[n], b + 1)
                g.tensor_tensor(rstd[n][:, 0:cols], ve[n][:, 0:cols], mhalf[:, 0:cols], ALU.pow).then_inc(rstd_made[n], 1)

            def prep_scale(s):
                pool.wait_ge(max_made, 4 * s + 4)
                passed(pool)
                g.partition_all_reduce(mxa[:, :], mx[:, :], P, bass.bass_isa.ReduceOp.max).then_inc(maxall_made, 1)

            def batch(b):
                for step in steps(b):
                    if step[0] == "ln1_stats":
                        root(LN1, b + 1, NT)
                        if isinstance(b, int) and b < 0:
                            pool.wait_ge(wmax_made, 1)
                            g.partition_all_reduce(mxa[:, 0:1], mx[:, 0:1], P, bass.bass_isa.ReduceOp.max).then_inc(wmaxall_made, 1)
                    if step[0] == "prep_scale":
                        prep_scale(b)
                    if step[0] == "ctx_norm":
                        root(GN, b, KD)
                    if step[0] == "lno_stats":
                        root(LNO, b, NT)
                    if step[0] == "x2":
                        root(LN2, b, NT)

            batch(-1)
            batch(0)
            with pool.Fori(1, B - 1) as b:
                batch(b)
            batch(B - 1)

            for step in TAIL:
                if step[0] == "prep_scale":
                    prep_scale(B)
                if step[0] == "one_hots":
                    pool.wait_ge(remainders_made, 1)
                    for h in range(1, OHB):
                        j = OHB * step[1] + h
                        wait(pool, onehot_used, j - OHB + 1)
                        for m in range(2):
                            n = m * NTB + j
                            ins = g.tensor_scalar(oh_lo[:, h, m, :], iota16, lof[:, n:n + 1], None, ALU.is_equal)
                        ins.then_inc(onehot_lo_made, 1)

            pool.wait_ge(idx_made, 2)
            pool.wait_ge(xn2_stored, B * 16)
            pool.wait_ge(comb_stored, 16)

            def gather_x(i, r, first):
                if not first:
                    pool.wait_ge(xg_turned, i - 1)
                    pool.wait_ge(yw_made, i - 1)
                    pool.wait_ge(xg_loaded[r], 16 * (i - r))
                g.tensor_copy(idxc[:, 2 * r:2 * r + 2], idx[:, bass.ds(i * TT, TT)]).then_inc(idxc_made, 1)
                pool.wait_ge(idxc_made, i + 1)
                passed(pool)
                for t in range(TT):
                    g.indirect_dma_start(xg[:, r, t, :], None, xn2_d[:, :],
                                         bass.IndirectOffsetOnAxis(ap=idxc[:, 2 * r + t:2 * r + t + 1], axis=0)).then_inc(xg_loaded[r], 16)

            def scatter(i, r, ahead=True):
                pool.wait_ge(y_made, (2 * B + i + 3) * TT)
                g.tensor_copy(idxc[:, 4:6], idx_s[:, bass.ds(i * TT, TT)]).then_inc(idxs_made, 1)
                pool.wait_ge(idxs_made, i + 1)
                passed(pool)
                for t in range(TT):
                    g.indirect_dma_start(acc_d, bass.IndirectOffsetOnAxis(ap=idxc[:, 4 + t:5 + t], axis=0), ysb[:, t * D:(t + 1) * D], None,
                                         compute_op=ALU.add).then_inc(scattered, 16)
                    if t == 0 and ahead:
                        gather_x(i + 3, r, False)
                    pool.wait_ge(scattered, 16 * (TT * i + t + 1))
                    passed(pool)
                pool.sem_inc(y_added, 1)

            gather_x(0, 0, True)
            gather_x(1, 1, True)
            pool.wait_ge(y_stored, 16 * (2 * B + 1))
            pool.wait_ge(setup_loaded, 48)
            gather_x(2, 0, False)
            with pool.Fori(0, (NTILE - 3) // 2) as pair:
                scatter(2 * pair, 1)
                scatter(2 * pair + 1, 0)
            for i in range(NTILE - 3, NTILE):
                scatter(i, 0, False)

            with pool.Fori(0, NGRP) as k:
                for r in range(GB):
                    pool.wait_ge(x2_loaded[r], 16 * (k + 1))
                    pool.wait_ge(cmb_norm, NT * (GB * k + r + 1))
                    passed(pool)
                    g.tensor_tensor(rows_of(x2_rows, k, r), rows_of(x2_rows, k, r), rows_of(y_rows, k, r), ALU.add).then_inc(out_made, 1)

        @block.scalar
        def _(act):
            a = nc.scalar
            act.sem_inc(y_made, 2 * TT)
            act.sem_inc(y_stored, 16)
            act.sem_inc(y_added, 1)

            act.wait_ge(setup_turned, 1)
            a.copy(attw[:, 1536:2048], att_bank(0)[:, :]).then_inc(setup_copied, 1)
            act.wait_ge(setup_turned, 2)
            a.copy(gateT[:, :], att_bank(1)[:, 0:16])
            a.copy(colv[:, 0:6], att_bank(1)[:, 16:22]).then_inc(setup_copied, 1)
            act.wait_ge(wscale_made, 1)
            for n in range(6):
                act.wait_ge(setup_turned, n + 3)
                k, j = n // 3, 2 * (n % 3)
                a.activation(wqkvT[:, 0, k, j * P:(j + 2) * P], setup_bank(n)[:, 0:256], ACT.Copy, scale=colv[:, 6:7]).then_inc(w_hi_made, 1)

            def gate_up(t, c, slot):
                q = t * FC + c
                act.wait_ge(gu_done, q + 1)
                passed(act)
                if c < FC - 1:
                    a.activation(silu[:, c % 2 * TW:(c % 2 + 1) * TW], gu_ps[c % 2][:, 0:TW], ACT.Silu,
                                 scale=scale_of(slot, 0)).then_inc(silu_made, 1)
                else:
                    a.activation(silu[64:P, TW:2 * TW], gu_ps[1][0:64, 0:TW], ACT.Silu,
                                 scale=scale_of(slot, 0, 0, 64)).then_inc(silu_made, 1)

            def hidden_hi(t, c):
                q = t * FC + c
                act.wait_ge(h_made, q + 3)
                act.wait_ge(dn_done, q + 1)
                h = hf[:, c % 2 * TW:(c % 2 + 1) * TW]
                o = hT[:, c * 2 * TW:c * 2 * TW + TW]
                if c < FC - 1:
                    a.copy(o, h).then_inc(hi_made, 1)
                else:
                    a.copy(o[0:64], h[64:P])
                    a.copy(o[64:P], h[64:P]).then_inc(hi_made, 1)

            def y_out(t, u, slot, routed=None):
                act.wait_ge(dn_done, FC + (t + 1) * FC)
                if routed is None:
                    act.wait_ge(y_stored, 16 * (t + 1))
                else:
                    act.wait_ge(y_added, routed + 1)
                    act.wait_ge(yw_made, routed + 1)
                passed(act)
                for tt in range(TT):
                    by = scale_of(slot, 2) if routed is None else yw[:, TT * u + tt:TT * u + tt + 1]
                    ins = a.activation(ysb[:, tt * D:(tt + 1) * D], y_bank(u, tt), ACT.Copy, scale=by)
                    ins.then_inc(y_made, 1)

            def ffn_step(kind, n, t0, slot):
                t, c = t0 + n // FC, n % FC
                if kind == "H":
                    gate_up(t, c, slot)
                    if n > 0:
                        hidden_hi(t0 + (n - 1) // FC, (n - 1) % FC)
                    if n == 2 * FC - 1:
                        hidden_hi(t, c)
                elif kind == "D" and c == FC - 1:
                    y_out(t, 0, slot)

            def prep(s, n):
                what, k, j, w = GROUPS[n]
                act.wait_ge(prep_turned, s * NG + n + 1)
                act.wait_ge(scale_made, s + 1)
                passed(act)
                src = prep_ps[n % 2]
                if what == "gu":
                    a.activation(slot_gu(s, 0, k, j, w), src[:, 0:w * P], ACT.Copy, scale=pw[:, 4:5]).then_inc(prep_hi, 1)
                else:
                    dst = wdn[:, bass.ds(s * SLOT_DN + j * 2 * D, 4 * D)].rearrange("p (c h d) -> p c h d", c=2, h=2)[:, :, 0, :]
                    a.activation(dst, src[:, :].rearrange("p (c d) -> p c d", c=2), ACT.Copy, scale=pw[:, 5:6]).then_inc(prep_hi, 1)

            def route_probs(n):
                act.wait_ge(diff_made, n + 1)
                a.activation(part_of(r_p, n), part_of(r_t, n), ACT.Exp).then_inc(exp_made, 1)

            def batch(b):
                for step in steps(b):
                    kind = step[0]
                    if kind in "GDH":
                        ffn_step(kind, step[1], 2 * b - 2, 0)
                    if kind == "route_probs":
                        route_probs(step[1])
                    if kind == "turn1_out":
                        for k in range(KD):
                            use_done(act, b, TURN1 + k)
                            a.activation(xq[:, 0, k, :], att_bank(TURN1 + k)[:, :], ACT.Copy, scale=X_SCALE).then_inc(xq_hi, 1)
                    if kind == "q_out":
                        for m in range(KD):
                            use_done(act, b, QU + m)
                            a.activation(qT[:, m, :], att_bank(QU + m)[:, :], ACT.Identity, bias=colv[:, m:m + 1],
                                         scale=colv[:, 7:8]).then_inc(q_made, 1)
                    if kind == "ctx_out":
                        for m in range(KD):
                            use_done(act, b, CTX + m)
                            a.copy(qT[:, m, :], att_bank(CTX + m)[:, :]).then_inc(ctx_made, 1)
                    if kind == "prep":
                        prep(b, step[1])
                    if kind == "lno_apply":
                        act.wait_ge(nmr_made, b + 1)
                        for t in range(NT):
                            a.activation(orow[:, t, :], orow[:, t, :], ACT.Identity, bias=nmr[:, t:t + 1], scale=rstd[LNO][:, t:t + 1]).then_inc(o_scaled, 1)
                    if kind == "turn2_out":
                        use_done(act, b, TURN2)
                        a.copy(xT[:, 0, :], att_bank(TURN2)[:, :]).then_inc(xT2a_made, 1)
                    if kind == "xhl":
                        act.wait_ge(xT2a_made, b + 1)
                        act.wait_ge(xT2b_made, b + 1)
                        for k in range(KD):
                            if k == 0:
                                wait(act, gu_done, 2 * FC * b)
                            a.activation(xhl_v[:, 0, k, :], xT[:, k, :], ACT.Copy, scale=X_SCALE).then_inc(hi_x_made, 1)
                    if kind == "logits_out":
                        use_done(act, b, LOGIT)
                        a.copy(logits[:, bass.ds(b * NT * E, NT * E)], att_bank(LOGIT)[:, 0:NT * E]).then_inc(logits_made, 1)

            batch(-1)
            batch(0)
            with act.Fori(1, B - 1) as b:
                batch(b)
            batch(B - 1)
            for step in TAIL:
                if step[0] in "GDH":
                    ffn_step(step[0], step[1], 2 * B - 2, 0)
                if step[0] == "prep":
                    prep(B, step[1])

            act.wait_ge(eid_made, 1)

            def turned_x(i, r):
                act.wait_ge(xg_turned, i + 1)
                a.activation(xt16[:, r, 0], xg_ps(r), ACT.Copy, scale=X_SCALE).then_inc(xt_hi, 1)

            def routed(i, r, slot, before, turn=True):
                t = 2 * B + i
                gate_up(t, 0, slot)
                if before is not None:
                    hidden_hi(t - 1, 5)
                gate_up(t, 1, slot)
                hidden_hi(t, 0)
                gate_up(t, 2, slot)
                hidden_hi(t, 1)
                gate_up(t, 3, slot)
                hidden_hi(t, 2)
                if before is not None:
                    y_out(t - 1, 1 - r, before, i - 1)
                if turn:
                    turned_x(i + 1, 1 - r)
                gate_up(t, 4, slot)
                hidden_hi(t, 3)
                gate_up(t, 5, slot)
                hidden_hi(t, 4)

            turned_x(0, 0)
            slot0 = act.value_load(eid[0:1, 0:1], min_val=1, max_val=E)
            routed(0, 0, slot0, None)
            act.wait_ge(y_stored, 16 * (2 * B + 1))
            with act.Fori(1, NTILE - 2, 2) as i:
                s1 = act.value_load(eid[0:1, bass.ds(i, 1)], min_val=1, max_val=E)
                routed(i, 1, s1, True)
                s2 = act.value_load(eid[0:1, bass.ds(i + 1, 1)], min_val=1, max_val=E)
                routed(i + 1, 0, s2, True)
            s1 = act.value_load(eid[0:1, NTILE - 2:NTILE - 1], min_val=1, max_val=E)
            routed(NTILE - 2, 1, s1, True)
            s2 = act.value_load(eid[0:1, NTILE - 1:NTILE], min_val=1, max_val=E)
            routed(NTILE - 1, 0, s2, True, turn=False)
            hidden_hi(2 * B + NTILE - 1, 5)
            y_out(2 * B + NTILE - 1, 0, None, NTILE - 1)

            def deviation(g, r):
                act.wait_ge(cmb_ve, GB * g + r + 1)
                a.activation(cmb_dev[r], ve[r][:, :], ACT.Sqrt).then_inc(cmb_sd, 1)

            def scaling(g, r):
                act.wait_ge(cmb_nmr, GB * g + r + 1)
                passed(act)
                rows = rows_of(y_rows, g, r)
                for t in range(NT):
                    a.activation(rows[:, t, :], rows[:, t, :], ACT.Identity, bias=cmb_shift[r][:, t:t + 1],
                                 scale=rstd[r][:, t:t + 1]).then_inc(cmb_norm, 1)

            with act.Fori(0, NGRP) as g:
                for r in range(GB):
                    deviation(g, r)
                    scaling(g, r)

        @block.tensor
        def _(pe):
            te = nc.tensor
            pe.sem_inc(dn_done, FC)
            pe.wait_ge(const_made, 6)
            pe.wait_ge(wqkv_staged, 96)
            for k in range(KD):
                for j in range(2):
                    src = early[:, 1536 + j * D + k * P:1536 + j * D + (k + 1) * P]
                    ins = te.transpose(att_bank(0)[:, k * D + j * P:k * D + (j + 1) * P], src, ident[:, :])
            ins.then_inc(setup_turned, 1)
            for k in range(KD):
                te.transpose(att_bank(1)[:, k * E:(k + 1) * E], early[0:E, 2048 + k * P:2048 + (k + 1) * P], ident[0:E, 0:E])
            for v in range(3):
                ins = te.transpose(att_bank(1)[:, 16 + 2 * v:18 + 2 * v], early[0:2, 2304 + v * P:2304 + (v + 1) * P], ident[0:2, 0:2])
            ins.then_inc(setup_turned, 1)
            for n in range(6):
                k, j = n // 3, 2 * (n % 3)
                for jj in range(2):
                    src = early[:, (j + jj) * D + k * P:(j + jj) * D + (k + 1) * P]
                    ins = te.transpose(setup_bank(n)[:, jj * P:(jj + 1) * P], src, ident[:, :])
                ins.then_inc(setup_turned, 1)
            pe.wait_ge(setup_copied, 2)

            def gate_up(t, c, slot, x, x_sem, x_count):
                q = t * FC + c
                if c == 0:
                    pe.wait_ge(x_sem, x_count)
                pe.wait_ge(h_made, q + 1)
                halves = ((c, 0), (5 + c, TW)) if c < FC - 1 else ((GJ - 1, 0),)
                for j, at in halves:
                    o = gu_ps[c % 2][:, at:at + TW]
                    for n, (k, hw, hx) in enumerate(TERMS):
                        ins = te.matmul(o, slot_gu(slot, hw, k, j), x(hx, k), start=(n == 0), stop=(n == len(TERMS) - 1))
                ins.then_inc(gu_done, 1)

            def down(t, u, c, slot, tiles_out=2):
                q = t * FC + c
                if c == 0:
                    pe.wait_ge(y_made, (t + tiles_out) * TT)
                pe.wait_ge(lo_made, q + 3)
                for tt in range(TT):
                    def h(hl):
                        at = (c * 2 + hl) * TW + tt * P
                        return hT[:, at:at + P]
                    pairs = ((0, 0), (0, 1), (1, 0)) if c < FC - 1 else ((0, 0), (0, 1))
                    for n, (hh, hw) in enumerate(pairs):
                        ins = te.matmul(y_bank(u, tt), h(hh), slot_dn(slot, c, hw), start=(c == 0 and n == 0),
                                        stop=(c == FC - 1 and n == 1))
                ins.then_inc(dn_done, 1)

            def ffn_step(kind, n, t0, b):
                t, c = t0 + n // FC, n % FC
                if kind == "G":
                    u = n // FC
                    gate_up(t, c, 0, lambda h, k: xhl_v[:, h, k, u * TW:(u + 1) * TW], xhl_made, b * KD)
                elif kind == "D":
                    down(t, 0, c, 0)

            def prep(s, n, gu, dn):
                what, k, j, w = GROUPS[n]
                if n == 0:
                    pe.wait_ge(stage_loaded, 96 * (s + 1))
                wait(pe, prep_lo, s * NG + max(n - 1, 0))
                dst = prep_ps[n % 2]
                if what == "gu":
                    for jj in range(w):
                        ins = te.transpose(dst[:, jj * P:(jj + 1) * P], gu[:, j + jj, k * P:(k + 1) * P], ident[:, :])
                else:
                    for cc in range(w):
                        for t in range(KD):
                            ins = te.transpose(dst[:, cc * D + t * P:cc * D + (t + 1) * P], dn[:, t, (j + cc) * P:(j + cc + 1) * P], ident[:, :])
                ins.then_inc(prep_turned, 1)

            def turn(b, n, rows, made, count):
                pe.wait_ge(made, count)
                for k in range(KD):
                    bank_ready(pe, b, n + k)
                    for t in range(NT):
                        ins = te.transpose(att_bank(n + k)[:, t * P:(t + 1) * P], rows[:, t, k * P:(k + 1) * P], ident[:, :])
                    ins.then_inc(att_done, 1)

            def batch(b):
                for step in steps(b):
                    kind = step[0]
                    if kind in "GDH":
                        ffn_step(kind, step[1], 2 * b - 2, b)
                    if kind == "turn1":
                        turn(b, TURN1, xn, xn_made, b + 2)
                    if kind == "q":
                        pe.wait_ge(xq_lo, KD * (b + 2))
                        if isinstance(b, int) and b < 0:
                            pe.wait_ge(w_lo_made, 6)
                        for m in range(KD):
                            bank_ready(pe, b, QU + m)
                            for n, (k, hw, hx) in enumerate(TERMS):
                                ins = te.matmul(att_bank(QU + m)[:, :], wqkvT[:, hw, k, m * P:(m + 1) * P], xq[:, hx, k, :], start=(n == 0), stop=(n == len(TERMS) - 1))
                            ins.then_inc(att_done, 1)
                    if kind == "kv":
                        t = step[1]
                        bank_ready(pe, b, KV_USES[t])
                        for n, (k, hw, hx) in enumerate(TERMS):
                            ins = te.matmul(att_bank(KV_USES[t])[:, :], xq[:, hx, k, t * P:(t + 1) * P], wqkvT[:, hw, k, D:3 * D], start=(n == 0), stop=(n == len(TERMS) - 1))
                        ins.then_inc(att_done, 1)
                    if kind == "state":
                        pe.wait_ge(kv_made, NT * (b + 2))
                        bank_ready(pe, b, STATE)
                        for m in range(KD):
                            for t in range(NT):
                                ins = te.matmul(att_bank(STATE)[:, m * P:(m + 1) * P], kv[:, t, m * P:(m + 1) * P],
                                                kv[:, t, D + m * P:D + (m + 1) * P], start=(t == 0), stop=(t == NT - 1))
                        ins.then_inc(att_done, 1)
                    if kind == "ctx":
                        pe.wait_ge(state_made, b + 1)
                        pe.wait_ge(q_made, KD * (b + 1))
                        for m in range(KD):
                            bank_ready(pe, b, CTX + m)
                            te.matmul(att_bank(CTX + m)[:, :], state[:, m * P:(m + 1) * P], qT[:, m, :], start=True, stop=True).then_inc(att_done, 1)
                    if kind == "group_mean":
                        pe.wait_ge(gstat_made, 2 * b + 1)
                        bank_ready(pe, b, GMEAN)
                        te.matmul(att_bank(GMEAN)[:, 0:4], mask[:, :], gst[:, 0:4], start=True, stop=True).then_inc(att_done, 1)
                    if kind == "group_var":
                        pe.wait_ge(gstat_made, 2 * b + 2)
                        bank_ready(pe, b, GVAR)
                        te.matmul(att_bank(GVAR)[:, 0:2], mask[:, :], gst[:, 8:10], start=True, stop=True).then_inc(att_done, 1)
                    if kind == "out":
                        pe.wait_ge(ctxn_made, KD * (b + 1))
                        for h in range(2):
                            bank_ready(pe, b, OUT + h)
                            for t in (2 * h, 2 * h + 1):
                                for k in range(KD):
                                    ins = te.matmul(att_bank(OUT + h)[:, (t % 2) * D:(t % 2 + 1) * D], qT[:, k, t * P:(t + 1) * P], woT[:, k, :],
                                                    start=(k == 0), stop=(k == KD - 1))
                            ins.then_inc(att_done, 1)
                    if kind == "prep":
                        prep(b, step[1], stg_gu, stg_dn)
                    if kind == "turn2":
                        turn(b, TURN2, xres, xn2_made, b + 1)
                    if kind == "logits":
                        pe.wait_ge(xT2a_made, b + 1)
                        pe.wait_ge(xT2b_made, b + 1)
                        bank_ready(pe, b, LOGIT)
                        for t in range(NT):
                            for k in range(KD):
                                ins = te.matmul(att_bank(LOGIT)[:, t * E:(t + 1) * E], xT[:, k, t * P:(t + 1) * P], gateT[:, k * E:(k + 1) * E],
                                                start=(k == 0), stop=(k == KD - 1))
                        ins.then_inc(att_done, 1)

            batch(-1)
            batch(0)
            with pe.Fori(1, B - 1) as b:
                batch(b)
            batch(B - 1)
            for step in TAIL:
                kind = step[0]
                if kind in "GDH":
                    ffn_step(kind, step[1], 2 * B - 2, B)
                if kind == "prep":
                    prep(B, step[1], last_gu, last_dn)
                if kind == "route_slots":
                    pe.wait_ge(m_made, 2)
                    pe.wait_ge(xT2b_made, B)
                    te.matmul(att_ps[0][:, 0:256], upper[:, :], r_m, start=True, stop=True)
                    te.matmul(att_ps[0][:, 256:512], ones[:, :], r_m, start=True, stop=True).then_inc(counted, 1)
                if kind == "invert":
                    for h in range(OHB):
                        j = OHB * step[1] + h
                        pe.wait_ge(onehot_made, j + 1)
                        wait(pe, onehot_lo_made, (OHB - 1) * step[1] + h)
                        for m in range(2):
                            ins = te.matmul(att_ps[1][:, 0:80], oh_lo[:, h, m, :], oh_hi[:, h, m, :], start=(j == 0 and m == 0), stop=(j == NTB - 1 and m == 1))
                        ins.then_inc(onehot_used, 1)

            pe.wait_ge(eid_made, 1)

            def turn_x(i, r, first):
                pe.wait_ge(xg_loaded[r], 16 * (i + 2 - r))
                if not first:
                    pe.wait_ge(xt_lo, i - 1)
                for k in range(KD):
                    for t in range(TT):
                        ins = te.transpose(xg_ps(r)[:, k, t * P:(t + 1) * P], xg[:, r, t, k * P:(k + 1) * P], ident[:, :])
                ins.then_inc(xg_turned, 1)

            def routed(i, r, slot, before, turn=True, later=None):
                t = 2 * B + i

                def gu(c):
                    gate_up(t, c, slot, lambda h, k: xt16[:, r, h, k, :], xt_lo, i + 1)
                gu(0)
                if before is not None:
                    down(t - 1, 1 - r, 3, before)
                gu(1)
                if before is not None:
                    down(t - 1, 1 - r, 4, before)
                gu(2)
                if before is not None:
                    down(t - 1, 1 - r, 5, before)
                after = later() if later else None
                gu(3)
                down(t, r, 0, slot, 2 if isinstance(i, int) and i == 0 else 1)
                if turn:
                    turn_x(i + 1, 1 - r, isinstance(i, int) and i == 0)
                gu(4)
                down(t, r, 1, slot)
                gu(5)
                down(t, r, 2, slot)
                return after

            def expert_of(i):
                return pe.value_load(eid[0:1, bass.ds(i, 1)], min_val=1, max_val=E)

            pe.wait_ge(prep_lo, NSLOT * NG)
            turn_x(0, 0, True)
            slot0 = expert_of(0)
            slot_before, slot_next = pe.alloc_register("slot_before"), pe.alloc_register("slot_next")
            nxt = routed(0, 0, slot0, None, later=lambda: expert_of(1))
            pe.reg_mov(slot_before, slot0)
            pe.reg_mov(slot_next, nxt)
            with pe.Fori(1, NTILE - 2, 2) as i:
                s0 = pe.snap(slot_before, min_val=1, max_val=E)
                s1 = pe.snap(slot_next, min_val=1, max_val=E)
                s2 = routed(i, 1, s1, s0, later=lambda: expert_of(i + 1))
                s3 = routed(i + 1, 0, s2, s1, later=lambda: expert_of(i + 2))
                pe.reg_mov(slot_before, s2)
                pe.reg_mov(slot_next, s3)
            s0 = pe.snap(slot_before, min_val=1, max_val=E)
            s1 = pe.snap(slot_next, min_val=1, max_val=E)
            s2 = routed(NTILE - 2, 1, s1, s0, later=lambda: expert_of(NTILE - 1))
            routed(NTILE - 1, 0, s2, s1, turn=False)
            for c in (3, 4, 5):
                down(2 * B + NTILE - 1, 0, c, s2)

        @block.vector
        def _(dve):
            v = nc.vector
            dve.sem_inc(h_made, 2)
            dve.sem_inc(lo_made, 2)
            def weight_scale():
                dve.wait_ge(wqkv_staged, 96)
                v.tensor_reduce(mx[:, 0:1], early[:, 0:1536], AX.X, ALU.max, apply_absolute_value=True).then_inc(wmax_made, 1)
                dve.wait_ge(wmaxall_made, 1)
                v.tensor_scalar(pw[:, 0:1], mxa[:, 0:1], 2.0 ** -30, None, ALU.max).then_inc(setup_link, 1)
                dve.wait_ge(setup_link, 1)
                v.tensor_scalar(pw[:, 2:3].bitcast(I32), pw[:, 0:1].bitcast(I32), 0x7F800000, None, ALU.bitwise_and).then_inc(setup_link, 1)
                dve.wait_ge(setup_link, 2)
                v.reciprocal(pw[:, 0:1], pw[:, 2:3]).then_inc(setup_link, 1)
                dve.wait_ge(setup_link, 3)
                v.tensor_scalar(colv[:, 6:7], pw[:, 0:1], 2.0 ** 14, None, ALU.mult)
                v.tensor_scalar(colv[:, 7:8], pw[:, 2:3], 2.0 ** -14 / X_SCALE, None, ALU.mult).then_inc(wscale_made, 1)
                dve.wait_ge(wscale_made, 1)

            def weight_lo():
                for n in range(6):
                    dve.wait_ge(w_hi_made, n + 1)
                    k, at = n // 3, 2 * (n % 3) * P
                    v.scalar_tensor_tensor(out=wqkvT[:, 1, k, at:at + 2 * P], in0=setup_bank(n)[:, 0:256], scalar=colv[:, 6:7], in1=wqkvT[:, 0, k, at:at + 2 * P],
                                           op0=ALU.mult, op1=ALU.subtract).then_inc(w_lo_made, 1)
                dve.wait_ge(setup_copied, 2)
                dve.wait_ge(setup_loaded, 48)
                dve.wait_ge(const_made, 6)

            L_FIRST, L_SECOND, L_PREP = 2, 9, 5
            links = [0]

            def linked(ins, base):
                ins.then_inc(link_v, 1)
                links[0] += 1
                dve.wait_ge(link_v, base + links[0])

            def link_base(b):
                return 0 if isinstance(b, int) and b < 0 else L_FIRST + b * (L_FIRST + L_SECOND + L_PREP)

            def stats(src, b, n, base):
                for t in range(NT):
                    ins = v.bn_stats(st6[n][:, 6 * t:6 * t + 6], src[:, t, :])
                linked(ins, base)
                passed(dve)
                for t in range(NT):
                    ins = v.bn_aggr(mv[n][:, 2 * t:2 * t + 2], st6[n][:, 6 * t:6 * t + 6])
                linked(ins, base)
                v.tensor_scalar(ve[n][:, :], mv[n].rearrange("p (t s) -> p t s", s=2)[:, :, 1], EPS, None, ALU.add).then_inc(ve_made[n], 1)

            def normalise(rows, n):
                for t in range(NT):
                    ins = v.tensor_scalar(rows[:, t, :], rows[:, t, :], mv[n][:, 2 * t:2 * t + 1], rstd[n][:, t:t + 1], ALU.subtract, ALU.mult)
                return ins

            def gate_up(t, c, slot):
                q = t * FC + c
                dve.wait_ge(silu_made, q + 1)
                dve.wait_ge(lo_made, q + 1)
                lo = 0 if c < FC - 1 else 64
                up = gu_ps[c % 2][:, TW:2 * TW] if c < FC - 1 else gu_ps[1][64:P, 0:TW]
                v.scalar_tensor_tensor(out=hf[lo:P, c % 2 * TW:(c % 2 + 1) * TW], in0=up, scalar=scale_of(slot, 1, lo, P),
                                       in1=silu[lo:P, c % 2 * TW:(c % 2 + 1) * TW], op0=ALU.mult, op1=ALU.mult).then_inc(h_made, 1)

            def hidden_lo(t, c):
                q = t * FC + c
                dve.wait_ge(hi_made, q + 1)
                h = hf[:, c % 2 * TW:(c % 2 + 1) * TW]
                hi = hT[:, c * 2 * TW:c * 2 * TW + TW]
                lo = hT[:, c * 2 * TW + TW:(c + 1) * 2 * TW]
                if c < FC - 1:
                    v.tensor_tensor(lo, h, hi, ALU.subtract).then_inc(lo_made, 1)
                else:
                    v.tensor_tensor(hi[64:P], h[64:P], hi[64:P], ALU.subtract).then_inc(lo_made, 1)

            def ffn_step(kind, n, t0, slot):
                if kind == "H":
                    gate_up(t0 + n // FC, n % FC, slot)
                    if n > 0:
                        hidden_lo(t0 + (n - 1) // FC, (n - 1) % FC)
                    if n == 2 * FC - 1:
                        hidden_lo(t0 + n // FC, n % FC)

            def prep_max(s, n, gu, dn):
                dve.wait_ge(stage_loaded, 96 * (s + 1))
                part = gu[:, 4 * n:min(4 * n + 4, GJ), :] if n < 3 else dn
                v.tensor_reduce(mx[:, n:n + 1], part, AX.XY, ALU.max, apply_absolute_value=True).then_inc(max_made, 1)

            def prep_scale(s, base):
                dve.wait_ge(maxall_made, s + 1)

                def l2(ins):
                    linked(ins, base)
                l2(v.tensor_reduce(mxa[:, 0:1], mxa[:, 0:3], AX.X, ALU.max))
                l2(v.tensor_scalar(pw[:, 0:2], mxa[:, 0:4:3], 2.0 ** -30, None, ALU.max))
                l2(v.tensor_scalar(pw[:, 2:4].bitcast(I32), pw[:, 0:2].bitcast(I32), 0x7F800000, None, ALU.bitwise_and))
                l2(v.reciprocal(pw[:, 0:2], pw[:, 2:4]))
                v.tensor_scalar(pw[:, 4:6], pw[:, 0:2], 2.0 ** 14, None, ALU.mult)
                v.tensor_scalar(scale_of(s, 0), pw[:, 2:3], 2.0 ** -14 / X_SCALE, None, ALU.mult)
                v.tensor_scalar(scale_of(s, 1), pw[:, 0:1], 2.0 ** -17 / X_SCALE, None, ALU.mult)
                l2(v.scalar_tensor_tensor(out=pw[:, 6:7], in0=pw[:, 2:3], scalar=pw[:, 2:3], in1=pw[:, 3:4], op0=ALU.mult, op1=ALU.mult))
                v.tensor_scalar(scale_of(s, 2), pw[:, 6:7], 2.0 ** -11, None, ALU.mult).then_inc(scale_made, 1)

            def prep(s, n):
                what, k, j, w = GROUPS[n]
                dve.wait_ge(prep_hi, s * NG + n + 1)
                if what == "gu":
                    v.scalar_tensor_tensor(out=slot_gu(s, 1, k, j, w), in0=prep_ps[n % 2][:, 0:w * P], scalar=pw[:, 4:5],
                                           in1=slot_gu(s, 0, k, j, w), op0=ALU.mult, op1=ALU.subtract).then_inc(prep_lo, 1)
                else:
                    dst = wdn[:, bass.ds(s * SLOT_DN + j * 2 * D, 4 * D)].rearrange("p (c h d) -> p c h d", c=2, h=2)
                    v.scalar_tensor_tensor(out=dst[:, :, 1, :], in0=prep_ps[n % 2][:, :].rearrange("p (c d) -> p c d", c=2), scalar=pw[:, 5:6],
                                           in1=dst[:, :, 0, :], op0=ALU.mult, op1=ALU.subtract).then_inc(prep_lo, 1)

            rlinks = [0]

            def rl(ins):
                ins.then_inc(rt_link, 1)
                rlinks[0] += 1
                dve.wait_ge(rt_link, rlinks[0])

            def te8(a):
                return a.rearrange("p (t e) -> p t e", e=E)

            def by_tile(a):
                return a.rearrange("p (t o) -> p t o", o=1).to_broadcast([P, a.shape[-1], E])

            ends, tiles, tiles_i, base_, n255 = (small[:, 128 + 8 * n:136 + 8 * n] for n in range(5))
            one8 = small[:, 168:176]

            def route(kind, n):
                count = PART[n][1] - PART[n][0]
                lg, pr, df, o1, o2, mm, cc, xx = (part_of(arr, n) for arr in (logits[:, :], r_p, r_t, r_o1, r_o2, r_m, r_c, r_x))
                m1, m2, mr, ms = (part_of(small[:, NTB * m:NTB * (m + 1)], n, 1) for m in range(4))
                w1, w2 = (part_of(wts[:, NTB * m:NTB * (m + 1)], n, 1) for m in range(2))
                rev_b = rev[:, :].rearrange("p (o e) -> p o e", o=1).to_broadcast([P, count, E])

                def first_of(dst, top):
                    rl(v.tensor_reduce(top, te8(pr), AX.X, ALU.max))
                    rl(v.tensor_tensor(te8(xx), te8(pr), by_tile(top), ALU.is_equal))
                    rl(v.tensor_tensor(te8(xx), te8(xx), rev_b, ALU.mult))
                    rl(v.tensor_reduce(mr, te8(xx), AX.X, ALU.max))
                    rl(v.tensor_tensor(te8(dst), rev_b, by_tile(mr), ALU.is_equal))

                if kind == "route_probs":
                    dve.wait_ge(logits_made, B - 1 + n)
                    rl(v.tensor_reduce(ms, te8(lg), AX.X, ALU.max))
                    v.tensor_tensor(te8(df), te8(lg), by_tile(ms), ALU.subtract).then_inc(diff_made, 1)
                if kind == "route_top1":
                    dve.wait_ge(exp_made, n + 1)
                    rl(v.tensor_reduce(ms, te8(pr), AX.X, ALU.add))
                    rl(v.reciprocal(mr, ms))
                    rl(v.tensor_tensor(te8(pr), te8(pr), by_tile(mr), ALU.mult))
                    first_of(o1, m1)
                if kind == "route_top2":
                    rl(v.scalar_tensor_tensor(out=pr, in0=o1, scalar=-2.0, in1=pr, op0=ALU.mult, op1=ALU.add))
                    first_of(o2, m2)
                    v.tensor_tensor(mm, o1, o2, ALU.add).then_inc(m_made, 1)
                    rl(v.tensor_tensor(ms, m1, m2, ALU.add))
                    rl(v.tensor_scalar(ms, ms, 1e-20, None, ALU.add))
                    rl(v.reciprocal(mr, ms))
                    v.tensor_tensor(w1, m1, mr, ALU.mult)
                    rl(v.tensor_tensor(w2, m2, mr, ALU.mult))
                    v.tensor_tensor(te8(df), te8(o1), by_tile(w1), ALU.mult)
                    rl(v.tensor_tensor(te8(cc), te8(o2), by_tile(w2), ALU.mult))
                    v.tensor_tensor(df, df, cc, ALU.add).then_inc(comb_made, 1)
                    if n == 0:
                        v.tensor_copy(iota16, iota[:, :])
                        v.tensor_scalar(tokf[:, 0:NTB // 2], tokf[:, 0:NTB // 2], -float(TOK // 2), None, ALU.add)
                        v.tensor_scalar(tokf[:, NTB // 2:], tokf[:, NTB // 2:], 1.0 - TOK // 2, None, ALU.add)
                        rl(v.memset(one8, 1.0))

            def batch(b):
                links[0] = 0
                base = link_base(b)
                g3 = gst[:, 0:8].rearrange("p (w m s) -> p w m s", w=2, s=2)
                for step in steps(b):
                    kind = step[0]
                    if kind in "GDH":
                        ffn_step(kind, step[1], 2 * b - 2, 0)
                    if kind == "ln1_stats":
                        dve.wait_ge(x_loaded, 16 * (b + 2))
                        stats(xn, b, LN1, base)
                        if isinstance(b, int) and b < 0:
                            weight_scale()
                    if kind == "ln1_apply":
                        dve.wait_ge(rstd_made[LN1], b + 2)
                        normalise(xn, LN1).then_inc(xn_made, 1)
                        if isinstance(b, int) and b < 0:
                            weight_lo()
                    if kind == "turn1_out":
                        for k in range(KD):
                            dve.wait_ge(xq_hi, KD * (b + 1) + k + 1)
                            v.scalar_tensor_tensor(out=xq[:, 1, k, :], in0=att_bank(TURN1 + k)[:, :], scalar=X_SCALE, in1=xq[:, 0, k, :],
                                                   op0=ALU.mult, op1=ALU.subtract).then_inc(xq_lo, 1)
                    if kind == "kv_out":
                        t = step[1]
                        use_done(dve, b, KV_USES[t])
                        v.scalar_tensor_tensor(out=kv[:, t, :], in0=att_bank(KV_USES[t])[:, :], scalar=colv[:, 7:8], in1=kvb,
                                               op0=ALU.mult, op1=ALU.add).then_inc(kv_made, 1)
                    if kind == "state_out":
                        use_done(dve, b, STATE)
                        for m in range(KD):
                            ins = v.tensor_tensor(state[:, m * P:(m + 1) * P], att_bank(STATE)[:, m * P:(m + 1) * P], mask[:, :], ALU.mult)
                        ins.then_inc(state_made, 1)
                    if kind.startswith("route"):
                        route(kind, step[1])
                    if kind == "prep_max":
                        prep_max(b, step[1], stg_gu, stg_dn)
                    if kind == "prep_scale":
                        prep_scale(b, base)
                    if kind == "prep":
                        prep(b, step[1])
                    if kind == "channel_stats":
                        dve.wait_ge(ctx_made, KD * (b + 1))
                        for m in range(KD):
                            ins = v.bn_stats(st6[GN][:, 6 * m:6 * m + 6], qT[:, m, :])
                        linked(ins, base)
                        passed(dve)
                        for m in range(KD):
                            ins = v.bn_aggr(gst[:, 2 * m:2 * m + 2], st6[GN][:, 6 * m:6 * m + 6])
                        ins.then_inc(gstat_made, 1)
                    if kind == "group_mean":
                        use_done(dve, b, GMEAN)
                        v.tensor_scalar(gst[:, 4:8], att_bank(GMEAN)[:, 0:4], 1.0 / HD, None, ALU.mult).then_inc(gmean_made, 1)
                        dve.wait_ge(gmean_made, b + 1)
                        linked(v.tensor_tensor(gst[:, 10:12], g3[:, 0, :, 0], g3[:, 1, :, 0], ALU.subtract), base)
                        v.tensor_tensor(gst[:, 8:10], gst[:, 10:12], gst[:, 10:12], ALU.mult).then_inc(gstat_made, 1)
                    if kind == "group_var":
                        use_done(dve, b, GVAR)
                        v.scalar_tensor_tensor(out=gst[:, 12:14], in0=att_bank(GVAR)[:, 0:2], scalar=1.0 / HD, in1=g3[:, 1, :, 1],
                                               op0=ALU.mult, op1=ALU.add).then_inc(gvar_made, 1)
                        dve.wait_ge(gvar_made, b + 1)
                        v.tensor_scalar(ve[GN][:, 0:KD], gst[:, 12:14], EPS, None, ALU.add).then_inc(ve_made[GN], 1)
                    if kind == "ctx_norm":
                        dve.wait_ge(rstd_made[GN], b + 1)
                        linked(v.tensor_tensor(gst[:, 12:14], rstd[GN][:, 0:KD], colv[:, 2:4], ALU.mult), base)
                        linked(v.tensor_tensor(gst[:, 14:16], g3[:, 1, :, 0], gst[:, 12:14], ALU.mult), base)
                        linked(v.tensor_tensor(gst[:, 10:12], colv[:, 4:6], gst[:, 14:16], ALU.subtract), base)
                        for m in range(KD):
                            v.tensor_scalar(qT[:, m, :], qT[:, m, :], gst[:, 12 + m:13 + m], gst[:, 10 + m:11 + m], ALU.mult, ALU.add).then_inc(ctxn_made, 1)
                    if kind == "out_out":
                        for h in range(2):
                            use_done(dve, b, OUT + h)
                            for t in (2 * h, 2 * h + 1):
                                ins = v.tensor_tensor(orow[:, t, :], att_bank(OUT + h)[:, (t % 2) * D:(t % 2 + 1) * D], outb, ALU.add)
                            ins.then_inc(o_made, 1)
                    if kind == "lno_stats":
                        dve.wait_ge(o_made, 2 * (b + 1))
                        stats(orow, b, LNO, base)
                    if kind == "lno_apply":
                        dve.wait_ge(rstd_made[LNO], b + 1)
                        v.scalar_tensor_tensor(out=nmr[:, :], in0=mv[LNO].rearrange("p (t s) -> p t s", s=2)[:, :, 0], scalar=-1.0,
                                               in1=rstd[LNO][:, :], op0=ALU.mult, op1=ALU.mult).then_inc(nmr_made, 1)
                    if kind == "x2":
                        dve.wait_ge(o_scaled, NT * (b + 1))
                        dve.wait_ge(xres_loaded, 16 * (b + 1))
                        v.tensor_tensor(att[:, 0:1024], att[:, 0:1024], att[:, 2048:3072], ALU.add).then_inc(x2_made, 1)
                        dve.wait_ge(x2_made, b + 1)
                        stats(xres, b, LN2, base)
                    if kind == "ln2_apply":
                        dve.wait_ge(rstd_made[LN2], b + 1)
                        dve.wait_ge(x2_stored, 16 * (b + 1))
                        normalise(xres, LN2).then_inc(xn2_made, 1)
                    if kind == "turn2_out":
                        use_done(dve, b, TURN2 + 1)
                        v.tensor_copy(xT[:, 1, :], att_bank(TURN2 + 1)[:, :]).then_inc(xT2b_made, 1)
                    if kind == "xhl":
                        dve.wait_ge(xT2b_made, b + 1)
                        for k in range(KD):
                            dve.wait_ge(hi_x_made, KD * b + k + 1)
                            v.scalar_tensor_tensor(out=xhl_v[:, 1, k, :], in0=xT[:, k, :], scalar=X_SCALE, in1=xhl_v[:, 0, k, :],
                                                   op0=ALU.mult, op1=ALU.subtract).then_inc(xhl_made, 1)
                return links[0]

            assert batch(-1) == L_FIRST
            n = batch(0)
            assert n == L_FIRST + L_SECOND + L_PREP, n
            with dve.Fori(1, B - 1) as b:
                batch(b)
            batch(B - 1)

            links[0] = 0
            tail_base = link_base(B - 1) + L_SECOND + L_PREP
            for step in TAIL:
                kind = step[0]
                if kind in "GDH":
                    ffn_step(kind, step[1], 2 * B - 2, 0)
                if kind == "prep_max":
                    prep_max(B, step[1], last_gu, last_dn)
                if kind == "prep_scale":
                    prep_scale(B, tail_base)
                if kind == "prep":
                    prep(B, step[1])
                if kind in ("route_top1", "route_top2"):
                    route(kind, step[1])
                if kind == "route_slots":
                    dve.wait_ge(counted, 1)
                    dve.wait_ge(comb_made, 2)
                    rl(v.tensor_copy(r_c, att_ps[0][:, 256:512]))
                    for e in range(E):
                        ins = v.tensor_tensor_scan(te8(r_s)[:, :, e], ones[:, 0:NTB], te8(r_c)[:, :, e], 0.0, ALU.mult, ALU.add)
                    rl(ins)
                    rl(v.tensor_tensor(r_x, r_s, r_c, ALU.subtract))
                    rl(v.tensor_tensor(r_x, r_x, att_ps[0][:, 0:256], ALU.add))
                    rl(v.tensor_scalar(n255.bitcast(I32), te8(r_s)[:, NTB - 1, :], float(TW - 1), None, ALU.add))
                    rl(v.tensor_scalar(tiles_i.bitcast(I32), n255.bitcast(I32), 8, None, ALU.logical_shift_right))
                    rl(v.tensor_copy(tiles, tiles_i.bitcast(I32)))
                    rl(v.tensor_tensor_scan(ends, one8, tiles, 0.0, ALU.mult, ALU.add))
                    rl(v.tensor_tensor(base_, ends, tiles, ALU.subtract))
                    rl(v.tensor_scalar(base_, base_, float(TW), None, ALU.mult))
                    rl(v.tensor_tensor(te8(r_x), te8(r_x), base_.rearrange("p (o e) -> p o e", o=1).to_broadcast([P, NTB, E]), ALU.add))
                if kind == "route_positions":
                    for n, oh in enumerate((r_o1, r_o2)):
                        rl(v.tensor_tensor(r_c, oh, r_x, ALU.mult))
                        rl(v.tensor_reduce(posf[:, n * NTB:(n + 1) * NTB], te8(r_c), AX.X, ALU.add))
                    dve.wait_ge(comb_stored, 16)
                    e3 = attw[:, 0:NTILE * E].rearrange("p (i e) -> p i e", e=E)
                    rl(v.tensor_tensor(e3, iota[:, 0:NTILE].rearrange("p (i o) -> p i o", o=1).to_broadcast([P, NTILE, E]),
                                       ends.rearrange("p (o e) -> p o e", o=1).to_broadcast([P, NTILE, E]), ALU.is_ge))
                    rl(v.tensor_reduce(attw[:, 512:512 + NTILE], e3, AX.X, ALU.add))
                    v.tensor_scalar(eid[:, :], attw[:, 512:512 + NTILE], float(E - 1), 1.0, ALU.min, ALU.add).then_inc(eid_made, 1)
                    rl(v.tensor_copy(posi[:, :], posf))
                    rl(v.tensor_scalar(lohi_i[:, :], posi[:, :], P - 1, None, ALU.bitwise_and))
                    rl(v.tensor_copy(lof, lohi_i[:, :]))
                    rl(v.tensor_scalar(lohi_i[:, :], posi[:, :], 7, None, ALU.logical_shift_right))
                    rl(v.tensor_copy(hif, lohi_i[:, :]))
                    dve.sem_inc(remainders_made, 1)
                if kind == "one_hots":
                    for h in range(OHB):
                        j = OHB * step[1] + h
                        wait(dve, onehot_used, j - OHB + 1)
                        for m in range(2):
                            n = m * NTB + j
                            if h == 0:
                                v.tensor_scalar(oh_lo[:, h, m, :], iota16, lof[:, n:n + 1], None, ALU.is_equal)
                            ins = v.tensor_scalar(oh_hi[:, h, m, :], iota16[:, 0:80], hif[:, n:n + 1], tokf[:, j:j + 1], ALU.is_equal, ALU.mult)
                        ins.then_inc(onehot_made, 1)
                if kind == "route_indices":
                    dve.wait_ge(onehot_used, NTB)
                    nums, empty, late = (attw[:, 128 * n:128 * n + NCOL] for n in range(3))
                    rl(v.tensor_copy(nums, att_ps[1][:, 0:NCOL]))
                    v.tensor_scalar(late, nums, 0.0, -1.0, ALU.is_gt, ALU.mult)
                    rl(v.tensor_scalar(empty, nums, 0.0, None, ALU.is_equal))
                    v.tensor_scalar(small[:, 0:1], tokf[:, 0:1], float(TOK), None, ALU.add)
                    rl(v.scalar_tensor_tensor(out=nums, in0=nums, scalar=float(TOK // 2), in1=late, op0=ALU.add, op1=ALU.add))
                    rl(v.tensor_scalar(late, empty, small[:, 0:1], None, ALU.mult))
                    v.tensor_tensor(idx_s, nums, late, ALU.add).then_inc(idx_made, 1)
                    v.scalar_tensor_tensor(out=idx[:, :], in0=empty, scalar=-float(TOK // 2), in1=nums, op0=ALU.mult, op1=ALU.add).then_inc(idx_made, 1)

            def turned_x(i, r):
                dve.wait_ge(xt_hi, i + 1)
                v.scalar_tensor_tensor(out=xt16[:, r, 1].rearrange("p k s -> p (k s)"), in0=ps[6 + r][:, :], scalar=X_SCALE,
                                       in1=xt16[:, r, 0].rearrange("p k s -> p (k s)"), op0=ALU.mult, op1=ALU.subtract).then_inc(xt_lo, 1)

            def routed(i, r, slot, before, turn=True):
                t = 2 * B + i

                def gu(c):
                    gate_up(t, c, slot)
                gu(0)
                dve.wait_ge(y_made, (t + 1) * TT)
                passed(dve)
                v.tensor_scalar(yw[:, TT * r:TT * (r + 1)], xg[:, r, :, bass.ds(slot + (D - 1), 1)].rearrange("p t o -> p (t o)"), scale_of(slot, 2), None,
                                ALU.mult).then_inc(yw_made, 1)
                if before:
                    hidden_lo(t - 1, 5)
                gu(1)
                hidden_lo(t, 0)
                gu(2)
                hidden_lo(t, 1)
                gu(3)
                hidden_lo(t, 2)
                if turn:
                    turned_x(i + 1, 1 - r)
                gu(4)
                hidden_lo(t, 3)
                gu(5)
                hidden_lo(t, 4)

            turned_x(0, 0)
            slot0 = dve.value_load(eid[0:1, 0:1], min_val=1, max_val=E)
            routed(0, 0, slot0, False)
            with dve.Fori(1, NTILE - 2, 2) as i:
                s1 = dve.value_load(eid[0:1, bass.ds(i, 1)], min_val=1, max_val=E)
                routed(i, 1, s1, True)
                s2 = dve.value_load(eid[0:1, bass.ds(i + 1, 1)], min_val=1, max_val=E)
                routed(i + 1, 0, s2, True)
            s1 = dve.value_load(eid[0:1, NTILE - 2:NTILE - 1], min_val=1, max_val=E)
            routed(NTILE - 2, 1, s1, True)
            s2 = dve.value_load(eid[0:1, NTILE - 1:NTILE], min_val=1, max_val=E)
            routed(NTILE - 1, 0, s2, True, turn=False)
            hidden_lo(2 * B + NTILE - 1, 5)


            def group_stats(g, r):
                dve.wait_ge(acc_loaded[r], 16 * (g + 1))
                passed(dve)
                rows = rows_of(y_rows, g, r)
                for t in range(NT):
                    ins = v.bn_stats(st6[r][:, 6 * t:6 * t + 6], rows[:, t, :])
                ins.then_inc(cmb_stats, 1)

            def group_variance(g, r):
                n = GB * g + r
                dve.wait_ge(cmb_stats, n + 1)
                passed(dve)
                for t in range(NT):
                    ins = v.bn_aggr(mv[r][:, 2 * t:2 * t + 2], st6[r][:, 6 * t:6 * t + 6])
                ins.then_inc(cmb_mean, 1)
                dve.wait_ge(cmb_mean, n + 1)
                v.tensor_scalar(ve[r][:, :], mv[r].rearrange("p (t s) -> p t s", s=2)[:, :, 1], EPS, None, ALU.add).then_inc(cmb_ve, 1)

            def group_shift(g, r):
                n = GB * g + r
                dve.wait_ge(cmb_sd, n + 1)
                v.reciprocal(rstd[r][:, :], cmb_dev[r]).then_inc(cmb_rstd, 1)
                dve.wait_ge(cmb_rstd, n + 1)
                v.scalar_tensor_tensor(out=cmb_shift[r], in0=mv[r].rearrange("p (t s) -> p t s", s=2)[:, :, 0], scalar=-1.0, in1=rstd[r][:, :],
                                       op0=ALU.mult, op1=ALU.mult).then_inc(cmb_nmr, 1)

            with dve.Fori(0, NGRP) as g:
                for r in range(GB):
                    group_stats(g, r)
                    group_variance(g, r)
                    group_shift(g, r)


_INS = ["L0_attn_x", "L0_attn_Wqkv_w", "L0_attn_Wqkv_b", "L0_attn_gn_w", "L0_attn_gn_b", "L0_attn_out_w", "L0_attn_out_b",
        "L0_ffn_gate_w", "L0_ffn_expert_gate", "L0_ffn_expert_up", "L0_ffn_expert_down", "L0_ffn_shared_gate", "L0_ffn_shared_up",
        "L0_ffn_shared_down"]


def kernel(**inputs):
    import numpy as _np
    import concourse.bacc as _bacc
    from concourse.bass_utils import run_bass_kernel_spmd as _run

    nc = _bacc.Bacc("TRN2", target_bir_lowering=False, num_devices=1)
    arrays, args = {}, []
    for name in _INS:
        a = _np.ascontiguousarray(inputs[name])
        arrays[f"in_{name}"] = a
        args.append(nc.dram_tensor(f"in_{name}", a.shape, mybir.dt.from_np(a.dtype), kind="ExternalInput").ap())
    args.append(nc.dram_tensor("out_x", (B, S, D), F32, kind="ExternalOutput").ap())
    build(nc, *args)
    r = _run(nc, [arrays], core_ids=[0])
    return r.results[0]["out_x"]
```
